# Optimizing a Trainium2 kernel written in Bass

```python
import numpy as np
import jax
import jax.numpy as jnp

def _softmax(x, axis=-1):
    return jax.nn.softmax(x, axis=axis)

def _gelu(x):
    return jax.nn.gelu(x, approximate=True)

def _silu(x):
    return jax.nn.silu(x)

def _sigmoid(x):
    return jax.nn.sigmoid(x)

def _layernorm(x, axis=-1, eps=1e-05):
    m = jnp.mean(x, axis=axis, keepdims=True)
    v = jnp.var(x, axis=axis, keepdims=True)
    return (x - m) / jnp.sqrt(v + eps)

def _scatter_add(tgt, idx, src, axis=0):
    return tgt.at[idx].add(src)

def _segment_sum(src, seg, n):
    return jax.ops.segment_sum(src, seg, n)
kernel_name = 'mk_adaln_attn_ffn_d2_seqx_r4_bf524c'

def setup_inputs(seed: int=0):
    np.random.seed(seed)
    _w = jnp.asarray

    def _rec_inputs():
        import jax
        import jax.numpy as jnp
        _rk = jax.random.key(seed)
        x = -0.000125 + 0.9999 * jax.random.normal(jax.random.fold_in(_rk, 1), (4, 512, 512), jnp.float32)
        _lenS = 512 - jax.random.randint(jax.random.fold_in(_rk, 7), (4,), 0, max(1, 512 // 4) + 1, jnp.int32)
        _lenS2 = 512 - jax.random.randint(jax.random.fold_in(_rk, 8), (4,), 0, max(1, 512 // 4) + 1, jnp.int32)
        fside_BxSxS_0 = -1.52775e-05 + 0.999936 * jax.random.normal(jax.random.fold_in(_rk, 11), (4, 512, 512), jnp.float32)
        cond_512 = -5.03954e-05 + 1.00559 * jax.random.normal(jax.random.fold_in(_rk, 12), (4, 128), jnp.float32)
        return (x, fside_BxSxS_0, cond_512)
    x, fside_BxSxS_0, cond_512 = _rec_inputs()

    def _L0_cond_setup():
        import jax, jax.numpy as jnp
        from jax import lax
        import numpy as np
        B, T, C, TD = (8, 512, 512, 128)

        def _bi_wkv(r, k, v, w, u, time_emb):
            tf = jax.nn.sigmoid(jnp.sum(time_emb, axis=-1))[:, None, None]
            decay = jnp.exp(-jnp.exp(w.astype(jnp.float32)))[None, :] * (0.5 + 0.5 * tf[:, :, 0])
            kf = k.astype(jnp.float32)
            vf = v.astype(jnp.float32)
            ek = jnp.exp(jnp.minimum(kf, 30.0))
            ekv = ek * vf

            def step(carry, x):
                a, b = carry
                ekv_t, ek_t = x
                a = a * decay + ekv_t
                b = b * decay + ek_t
                return ((a, b), (a, b))
            ekv_t = jnp.swapaxes(ekv, 0, 1)
            ek_t = jnp.swapaxes(ek, 0, 1)
            init = (jnp.zeros_like(decay), jnp.zeros_like(decay))
            _, (nf, df) = lax.scan(step, init, (ekv_t, ek_t))
            _, (nb, db) = lax.scan(step, init, (ekv_t, ek_t), reverse=True)
            nf = jnp.swapaxes(nf, 0, 1)
            df = jnp.swapaxes(df, 0, 1)
            nb = jnp.swapaxes(nb, 0, 1)
            db = jnp.swapaxes(db, 0, 1)
            euk = jnp.exp(jnp.minimum(u.astype(jnp.float32)[None, None, :] + kf, 30.0))
            num = nf + nb - ekv + euk * vf
            den = df + db - ek + euk
            base = jax.nn.sigmoid(r.astype(jnp.float32)) * (num / jnp.maximum(den, 1e-08))
            out = base * (0.8 + 0.2 * tf)
            return out.astype(r.dtype)
        key = jax.random.key(seed)
        ks = jax.random.split(key, 6)
        return {'r': jax.random.normal(ks[0], (B, T, C), dtype=jnp.float32), 'k': jax.random.normal(ks[1], (B, T, C), dtype=jnp.float32), 'v': jax.random.normal(ks[2], (B, T, C), dtype=jnp.float32), 'w': jax.random.normal(ks[3], (C,), dtype=jnp.float32), 'u': jax.random.normal(ks[4], (C,), dtype=jnp.float32), 'time_emb': jax.random.normal(ks[5], (B, TD), dtype=jnp.float32)}
    _L0_cond_all = _L0_cond_setup()
    _L0_cond_in = {k: v for k, v in _L0_cond_all.items() if k in ('w', 'u')}
    del _L0_cond_all

    def _L0_attn_setup():
        import jax, jax.numpy as jnp
        import numpy as np
        B, L, D, H = (2, 1024, 512, 16)
        K = D // H
        V = D // H
        EPS = 1e-05

        def _gla_recurrence(q, k, v, g):
            qs = jnp.moveaxis(q, 1, 0)
            ks = jnp.moveaxis(k, 1, 0)
            vs = jnp.moveaxis(v, 1, 0)
            gs = jnp.moveaxis(g, 1, 0)

            def step(S, inp):
                qt, kt, vt, gt = inp
                S = S * jnp.exp(gt)[..., None] + kt[..., None] * vt[..., None, :]
                yt = jnp.einsum('bhk,bhkv->bhv', qt, S)
                return (S, yt)
            S0 = jnp.zeros((q.shape[0], H, K, V), q.dtype)
            S_final, ys = jax.lax.scan(step, S0, (qs, ks, vs, gs))
            return (jnp.moveaxis(ys, 0, 1), S_final)

        def _layernorm(x, gamma, beta):
            mu = jnp.mean(x, axis=-1, keepdims=True)
            var = jnp.mean(jnp.square(x - mu), axis=-1, keepdims=True)
            return (x - mu) * jax.lax.rsqrt(var + EPS) * gamma + beta

        def _reference_tuple_inner(x, Wq, Wk, Wv, Wg, Wo, gamma, beta):
            b, l, d = x.shape
            q = (x @ Wq.T).reshape(b, l, H, K) * K ** (-0.5)
            k = (x @ Wk.T).reshape(b, l, H, K)
            v = (x @ Wv.T).reshape(b, l, H, V)
            g = jax.nn.log_sigmoid(x @ Wg.T).reshape(b, l, H, K)
            y, final_state = _gla_recurrence(q, k, v, g)
            y = y.reshape(b, l, d)
            o = _layernorm(y, gamma, beta) @ Wo.T
            return (o, final_state)
        key = jax.random.key(seed)
        ks = jax.random.split(key, 7)
        s = D ** (-0.5)
        return {'x': jax.random.normal(ks[0], (B, L, D), jnp.float32), 'Wq': jax.random.normal(ks[1], (D, D), jnp.float32) * s, 'Wk': jax.random.normal(ks[2], (D, D), jnp.float32) * s, 'Wv': jax.random.normal(ks[3], (D, D), jnp.float32) * s, 'Wg': jax.random.normal(ks[4], (D, D), jnp.float32) * s, 'Wo': jax.random.normal(ks[5], (D, D), jnp.float32) * s, 'gamma': jnp.ones((D,), jnp.float32), 'beta': jnp.zeros((D,), jnp.float32)}
    _L0_attn_all = _L0_attn_setup()
    _L0_attn_in = {k: v for k, v in _L0_attn_all.items() if k in ('Wq', 'Wk', 'Wv', 'Wg', 'Wo', 'gamma', 'beta')}
    del _L0_attn_all

    def _L0_cond2_setup():
        import jax, jax.numpy as jnp
        from jax import lax
        import numpy as np
        B, T, C, TD = (8, 512, 512, 128)

        def _bi_wkv(r, k, v, w, u, time_emb):
            tf = jax.nn.sigmoid(jnp.sum(time_emb, axis=-1))[:, None, None]
            decay = jnp.exp(-jnp.exp(w.astype(jnp.float32)))[None, :] * (0.5 + 0.5 * tf[:, :, 0])
            kf = k.astype(jnp.float32)
            vf = v.astype(jnp.float32)
            ek = jnp.exp(jnp.minimum(kf, 30.0))
            ekv = ek * vf

            def step(carry, x):
                a, b = carry
                ekv_t, ek_t = x
                a = a * decay + ekv_t
                b = b * decay + ek_t
                return ((a, b), (a, b))
            ekv_t = jnp.swapaxes(ekv, 0, 1)
            ek_t = jnp.swapaxes(ek, 0, 1)
            init = (jnp.zeros_like(decay), jnp.zeros_like(decay))
            _, (nf, df) = lax.scan(step, init, (ekv_t, ek_t))
            _, (nb, db) = lax.scan(step, init, (ekv_t, ek_t), reverse=True)
            nf = jnp.swapaxes(nf, 0, 1)
            df = jnp.swapaxes(df, 0, 1)
            nb = jnp.swapaxes(nb, 0, 1)
            db = jnp.swapaxes(db, 0, 1)
            euk = jnp.exp(jnp.minimum(u.astype(jnp.float32)[None, None, :] + kf, 30.0))
            num = nf + nb - ekv + euk * vf
            den = df + db - ek + euk
            base = jax.nn.sigmoid(r.astype(jnp.float32)) * (num / jnp.maximum(den, 1e-08))
            out = base * (0.8 + 0.2 * tf)
            return out.astype(r.dtype)
        key = jax.random.key(seed)
        ks = jax.random.split(key, 6)
        return {'r': jax.random.normal(ks[0], (B, T, C), dtype=jnp.float32), 'k': jax.random.normal(ks[1], (B, T, C), dtype=jnp.float32), 'v': jax.random.normal(ks[2], (B, T, C), dtype=jnp.float32), 'w': jax.random.normal(ks[3], (C,), dtype=jnp.float32), 'u': jax.random.normal(ks[4], (C,), dtype=jnp.float32), 'time_emb': jax.random.normal(ks[5], (B, TD), dtype=jnp.float32)}
    _L0_cond2_all = _L0_cond2_setup()
    _L0_cond2_in = {k: v for k, v in _L0_cond2_all.items() if k in ('w', 'u')}
    del _L0_cond2_all

    def _L0_ffn_setup():
        import jax, jax.numpy as jnp
        import numpy as np
        H = 512
        I = 352
        E = 16
        G = 4
        TOPK_GROUP = 2
        TOP_K = 6
        N_SHARED = 2
        SCALE_FACTOR = 2.5
        B, S = (2, 512)

        def _gate(hs_flat, gate_weight, bias):
            T = hs_flat.shape[0]
            logits = hs_flat @ gate_weight.T
            scores = jax.nn.sigmoid(logits)
            scores_for_choice = scores + bias[None, :]
            gs = scores_for_choice.reshape(T, G, E // G)
            group_scores = jnp.sum(jax.lax.top_k(gs, 2)[0], axis=-1)
            _, group_idx = jax.lax.top_k(group_scores, TOPK_GROUP)
            group_mask = jnp.zeros((T, G), scores.dtype).at[jnp.arange(T)[:, None], group_idx].set(1.0)
            score_mask = jnp.repeat(group_mask, E // G, axis=1)
            tmp_scores = jnp.where(score_mask > 0, scores_for_choice, 0.0)
            _, topk_idx = jax.lax.top_k(tmp_scores, TOP_K)
            topk_weight = jnp.take_along_axis(scores, topk_idx, axis=1)
            topk_weight = topk_weight / (jnp.sum(topk_weight, axis=-1, keepdims=True) + 1e-20)
            topk_weight = topk_weight * SCALE_FACTOR
            return (topk_idx, topk_weight)
        key = jax.random.key(seed)
        ks = jax.random.split(key, 8)
        scale = 0.01
        SI = I * N_SHARED
        return {'hidden_states': jax.random.normal(ks[0], (B, S, H), jnp.float32), 'gate_weight': jax.random.uniform(ks[1], (E, H), jnp.float32, -0.05, 0.05), 'e_score_correction_bias': jnp.zeros((E,), jnp.float32), 'gate_proj': jax.random.normal(ks[2], (E, I, H), jnp.float32) * scale, 'up_proj': jax.random.normal(ks[3], (E, I, H), jnp.float32) * scale, 'down_proj': jax.random.normal(ks[4], (E, H, I), jnp.float32) * scale, 'shared_gate_w': jax.random.normal(ks[5], (SI, H), jnp.float32) * scale, 'shared_up_w': jax.random.normal(ks[6], (SI, H), jnp.float32) * scale, 'shared_down_w': jax.random.normal(ks[7], (H, SI), jnp.float32) * scale}
    _L0_ffn_all = _L0_ffn_setup()
    _L0_ffn_in = {k: v for k, v in _L0_ffn_all.items() if k in ('gate_weight', 'e_score_correction_bias', 'gate_proj', 'up_proj', 'down_proj', 'shared_gate_w', 'shared_up_w', 'shared_down_w')}
    del _L0_ffn_all

    def _L1_cond_setup():
        import jax, jax.numpy as jnp
        from jax import lax
        import numpy as np
        B, T, C, TD = (8, 512, 512, 128)

        def _bi_wkv(r, k, v, w, u, time_emb):
            tf = jax.nn.sigmoid(jnp.sum(time_emb, axis=-1))[:, None, None]
            decay = jnp.exp(-jnp.exp(w.astype(jnp.float32)))[None, :] * (0.5 + 0.5 * tf[:, :, 0])
            kf = k.astype(jnp.float32)
            vf = v.astype(jnp.float32)
            ek = jnp.exp(jnp.minimum(kf, 30.0))
            ekv = ek * vf

            def step(carry, x):
                a, b = carry
                ekv_t, ek_t = x
                a = a * decay + ekv_t
                b = b * decay + ek_t
                return ((a, b), (a, b))
            ekv_t = jnp.swapaxes(ekv, 0, 1)
            ek_t = jnp.swapaxes(ek, 0, 1)
            init = (jnp.zeros_like(decay), jnp.zeros_like(decay))
            _, (nf, df) = lax.scan(step, init, (ekv_t, ek_t))
            _, (nb, db) = lax.scan(step, init, (ekv_t, ek_t), reverse=True)
            nf = jnp.swapaxes(nf, 0, 1)
            df = jnp.swapaxes(df, 0, 1)
            nb = jnp.swapaxes(nb, 0, 1)
            db = jnp.swapaxes(db, 0, 1)
            euk = jnp.exp(jnp.minimum(u.astype(jnp.float32)[None, None, :] + kf, 30.0))
            num = nf + nb - ekv + euk * vf
            den = df + db - ek + euk
            base = jax.nn.sigmoid(r.astype(jnp.float32)) * (num / jnp.maximum(den, 1e-08))
            out = base * (0.8 + 0.2 * tf)
            return out.astype(r.dtype)
        key = jax.random.key(seed)
        ks = jax.random.split(key, 6)
        return {'r': jax.random.normal(ks[0], (B, T, C), dtype=jnp.float32), 'k': jax.random.normal(ks[1], (B, T, C), dtype=jnp.float32), 'v': jax.random.normal(ks[2], (B, T, C), dtype=jnp.float32), 'w': jax.random.normal(ks[3], (C,), dtype=jnp.float32), 'u': jax.random.normal(ks[4], (C,), dtype=jnp.float32), 'time_emb': jax.random.normal(ks[5], (B, TD), dtype=jnp.float32)}
    _L1_cond_all = _L1_cond_setup()
    _L1_cond_in = {k: v for k, v in _L1_cond_all.items() if k in ('w', 'u')}
    del _L1_cond_all

    def _L1_attn_setup():
        import jax, jax.numpy as jnp
        import numpy as np
        DIM = 512
        EXPAND = 2
        D_STATE = 64
        HEADDIM = 64
        NGROUPS = 1
        CHUNK = 64
        GROUP_SIZE = 128
        D_INNER = EXPAND * DIM
        NHEADS = D_INNER // HEADDIM
        D_IN_PROJ = 2 * D_INNER + 2 * NGROUPS * D_STATE + NHEADS
        RMS_EPS = 1.1920929e-07
        EXP_CLAMP = 10000.0

        def fq4(w, gs=GROUP_SIZE):
            shp = w.shape
            wr = w.reshape(-1, gs)
            scale = jnp.maximum(jnp.max(jnp.abs(wr), axis=-1, keepdims=True), 1e-10) / 7.0
            wdq = (jnp.clip(jnp.round(wr / scale), -8, 7) * scale).reshape(shp)
            return w + jax.lax.stop_gradient(wdq - w)

        def rmsnorm(x):
            return x * jax.lax.rsqrt(jnp.mean(x * x, axis=-1, keepdims=True) + RMS_EPS)

        def apply_rope(mat, cos, sin):
            real, imag = jnp.split(mat, 2, axis=-1)
            return jnp.concatenate([real * cos - imag * sin, real * sin + imag * cos], axis=-1)

        def segsum(x):
            T = x.shape[-1]
            low = jnp.tril(jnp.ones((T, T), bool), -1)
            cs = jnp.cumsum(jnp.where(low, x[..., :, None], 0.0), axis=-2)
            return jnp.where(jnp.tril(jnp.ones((T, T), bool)), cs, -jnp.inf)

        def ssd_chunk(X, A, Bm, Cm):
            b, s, h, p = X.shape
            n = Bm.shape[-1]
            c, Q = (s // CHUNK, CHUNK)
            X = X.reshape(b, c, Q, h, p)
            A = A.reshape(b, c, Q, h).transpose(0, 3, 1, 2)
            Bm = Bm.reshape(b, c, Q, h, n)
            Cm = Cm.reshape(b, c, Q, h, n)
            A_cs = jnp.cumsum(A, axis=-1)
            Lmat = jnp.minimum(jnp.exp(segsum(A)), EXP_CLAMP)
            Y_diag = jnp.einsum('bclhn,bcshn,bhcls,bcshp->bclhp', Cm, Bm, Lmat, X)
            decay_states = jnp.exp(A_cs[..., -1:] - A_cs)
            states = jnp.einsum('bclhn,bhcl,bclhp->bchpn', Bm, decay_states, X)
            states = jnp.concatenate([jnp.zeros((b, 1, h, p, n), X.dtype), states], axis=1)
            decay_chunk = jnp.minimum(jnp.exp(segsum(jnp.pad(A_cs[..., -1], ((0, 0), (0, 0), (1, 0))))), EXP_CLAMP)
            new_states = jnp.einsum('bhzc,bchpn->bzhpn', decay_chunk, states)
            final_state = new_states[:, -1]
            inter = new_states[:, :-1]
            Y_off = jnp.einsum('bclhn,bchpn,bhcl->bclhp', Cm, inter, jnp.exp(A_cs))
            return ((Y_diag + Y_off).reshape(b, s, h, p), final_state)
        key = jax.random.key(seed)
        ks = jax.random.split(key, 8)
        B, L = (2, 1024)
        return {'x': jax.random.normal(ks[0], (B, L, DIM), jnp.float32), 'W_in': jax.random.normal(ks[1], (D_IN_PROJ, DIM), jnp.float32) * 0.02, 'W_theta': jax.random.normal(ks[2], (NGROUPS * (D_STATE // 2), DIM), jnp.float32) * 0.02, 'W_lambda': jax.random.normal(ks[3], (NHEADS, DIM), jnp.float32) * 0.02, 'W_out': jax.random.normal(ks[4], (DIM, D_INNER), jnp.float32) * 0.02, 'B_bias': jnp.ones((NGROUPS, D_STATE), jnp.float32), 'C_bias': jnp.ones((NGROUPS, D_STATE), jnp.float32), 'A_log': jnp.linspace(-4.5, 0.5, NHEADS).astype(jnp.float32) + jax.random.normal(ks[5], (NHEADS,), jnp.float32) * 0.1, 'D_param': jnp.ones((NHEADS,), jnp.float32), 'dt_bias': jnp.full((NHEADS,), -3.0, jnp.float32)}
    _L1_attn_all = _L1_attn_setup()
    _L1_attn_in = {k: v for k, v in _L1_attn_all.items() if k in ('W_in', 'W_theta', 'W_lambda', 'W_out', 'B_bias', 'C_bias', 'A_log', 'D_param', 'dt_bias')}
    del _L1_attn_all

    def _L1_cond2_setup():
        import jax, jax.numpy as jnp
        from jax import lax
        import numpy as np
        B, T, C, TD = (8, 512, 512, 128)

        def _bi_wkv(r, k, v, w, u, time_emb):
            tf = jax.nn.sigmoid(jnp.sum(time_emb, axis=-1))[:, None, None]
            decay = jnp.exp(-jnp.exp(w.astype(jnp.float32)))[None, :] * (0.5 + 0.5 * tf[:, :, 0])
            kf = k.astype(jnp.float32)
            vf = v.astype(jnp.float32)
            ek = jnp.exp(jnp.minimum(kf, 30.0))
            ekv = ek * vf

            def step(carry, x):
                a, b = carry
                ekv_t, ek_t = x
                a = a * decay + ekv_t
                b = b * decay + ek_t
                return ((a, b), (a, b))
            ekv_t = jnp.swapaxes(ekv, 0, 1)
            ek_t = jnp.swapaxes(ek, 0, 1)
            init = (jnp.zeros_like(decay), jnp.zeros_like(decay))
            _, (nf, df) = lax.scan(step, init, (ekv_t, ek_t))
            _, (nb, db) = lax.scan(step, init, (ekv_t, ek_t), reverse=True)
            nf = jnp.swapaxes(nf, 0, 1)
            df = jnp.swapaxes(df, 0, 1)
            nb = jnp.swapaxes(nb, 0, 1)
            db = jnp.swapaxes(db, 0, 1)
            euk = jnp.exp(jnp.minimum(u.astype(jnp.float32)[None, None, :] + kf, 30.0))
            num = nf + nb - ekv + euk * vf
            den = df + db - ek + euk
            base = jax.nn.sigmoid(r.astype(jnp.float32)) * (num / jnp.maximum(den, 1e-08))
            out = base * (0.8 + 0.2 * tf)
            return out.astype(r.dtype)
        key = jax.random.key(seed)
        ks = jax.random.split(key, 6)
        return {'r': jax.random.normal(ks[0], (B, T, C), dtype=jnp.float32), 'k': jax.random.normal(ks[1], (B, T, C), dtype=jnp.float32), 'v': jax.random.normal(ks[2], (B, T, C), dtype=jnp.float32), 'w': jax.random.normal(ks[3], (C,), dtype=jnp.float32), 'u': jax.random.normal(ks[4], (C,), dtype=jnp.float32), 'time_emb': jax.random.normal(ks[5], (B, TD), dtype=jnp.float32)}
    _L1_cond2_all = _L1_cond2_setup()
    _L1_cond2_in = {k: v for k, v in _L1_cond2_all.items() if k in ('w', 'u')}
    del _L1_cond2_all

    def _L1_ffn_setup():
        import jax, jax.numpy as jnp
        import numpy as np
        _FP8_MAX = 448.0
        _BLOCK = 32
        _EPS = 1e-30

        def _mx_dequant(t):
            rows, feat = t.shape
            blocks = t.reshape(rows, feat // _BLOCK, _BLOCK)
            max_abs = jnp.max(jnp.abs(blocks), axis=-1)
            scales = jnp.maximum(max_abs / _FP8_MAX, _EPS)
            q = (blocks / scales[..., None]).astype(jnp.float8_e4m3fn).astype(jnp.float32)
            return (q * scales[..., None]).reshape(rows, feat)

        def _mx_linear(x2d, w):
            return _mx_dequant(x2d) @ _mx_dequant(w).T
        key = jax.random.key(seed)
        k1, k2, k3, k4 = jax.random.split(key, 4)
        B, S, H, I = (2, 256, 512, 2048)
        return {'x': jax.random.normal(k1, (B, S, H), dtype=jnp.float32), 'gate_w': jax.random.normal(k2, (I, H), dtype=jnp.float32) * 0.02, 'up_w': jax.random.normal(k3, (I, H), dtype=jnp.float32) * 0.02, 'down_w': jax.random.normal(k4, (H, I), dtype=jnp.float32) * 0.02}
    _L1_ffn_all = _L1_ffn_setup()
    _L1_ffn_in = {k: v for k, v in _L1_ffn_all.items() if k in ('gate_w', 'up_w', 'down_w')}
    del _L1_ffn_all
    return {'x': x, 'fside_BxSxS_0': fside_BxSxS_0, 'cond_512': cond_512, 'L0_cond_w': _L0_cond_in['w'], 'L0_cond_u': _L0_cond_in['u'], 'L0_attn_Wq': _L0_attn_in['Wq'], 'L0_attn_Wk': _L0_attn_in['Wk'], 'L0_attn_Wv': _L0_attn_in['Wv'], 'L0_attn_Wg': _L0_attn_in['Wg'], 'L0_attn_Wo': _L0_attn_in['Wo'], 'L0_attn_gamma': _L0_attn_in['gamma'], 'L0_attn_beta': _L0_attn_in['beta'], 'L0_cond2_w': _L0_cond2_in['w'], 'L0_cond2_u': _L0_cond2_in['u'], 'L0_ffn_gate_weight': _L0_ffn_in['gate_weight'], 'L0_ffn_e_score_correction_bias': _L0_ffn_in['e_score_correction_bias'], 'L0_ffn_gate_proj': _L0_ffn_in['gate_proj'], 'L0_ffn_up_proj': _L0_ffn_in['up_proj'], 'L0_ffn_down_proj': _L0_ffn_in['down_proj'], 'L0_ffn_shared_gate_w': _L0_ffn_in['shared_gate_w'], 'L0_ffn_shared_up_w': _L0_ffn_in['shared_up_w'], 'L0_ffn_shared_down_w': _L0_ffn_in['shared_down_w'], 'L1_cond_w': _L1_cond_in['w'], 'L1_cond_u': _L1_cond_in['u'], 'L1_attn_W_in': _L1_attn_in['W_in'], 'L1_attn_W_theta': _L1_attn_in['W_theta'], 'L1_attn_W_lambda': _L1_attn_in['W_lambda'], 'L1_attn_W_out': _L1_attn_in['W_out'], 'L1_attn_B_bias': _L1_attn_in['B_bias'], 'L1_attn_C_bias': _L1_attn_in['C_bias'], 'L1_attn_A_log': _L1_attn_in['A_log'], 'L1_attn_D_param': _L1_attn_in['D_param'], 'L1_attn_dt_bias': _L1_attn_in['dt_bias'], 'L1_cond2_w': _L1_cond2_in['w'], 'L1_cond2_u': _L1_cond2_in['u'], 'L1_ffn_gate_w': _L1_ffn_in['gate_w'], 'L1_ffn_up_w': _L1_ffn_in['up_w'], 'L1_ffn_down_w': _L1_ffn_in['down_w']}

def reference(x, fside_BxSxS_0, cond_512, L0_cond_w, L0_cond_u, L0_attn_Wq, L0_attn_Wk, L0_attn_Wv, L0_attn_Wg, L0_attn_Wo, L0_attn_gamma, L0_attn_beta, L0_cond2_w, L0_cond2_u, L0_ffn_gate_weight, L0_ffn_e_score_correction_bias, L0_ffn_gate_proj, L0_ffn_up_proj, L0_ffn_down_proj, L0_ffn_shared_gate_w, L0_ffn_shared_up_w, L0_ffn_shared_down_w, L1_cond_w, L1_cond_u, L1_attn_W_in, L1_attn_W_theta, L1_attn_W_lambda, L1_attn_W_out, L1_attn_B_bias, L1_attn_C_bias, L1_attn_A_log, L1_attn_D_param, L1_attn_dt_bias, L1_cond2_w, L1_cond2_u, L1_ffn_gate_w, L1_ffn_up_w, L1_ffn_down_w):
    import jax
    import jax.numpy as jnp

    def _L0_cond_ref(r, k, v, w, u, time_emb):
        import jax, jax.numpy as jnp
        from jax import lax
        import numpy as np
        B, T, C, TD = (8, 512, 512, 128)

        def _bi_wkv(r, k, v, w, u, time_emb):
            tf = jax.nn.sigmoid(jnp.sum(time_emb, axis=-1))[:, None, None]
            decay = jnp.exp(-jnp.exp(w.astype(jnp.float32)))[None, :] * (0.5 + 0.5 * tf[:, :, 0])
            kf = k.astype(jnp.float32)
            vf = v.astype(jnp.float32)
            ek = jnp.exp(jnp.minimum(kf, 30.0))
            ekv = ek * vf

            def step(carry, x):
                a, b = carry
                ekv_t, ek_t = x
                a = a * decay + ekv_t
                b = b * decay + ek_t
                return ((a, b), (a, b))
            ekv_t = jnp.swapaxes(ekv, 0, 1)
            ek_t = jnp.swapaxes(ek, 0, 1)
            init = (jnp.zeros_like(decay), jnp.zeros_like(decay))
            _, (nf, df) = lax.scan(step, init, (ekv_t, ek_t))
            _, (nb, db) = lax.scan(step, init, (ekv_t, ek_t), reverse=True)
            nf = jnp.swapaxes(nf, 0, 1)
            df = jnp.swapaxes(df, 0, 1)
            nb = jnp.swapaxes(nb, 0, 1)
            db = jnp.swapaxes(db, 0, 1)
            euk = jnp.exp(jnp.minimum(u.astype(jnp.float32)[None, None, :] + kf, 30.0))
            num = nf + nb - ekv + euk * vf
            den = df + db - ek + euk
            base = jax.nn.sigmoid(r.astype(jnp.float32)) * (num / jnp.maximum(den, 1e-08))
            out = base * (0.8 + 0.2 * tf)
            return out.astype(r.dtype)
        return _bi_wkv(r, k, v, w, u, time_emb)

    def _L0_attn_ref(x, Wq, Wk, Wv, Wg, Wo, gamma, beta):
        import jax, jax.numpy as jnp
        import numpy as np
        B, L, D, H = (2, 1024, 512, 16)
        K = D // H
        V = D // H
        EPS = 1e-05

        def _gla_recurrence(q, k, v, g):
            qs = jnp.moveaxis(q, 1, 0)
            ks = jnp.moveaxis(k, 1, 0)
            vs = jnp.moveaxis(v, 1, 0)
            gs = jnp.moveaxis(g, 1, 0)

            def step(S, inp):
                qt, kt, vt, gt = inp
                S = S * jnp.exp(gt)[..., None] + kt[..., None] * vt[..., None, :]
                yt = jnp.einsum('bhk,bhkv->bhv', qt, S)
                return (S, yt)
            S0 = jnp.zeros((q.shape[0], H, K, V), q.dtype)
            S_final, ys = jax.lax.scan(step, S0, (qs, ks, vs, gs))
            return (jnp.moveaxis(ys, 0, 1), S_final)

        def _layernorm(x, gamma, beta):
            mu = jnp.mean(x, axis=-1, keepdims=True)
            var = jnp.mean(jnp.square(x - mu), axis=-1, keepdims=True)
            return (x - mu) * jax.lax.rsqrt(var + EPS) * gamma + beta

        def _reference_tuple_inner(x, Wq, Wk, Wv, Wg, Wo, gamma, beta):
            b, l, d = x.shape
            q = (x @ Wq.T).reshape(b, l, H, K) * K ** (-0.5)
            k = (x @ Wk.T).reshape(b, l, H, K)
            v = (x @ Wv.T).reshape(b, l, H, V)
            g = jax.nn.log_sigmoid(x @ Wg.T).reshape(b, l, H, K)
            y, final_state = _gla_recurrence(q, k, v, g)
            y = y.reshape(b, l, d)
            o = _layernorm(y, gamma, beta) @ Wo.T
            return (o, final_state)
        return _reference_tuple_inner(x, Wq, Wk, Wv, Wg, Wo, gamma, beta)[0]

    def _L0_cond2_ref(r, k, v, w, u, time_emb):
        import jax, jax.numpy as jnp
        from jax import lax
        import numpy as np
        B, T, C, TD = (8, 512, 512, 128)

        def _bi_wkv(r, k, v, w, u, time_emb):
            tf = jax.nn.sigmoid(jnp.sum(time_emb, axis=-1))[:, None, None]
            decay = jnp.exp(-jnp.exp(w.astype(jnp.float32)))[None, :] * (0.5 + 0.5 * tf[:, :, 0])
            kf = k.astype(jnp.float32)
            vf = v.astype(jnp.float32)
            ek = jnp.exp(jnp.minimum(kf, 30.0))
            ekv = ek * vf

            def step(carry, x):
                a, b = carry
                ekv_t, ek_t = x
                a = a * decay + ekv_t
                b = b * decay + ek_t
                return ((a, b), (a, b))
            ekv_t = jnp.swapaxes(ekv, 0, 1)
            ek_t = jnp.swapaxes(ek, 0, 1)
            init = (jnp.zeros_like(decay), jnp.zeros_like(decay))
            _, (nf, df) = lax.scan(step, init, (ekv_t, ek_t))
            _, (nb, db) = lax.scan(step, init, (ekv_t, ek_t), reverse=True)
            nf = jnp.swapaxes(nf, 0, 1)
            df = jnp.swapaxes(df, 0, 1)
            nb = jnp.swapaxes(nb, 0, 1)
            db = jnp.swapaxes(db, 0, 1)
            euk = jnp.exp(jnp.minimum(u.astype(jnp.float32)[None, None, :] + kf, 30.0))
            num = nf + nb - ekv + euk * vf
            den = df + db - ek + euk
            base = jax.nn.sigmoid(r.astype(jnp.float32)) * (num / jnp.maximum(den, 1e-08))
            out = base * (0.8 + 0.2 * tf)
            return out.astype(r.dtype)
        return _bi_wkv(r, k, v, w, u, time_emb)

    def _L0_ffn_ref(hidden_states, gate_weight, e_score_correction_bias, gate_proj, up_proj, down_proj, shared_gate_w, shared_up_w, shared_down_w):
        import jax, jax.numpy as jnp
        import numpy as np
        H = 512
        I = 352
        E = 16
        G = 4
        TOPK_GROUP = 2
        TOP_K = 6
        N_SHARED = 2
        SCALE_FACTOR = 2.5
        B, S = (2, 512)

        def _gate(hs_flat, gate_weight, bias):
            T = hs_flat.shape[0]
            logits = hs_flat @ gate_weight.T
            scores = jax.nn.sigmoid(logits)
            scores_for_choice = scores + bias[None, :]
            gs = scores_for_choice.reshape(T, G, E // G)
            group_scores = jnp.sum(jax.lax.top_k(gs, 2)[0], axis=-1)
            _, group_idx = jax.lax.top_k(group_scores, TOPK_GROUP)
            group_mask = jnp.zeros((T, G), scores.dtype).at[jnp.arange(T)[:, None], group_idx].set(1.0)
            score_mask = jnp.repeat(group_mask, E // G, axis=1)
            tmp_scores = jnp.where(score_mask > 0, scores_for_choice, 0.0)
            _, topk_idx = jax.lax.top_k(tmp_scores, TOP_K)
            topk_weight = jnp.take_along_axis(scores, topk_idx, axis=1)
            topk_weight = topk_weight / (jnp.sum(topk_weight, axis=-1, keepdims=True) + 1e-20)
            topk_weight = topk_weight * SCALE_FACTOR
            return (topk_idx, topk_weight)
        b, s, h = hidden_states.shape
        hs = hidden_states.reshape(-1, h)
        T = hs.shape[0]
        topk_idx, topk_weight = _gate(hs, gate_weight, e_score_correction_bias)
        comb = jnp.zeros((T, E), hs.dtype).at[jnp.arange(T)[:, None], topk_idx].add(topk_weight)
        out = jnp.zeros_like(hs)
        for e in range(E):
            g = hs @ gate_proj[e].T
            u = hs @ up_proj[e].T
            inter = jax.nn.silu(g) * u
            out = out + comb[:, e:e + 1] * (inter @ down_proj[e].T)
        y = out.reshape(b, s, h)
        sg = hidden_states @ shared_gate_w.T
        su = hidden_states @ shared_up_w.T
        shared_out = jax.nn.silu(sg) * su @ shared_down_w.T
        return y + shared_out

    def _L1_cond_ref(r, k, v, w, u, time_emb):
        import jax, jax.numpy as jnp
        from jax import lax
        import numpy as np
        B, T, C, TD = (8, 512, 512, 128)

        def _bi_wkv(r, k, v, w, u, time_emb):
            tf = jax.nn.sigmoid(jnp.sum(time_emb, axis=-1))[:, None, None]
            decay = jnp.exp(-jnp.exp(w.astype(jnp.float32)))[None, :] * (0.5 + 0.5 * tf[:, :, 0])
            kf = k.astype(jnp.float32)
            vf = v.astype(jnp.float32)
            ek = jnp.exp(jnp.minimum(kf, 30.0))
            ekv = ek * vf

            def step(carry, x):
                a, b = carry
                ekv_t, ek_t = x
                a = a * decay + ekv_t
                b = b * decay + ek_t
                return ((a, b), (a, b))
            ekv_t = jnp.swapaxes(ekv, 0, 1)
            ek_t = jnp.swapaxes(ek, 0, 1)
            init = (jnp.zeros_like(decay), jnp.zeros_like(decay))
            _, (nf, df) = lax.scan(step, init, (ekv_t, ek_t))
            _, (nb, db) = lax.scan(step, init, (ekv_t, ek_t), reverse=True)
            nf = jnp.swapaxes(nf, 0, 1)
            df = jnp.swapaxes(df, 0, 1)
            nb = jnp.swapaxes(nb, 0, 1)
            db = jnp.swapaxes(db, 0, 1)
            euk = jnp.exp(jnp.minimum(u.astype(jnp.float32)[None, None, :] + kf, 30.0))
            num = nf + nb - ekv + euk * vf
            den = df + db - ek + euk
            base = jax.nn.sigmoid(r.astype(jnp.float32)) * (num / jnp.maximum(den, 1e-08))
            out = base * (0.8 + 0.2 * tf)
            return out.astype(r.dtype)
        return _bi_wkv(r, k, v, w, u, time_emb)

    def _L1_attn_ref(x, W_in, W_theta, W_lambda, W_out, B_bias, C_bias, A_log, D_param, dt_bias):
        import jax, jax.numpy as jnp
        import numpy as np
        DIM = 512
        EXPAND = 2
        D_STATE = 64
        HEADDIM = 64
        NGROUPS = 1
        CHUNK = 64
        GROUP_SIZE = 128
        D_INNER = EXPAND * DIM
        NHEADS = D_INNER // HEADDIM
        D_IN_PROJ = 2 * D_INNER + 2 * NGROUPS * D_STATE + NHEADS
        RMS_EPS = 1.1920929e-07
        EXP_CLAMP = 10000.0

        def fq4(w, gs=GROUP_SIZE):
            shp = w.shape
            wr = w.reshape(-1, gs)
            scale = jnp.maximum(jnp.max(jnp.abs(wr), axis=-1, keepdims=True), 1e-10) / 7.0
            wdq = (jnp.clip(jnp.round(wr / scale), -8, 7) * scale).reshape(shp)
            return w + jax.lax.stop_gradient(wdq - w)

        def rmsnorm(x):
            return x * jax.lax.rsqrt(jnp.mean(x * x, axis=-1, keepdims=True) + RMS_EPS)

        def apply_rope(mat, cos, sin):
            real, imag = jnp.split(mat, 2, axis=-1)
            return jnp.concatenate([real * cos - imag * sin, real * sin + imag * cos], axis=-1)

        def segsum(x):
            T = x.shape[-1]
            low = jnp.tril(jnp.ones((T, T), bool), -1)
            cs = jnp.cumsum(jnp.where(low, x[..., :, None], 0.0), axis=-2)
            return jnp.where(jnp.tril(jnp.ones((T, T), bool)), cs, -jnp.inf)

        def ssd_chunk(X, A, Bm, Cm):
            b, s, h, p = X.shape
            n = Bm.shape[-1]
            c, Q = (s // CHUNK, CHUNK)
            X = X.reshape(b, c, Q, h, p)
            A = A.reshape(b, c, Q, h).transpose(0, 3, 1, 2)
            Bm = Bm.reshape(b, c, Q, h, n)
            Cm = Cm.reshape(b, c, Q, h, n)
            A_cs = jnp.cumsum(A, axis=-1)
            Lmat = jnp.minimum(jnp.exp(segsum(A)), EXP_CLAMP)
            Y_diag = jnp.einsum('bclhn,bcshn,bhcls,bcshp->bclhp', Cm, Bm, Lmat, X)
            decay_states = jnp.exp(A_cs[..., -1:] - A_cs)
            states = jnp.einsum('bclhn,bhcl,bclhp->bchpn', Bm, decay_states, X)
            states = jnp.concatenate([jnp.zeros((b, 1, h, p, n), X.dtype), states], axis=1)
            decay_chunk = jnp.minimum(jnp.exp(segsum(jnp.pad(A_cs[..., -1], ((0, 0), (0, 0), (1, 0))))), EXP_CLAMP)
            new_states = jnp.einsum('bhzc,bchpn->bzhpn', decay_chunk, states)
            final_state = new_states[:, -1]
            inter = new_states[:, :-1]
            Y_off = jnp.einsum('bclhn,bchpn,bhcl->bclhp', Cm, inter, jnp.exp(A_cs))
            return ((Y_diag + Y_off).reshape(b, s, h, p), final_state)
        Bsz, L, _ = x.shape
        zxBCdt = x @ fq4(W_in).T
        z = zxBCdt[..., :D_INNER]
        xBC = zxBCdt[..., D_INNER:2 * D_INNER + 2 * NGROUPS * D_STATE]
        dt_raw = zxBCdt[..., -NHEADS:]
        x_conv = xBC[..., :D_INNER]
        Bm = xBC[..., D_INNER:D_INNER + NGROUPS * D_STATE].reshape(Bsz, L, NGROUPS, D_STATE)
        Cm = xBC[..., D_INNER + NGROUPS * D_STATE:].reshape(Bsz, L, NGROUPS, D_STATE)
        x_heads = jax.nn.silu(x_conv).reshape(Bsz, L, NHEADS, HEADDIM)
        Bm = rmsnorm(Bm) + B_bias
        Cm = rmsnorm(Cm) + C_bias
        dt = jax.nn.softplus(dt_raw + dt_bias)
        A_disc = -jnp.exp(A_log)[None, None, :] * dt
        theta = (x @ fq4(W_theta).T).reshape(Bsz, L, NGROUPS, D_STATE // 2)
        dt_avg = jnp.mean(dt, axis=-1, keepdims=True)[..., None]
        angles = jnp.cumsum(theta * dt_avg, axis=1)
        cos_a, sin_a = (jnp.cos(angles), jnp.sin(angles))
        Bm = apply_rope(Bm, cos_a, sin_a)
        Cm = apply_rope(Cm, cos_a, sin_a)
        if NGROUPS < NHEADS:
            Bm = jnp.repeat(Bm, NHEADS // NGROUPS, axis=2)
            Cm = jnp.repeat(Cm, NHEADS // NGROUPS, axis=2)
        lam = jax.nn.sigmoid(x @ fq4(W_lambda).T)
        gamma = lam * dt
        beta = (1.0 - lam) * dt * jnp.exp(A_disc)
        X = x_heads * gamma[..., None] + jnp.pad(x_heads[:, :-1] * beta[:, 1:, :, None], ((0, 0), (1, 0), (0, 0), (0, 0)))
        Y, _ = ssd_chunk(X, A_disc, Bm, Cm)
        Y = Y + x_heads * D_param[:, None]
        Y = Y.reshape(Bsz, L, D_INNER) * jax.nn.silu(z)
        return rmsnorm(Y) @ fq4(W_out).T

    def _L1_cond2_ref(r, k, v, w, u, time_emb):
        import jax, jax.numpy as jnp
        from jax import lax
        import numpy as np
        B, T, C, TD = (8, 512, 512, 128)

        def _bi_wkv(r, k, v, w, u, time_emb):
            tf = jax.nn.sigmoid(jnp.sum(time_emb, axis=-1))[:, None, None]
            decay = jnp.exp(-jnp.exp(w.astype(jnp.float32)))[None, :] * (0.5 + 0.5 * tf[:, :, 0])
            kf = k.astype(jnp.float32)
            vf = v.astype(jnp.float32)
            ek = jnp.exp(jnp.minimum(kf, 30.0))
            ekv = ek * vf

            def step(carry, x):
                a, b = carry
                ekv_t, ek_t = x
                a = a * decay + ekv_t
                b = b * decay + ek_t
                return ((a, b), (a, b))
            ekv_t = jnp.swapaxes(ekv, 0, 1)
            ek_t = jnp.swapaxes(ek, 0, 1)
            init = (jnp.zeros_like(decay), jnp.zeros_like(decay))
            _, (nf, df) = lax.scan(step, init, (ekv_t, ek_t))
            _, (nb, db) = lax.scan(step, init, (ekv_t, ek_t), reverse=True)
            nf = jnp.swapaxes(nf, 0, 1)
            df = jnp.swapaxes(df, 0, 1)
            nb = jnp.swapaxes(nb, 0, 1)
            db = jnp.swapaxes(db, 0, 1)
            euk = jnp.exp(jnp.minimum(u.astype(jnp.float32)[None, None, :] + kf, 30.0))
            num = nf + nb - ekv + euk * vf
            den = df + db - ek + euk
            base = jax.nn.sigmoid(r.astype(jnp.float32)) * (num / jnp.maximum(den, 1e-08))
            out = base * (0.8 + 0.2 * tf)
            return out.astype(r.dtype)
        return _bi_wkv(r, k, v, w, u, time_emb)

    def _L1_ffn_ref(x, gate_w, up_w, down_w):
        import jax, jax.numpy as jnp
        import numpy as np
        _FP8_MAX = 448.0
        _BLOCK = 32
        _EPS = 1e-30

        def _mx_dequant(t):
            rows, feat = t.shape
            blocks = t.reshape(rows, feat // _BLOCK, _BLOCK)
            max_abs = jnp.max(jnp.abs(blocks), axis=-1)
            scales = jnp.maximum(max_abs / _FP8_MAX, _EPS)
            q = (blocks / scales[..., None]).astype(jnp.float8_e4m3fn).astype(jnp.float32)
            return (q * scales[..., None]).reshape(rows, feat)

        def _mx_linear(x2d, w):
            return _mx_dequant(x2d) @ _mx_dequant(w).T
        B, S, H = x.shape
        x2d = x.reshape(B * S, H)
        gate = _mx_linear(x2d, gate_w)
        up = _mx_linear(x2d, up_w)
        h = jax.nn.silu(gate) * up
        out = _mx_linear(h, down_w)
        return out.reshape(B, S, H)
    x = x + _L0_attn_ref(_L0_cond_ref(x, fside_BxSxS_0, fside_BxSxS_0, L0_cond_w, L0_cond_u, cond_512), L0_attn_Wq, L0_attn_Wk, L0_attn_Wv, L0_attn_Wg, L0_attn_Wo, L0_attn_gamma, L0_attn_beta)
    x = x + _L0_ffn_ref(_L0_cond2_ref(x, fside_BxSxS_0, fside_BxSxS_0, L0_cond2_w, L0_cond2_u, cond_512), L0_ffn_gate_weight, L0_ffn_e_score_correction_bias, L0_ffn_gate_proj, L0_ffn_up_proj, L0_ffn_down_proj, L0_ffn_shared_gate_w, L0_ffn_shared_up_w, L0_ffn_shared_down_w)
    x = x + _L1_attn_ref(_L1_cond_ref(x, fside_BxSxS_0, fside_BxSxS_0, L1_cond_w, L1_cond_u, cond_512), L1_attn_W_in, L1_attn_W_theta, L1_attn_W_lambda, L1_attn_W_out, L1_attn_B_bias, L1_attn_C_bias, L1_attn_A_log, L1_attn_D_param, L1_attn_dt_bias)
    x = x + _L1_ffn_ref(_L1_cond2_ref(x, fside_BxSxS_0, fside_BxSxS_0, L1_cond2_w, L1_cond2_u, cond_512), L1_ffn_gate_w, L1_ffn_up_w, L1_ffn_down_w)
    return x

_drawn_inputs = setup_inputs


def setup_inputs(seed=0):
    import zlib

    import numpy as np

    out = dict(_drawn_inputs(seed))
    spreads = {'L0_attn_gamma': (1.0, 0.2),
     'L0_attn_beta': (0.0, 0.1),
     'L0_ffn_e_score_correction_bias': (0.0, 0.8),
     'L1_attn_B_bias': (1.0, 0.6),
     'L1_attn_C_bias': (1.0, 0.6),
     'L1_attn_D_param': (1.0, 0.6),
     'L1_attn_dt_bias': (-3.0, 0.2)}
    factors = {'L0_cond2_w': 8.0,
     'L0_cond2_u': 8.0,
     'L0_ffn_gate_weight': 8.0,
     'L0_ffn_gate_proj': 8.0,
     'L0_ffn_up_proj': 8.0,
     'L0_ffn_down_proj': 8.0,
     'L0_ffn_shared_gate_w': 8.0,
     'L0_ffn_shared_up_w': 8.0,
     'L0_ffn_shared_down_w': 8.0,
     'L1_attn_W_lambda': 8.0,
     'L1_cond2_w': 6.776,
     'L1_cond2_u': 8.0,
     'L1_ffn_gate_w': 3.938,
     'L1_ffn_up_w': 3.943,
     'L1_ffn_down_w': 3.909}
    for name, (base, spread) in spreads.items():
        noise = np.random.default_rng([zlib.crc32(name.encode()), seed]).standard_normal(out[name].shape)
        drawn = base * np.exp(spread * noise) if base else spread * noise
        out[name] = jnp.asarray(drawn.astype(out[name].dtype))
    for name, factor in factors.items():
        out[name] = (out[name] * factor).astype(out[name].dtype)
    return out
```

```python
from contextlib import ExitStack

import concourse.bass as bass
from concourse import mybir
import numpy as np

F32 = mybir.dt.float32
U32 = mybir.dt.uint32
ALU = mybir.AluOpType
ACT = mybir.ActivationFunctionType
AX = mybir.AxisListType

P = 128
NB, T, D = 4, 512, 512
NC = D // P
NT = T // P
LAYERS = 4
GH, GK = 16, 32
HPC = P // GK
NE, EI, NSH = 16, 352, 2
ROWS = NE + NSH
MT_FULL = ROWS * EI // P
MT_TAIL = ROWS * EI - MT_FULL * P
MT = MT_FULL + 1
WSLOTS = 4
SH, SP_, SN = 16, 64, 64
DI = SH * SP_
FI = 2048
FB = FI // 512
QB = 32

MAGIC = 12582912.0
TWO_PI = (6.28125, float(np.float32(2 * np.pi - 6.28125)),
          2 * np.pi - 6.28125 - float(np.float32(2 * np.pi - 6.28125)))


class Event:

    def __init__(self, sem, per, unit=1):
        self.sem, self.per, self.unit = sem, per, unit

    def at(self, b, k):
        return (b * self.per + k) * self.unit


def constant_table():
    parts = {}
    eye = np.eye(P)
    parts["ident"] = eye
    parts["ones"] = np.ones((P, P))
    parts["avg_d"] = np.full((P, P), 1.0 / D)
    parts["shift"] = np.eye(P, k=1)
    edge = np.zeros((P, P))
    edge[P - 1, 0] = 1.0
    parts["edge"] = edge
    red = np.zeros((P, 2 * GK - 1, HPC))
    for h in range(HPC):
        red[h * GK:(h + 1) * GK, GK - 1, h] = 1.0
    parts["red"] = red.reshape(P, -1)
    selv = np.zeros((P, GK, HPC, GK))
    for h in range(HPC):
        for v in range(GK):
            selv[h * GK + v, v, h, :] = 1.0
    parts["selv"] = selv.reshape(P, -1)
    rope = np.zeros((P, SN))
    for m in range(SN // 2):
        rope[m + SN // 2, m] = -1.0
        rope[m, m + SN // 2] = 1.0
    parts["rope"] = rope
    parts["avg_n"] = np.full((P, SN), 1.0 / SN)
    parts["avg_h"] = np.full((P, SN), 1.0 / SH)
    selh = np.zeros((P, SH, P))
    for h in range(SH):
        selh[h, h, :] = 1.0
    parts["selh"] = selh.reshape(P, -1)
    parts["tri"] = np.triu(np.ones((P, P)))
    parts["low16"] = np.tile(np.tril(np.ones((NE, NE)), -1).reshape(1, -1), (P, 1))
    parts["low4"] = np.tile(np.tril(np.ones((4, 4)), -1).reshape(1, -1), (P, 1))
    parts["eps"] = np.tile(np.array([[1e-5, 1.1920929e-07, 1.0, 0.0]]), (P, 1))
    at, n = {}, 0
    for k, v in parts.items():
        at[k] = (n, v.shape[1])
        n += v.shape[1]
    return at, np.concatenate(list(parts.values()), 1).astype(np.float32)


def expert_rows():
    sel = np.zeros((ROWS, ROWS * EI), np.float32)
    for e in range(ROWS):
        sel[e, e * EI:(e + 1) * EI] = 1.0
    return sel


def build(nc, A, out, scratch_fq, scratch_mx):
    cat, ctab = constant_table()
    ctx = ExitStack()
    with ctx:
        def sb(name, cols, parts=P):
            return ctx.enter_context(nc.sbuf_tensor("sb_" + name, [parts, cols], F32))

        def ev(name, per, unit=1):
            return Event(ctx.enter_context(nc.semaphore(name)), per, unit)

        banks = [ctx.enter_context(nc.psum_tensor(f"bank{i}", [P, 512], F32)) for i in range(8)]

        def bank(i, rows=P):
            return banks[i][0:rows, :]

        passed = ctx.enter_context(nc.semaphore("passed"))

        def hold(eng):
            eng.sem_inc(passed, 1)

        const = sb("const", ctab.shape[1])

        def cst(name, rows=P):
            a, n = cat[name]
            return const[0:rows, a:a + n]

        eps_ln, eps_rms, one = (const[:, cat["eps"][0] + i:cat["eps"][0] + i + 1] for i in range(3))
        xT = sb("xT", NC * T)
        fT = sb("fT", NC * T)
        hT = sb("hT", NC * T)
        ek2 = sb("ek2", NC * 2 * T)
        R = sb("R", NC * T)
        small = sb("small", 1024)
        pos = [0]

        def carve(n, parts=P):
            pos[0] += n
            return small[0:parts, pos[0] - n:pos[0]]

        wu = carve(LAYERS * 2 * NC)
        wu4 = wu.rearrange("p (l a c) -> p l a c", l=LAYERS, a=2)
        condT = carve(NB)
        tf = carve(NB)
        dscale = carve(NB)
        oscale = carve(NB)
        dec0 = carve(LAYERS * NC)
        decay = carve(NB * LAYERS * NC)
        decay_b = carve(LAYERS * NC)
        osc_b = carve(1)
        gb = carve(2 * NC)
        gate_bias = carve(NE)
        gwT = carve(NC * NE)
        bcb = carve(2, SN)
        alog = carve(1, SH)
        negA = carve(1, SH)
        dtb = carve(1, SH)
        Dbc = carve(SH)
        csl = carve(NT * SH)
        eL = carve(NT * SH)
        ecs = carve(NT * SH)
        dend = carve(NT * SH)
        ss = carve(4)

        work = sb("work", 26000)

        def w(a, n, parts=P):
            assert a + n <= 26000, (a, n)
            return work[0:parts, a:a + n]

        ld_const = ev("ld_const", 0, 16)
        ld_x = ev("ld_x", 2, 16)
        stored = ev("stored", 1, 16)
        setup_pe = ev("setup_pe", 0)
        setup_act = ev("setup_act", 0)
        setup_dve = ev("setup_dve", 0)
        fmin_ready = ev("fmin_ready", 1)
        ek_ready = ev("ek_ready", 1)
        um_ready = ev("um_ready", LAYERS)
        euk_ready = ev("euk_ready", LAYERS)
        sig_ready = ev("sig_ready", LAYERS)
        h_ready = ev("h_ready", LAYERS)
        x_ready = ev("x_ready", LAYERS)
        prep_ld = [ev(f"prep_ld{i}", 0, 16) for i in range(2)]
        prep_q = ev("prep_q", 0)
        prep_t = ev("prep_t", 0)
        prep_c = ev("prep_c", 0)
        prep_st = [ev(f"prep_st{i}", 0, 16) for i in range(2)]
        ld_gw = ev("ld_gw", NC, 16)
        g_proj = ev("g_proj", NC)
        g_evac = ev("g_evac", NC)
        NS = NC * GK
        g_bc = ev("g_bc", NS)
        g_kv = ev("g_kv", NS)
        g_scan = ev("g_scan", NS)
        g_prod = ev("g_prod", NS)
        g_red = ev("g_red", NS)
        y_evac = ev("y_evac", NC)
        ld_wo = ev("ld_wo", 1, 16)
        ln_mean = ev("ln_mean", 1)
        ln_cent = ev("ln_cent", 1)
        ln_sq = ev("ln_sq", 1)
        ln_var = ev("ln_var", 1)
        ln_sd = ev("ln_sd", 1)
        ln_out = ev("ln_out", 1)
        o_done = ev("o_done", 1)
        m_logit = ev("m_logit", 1)
        m_score = ev("m_score", 1)
        m_comb = ev("m_comb", 1)
        m_combT = ev("m_combT", 1)
        m_combC = ev("m_combC", 1)
        ld_mw = [ev(f"ld_mw{s}", 0, 48) for s in range(WSLOTS)]
        m_gate = ev("m_gate", MT)
        m_up = ev("m_up", MT)
        m_silu = ev("m_silu", MT)
        m_inter = ev("m_inter", MT)
        m_down = ev("m_down", MT)
        ld_sw = ev("ld_sw", 7, 16)
        s_proj = ev("s_proj", 1)
        s_sq = ev("s_sq", 1)
        s_ms = ev("s_ms", 1)
        s_rms = ev("s_rms", 1)
        s_th = ev("s_th", 1)
        s_v = ev("s_v", 1)
        s_ln = ev("s_ln", 1)
        s_dt = ev("s_dt", 1)
        s_dtavg = ev("s_dtavg", 1)
        s_ea = ev("s_ea", 1)
        s_bcn = ev("s_bcn", 1)
        s_perm = ev("s_perm", 1)
        s_ang = ev("s_ang", 1)
        s_sin = ev("s_sin", 1)
        s_rope = ev("s_rope", 1)
        s_tm = ev("s_tm", 1)
        s_tmc = ev("s_tmc", 1)
        s_exps = ev("s_exps", 1)
        s_x = ev("s_x", NT)
        s_silu = ev("s_silu", NT)
        s_shift = ev("s_shift", NT)
        s_xg = ev("s_xg", NT)
        s_cb = ev("s_cb", NT)
        s_gm = ev("s_gm", NT)
        s_csb = ev("s_csb", NT * 4)
        s_diff = ev("s_diff", NT * 4)
        s_exp = ev("s_exp", NT * 4)
        s_m = ev("s_m", NT * 4)
        s_mu = ev("s_mu", NT * 3)
        s_cs = ev("s_cs", 1)
        s_yd = ev("s_yd", NT)
        s_yo = ev("s_yo", NT)
        s_st = ev("s_st", NT)
        s_y = ev("s_y", NT)
        s_yss = ev("s_yss", NT)
        s_yn = ev("s_yn", NT)
        s_tr = ev("s_tr", NT)
        s_ynT = ev("s_ynT", NT)
        s_out = ev("s_out", 1)
        ld_fw = [ev(f"ld_fw{s}", 2, 16) for s in range(2)]
        f_tx = ev("f_tx", NT)
        f_qx = ev("f_qx", NT)
        f_tq = ev("f_tq", NT)
        f_xT = ev("f_xT", NT)
        f_gate = ev("f_gate", NT * FB)
        f_mul = ev("f_mul", NT * FB)
        f_gu = ev("f_gu", NT * FB)
        f_silu = ev("f_silu", NT * FB)
        f_q = ev("f_q", NT * FB)
        f_tr = ev("f_tr", NT * FB)
        f_hT = ev("f_hT", NT * FB)
        f_down = ev("f_down", FB)

        um = w(0, NC * T)
        eu2 = w(2048, NC * 2 * T)
        nf2 = w(6144, 2 * T)
        nb2 = w(7168, 2 * T)
        gw = w(8192, 4 * NC * P).rearrange("p (m c o) -> p m c o", m=4, c=NC)
        qkva = w(10240, 4 * T).rearrange("p (m t) -> p m t", m=4)
        kvb = w(12288, 2 * T).rearrange("p (s t) -> p s t", s=2)
        Sb = w(13312, 2 * T).rearrange("p (s t) -> p s t", s=2)
        Pb = w(14336, 2 * T).rearrange("p (s t) -> p s t", s=2)
        yT = w(15360, NC * T)
        ysq = w(17408, NC * T)
        sdv = w(19456, T)
        wo = w(19968, NC * D).rearrange("p (c o) -> p c o", c=NC)
        mgu = [w(8192 + s * 1664, 1024).rearrange("p (g c i) -> p g c i", g=2, c=NC) for s in range(WSLOTS)]
        mdn = [w(8192 + s * 1664 + 1024, 512) for s in range(WSLOTS)]
        msel = [w(8192 + s * 1664 + 1536, 128, ROWS) for s in range(WSLOTS)]
        combT = w(14848, T, ROWS)
        sgt = w(15360, 2 * T).rearrange("p (s t) -> p s t", s=2)
        inter = w(16384, 2 * T).rearrange("p (s t) -> p s t", s=2)
        tcb = w(17408, T)
        rk = w(18000, 6 * 1024)

        def ch(ap, c):
            return ap[:, c * T:(c + 1) * T]

        block = ctx.enter_context(nc.Block())

        pin = [w(s * 512, 512) for s in range(2)]
        pq = [w(1024 + s * 512, 512) for s in range(2)]
        pt_ = [w(2048 + s * 512, 512) for s in range(2)]
        ptmp = w(3072, 512)
        ptmp2 = w(3584, 512)
        pamx = w(4096, 64)
        NFQ, NMX = 26, 48
        NPREP = NFQ + NMX

        WA = 0
        wzx = w(0, 4 * 2048).rearrange("p (m c o) -> p m c o", m=4, c=NC)
        wout = w(8192, 2 * 2048).rearrange("p (m c o) -> p m c o", m=2, c=4)
        wm6 = w(12288, 1024).rearrange("p (c o) -> p c o", c=NC)
        ynT = w(12288, 8 * T)
        o = 16384
        xh = [w(o + s * 1024, 1024) for s in range(2)]
        zs = w(o + 2048, 1024)
        Xg = w(o + 3072, 1024)
        Xd = w(o + 4096, 1024)
        Yt = w(o + 5120, 1024)
        Md = w(o + 6144, 1024).rearrange("p (s n) -> p s n", s=2)
        state = w(o + 7168, 1024, SN)
        Gm = w(o + 8192, P)
        tm = w(o + 8192 + P, NT * 3 * SH).rearrange("p (k a h) -> p k a h", k=NT, a=3)
        Btm = w(o + 8192 + P + 192, NT * SN).rearrange("p (k n) -> p k n", k=NT)
        o2 = o + 8192 + P + 192 + 256
        small2 = sb("small2", 2 * T + 3 * T)
        BCn = small2[0:SN, 0:2 * T].rearrange("p (a t) -> p a t", a=2)
        dtt = small2[0:SH, 2 * T:3 * T]
        cst_ = small2[0:SH, 3 * T:4 * T]
        gmt = small2[0:SH, 4 * T:5 * T]
        bsq = w(o, 2 * T, SN).rearrange("p (a t) -> p a t", a=2)
        brs = w(o + 1024, 2 * T, SN).rearrange("p (a t) -> p a t", a=2)
        th = w(o + 2048, T, SN)
        ang = w(o + 2560, T, SN)
        trg = w(o + 3072, 2 * T, SN).rearrange("p (a t) -> p a t", a=2)
        nrd = w(o + 4096, 2 * T, SN).rearrange("p (a t) -> p a t", a=2)
        vt = w(o + 5120, T, SH)
        nab = w(o + 5632, T, SH)
        lamt = w(o + 6144, T, SH)
        eat = w(o + 6656, T, SH)
        bet = w(o + 7168, T, SH)
        dl = w(o + 7680, NT * SH, SH)

        fw = [w(s * 6144, 6144).rearrange("p (m c o) -> p m c o", m=3, c=4) for s in range(2)]
        xqT = w(12288, NC * T).rearrange("p (c t) -> p c t", c=NC)
        fs = [w(14336 + s * 512, 512) for s in range(2)]
        fh = w(15360, 512)
        fv = w(15872, 512)
        fm = w(16384, 512)
        fq = [w(16896 + s * 512, 512) for s in range(2)]
        hqT = [w(17920 + s * 2048, 2048).rearrange("p (i t) -> p i t", i=4) for s in range(2)]
        famx = w(22016, 64)

        def r3(ap, n):
            return ap.rearrange("p (a n) -> p a n", n=n)

        def r4(ap):
            return ap[:, :].rearrange("p (c a t) -> p c a t", c=NC, a=2)

        def store_prepared(sp, i):
            s = i % 2
            sp.wait_ge(prep_c.sem, i + 1)
            src = r3(pt_[s], P)
            if i < NFQ:
                dst = scratch_fq[i // 4][:, :, (i % 4) * P:(i % 4 + 1) * P]
            else:
                k = i - NFQ
                dst = scratch_mx[k // 12][(k // 4) % 3][:, :, (k % 4) * P:(k % 4 + 1) * P]
            sp.dma_start(dst, src).then_inc(prep_st[s].sem, 16)

        @block.sync
        def _(sp):
            n = 0
            for dst, src in ((const[:, :], A["consts"]), (condT, A["condT"]),
                             (wu, A["wu"]), (gb, A["gb"]), (gwT, A["gwT"]),
                             (gate_bias, A["gate_bias"].rearrange("(a n) -> a n", a=1).to_broadcast([P, NE])),
                             (bcb, A["bc_bias"]), (alog, A["A_log"].rearrange("(a n) -> a n", n=1)),
                             (dtb, A["dt_bias"].rearrange("(a n) -> a n", n=1)),
                             (Dbc, A["D_param"].rearrange("(a n) -> a n", a=1).to_broadcast([P, SH]))):
                sp.dma_start(dst, src).then_inc(ld_const.sem, 16)
                n += 1
            for i in range(NPREP):
                s = i % 2
                if i >= 2:
                    sp.wait_ge(prep_q.sem, i - 1)
                sp.dma_start(pin[s], A["w_fq"][i] if i < NFQ else A["w_mx"][i - NFQ]).then_inc(prep_ld[s].sem, 16)
                if i >= 1:
                    store_prepared(sp, i - 1)
            store_prepared(sp, NPREP - 1)
            sp.wait_ge(prep_st[0].sem, 16 * (NPREP // 2))
            sp.wait_ge(prep_st[1].sem, 16 * (NPREP // 2))

            with sp.Fori(0, NB) as b:
                sp.dma_start(r3(xT[:, :], T), A["xT"][b]).then_inc(ld_x.sem, 16)
                sp.dma_start(r3(fT[:, :], T), A["fT"][b]).then_inc(ld_x.sem, 16)
                sp.wait_ge(h_ready.sem, h_ready.at(b, 1))
                sp.dma_start(wo, A["wo"]).then_inc(ld_wo.sem, 16)
                with sp.Fori(0, NC) as c:
                    sp.dma_start(gw, A["w_qkvg"][c]).then_inc(ld_gw.sem, 16)
                    sp.wait_ge(g_proj.sem, b * NC + c + 1)
                    hold(sp)
                sp.wait_ge(h_ready.sem, h_ready.at(b, 2))
                for j in range(MT):
                    if j >= WSLOTS:
                        sp.wait_ge(m_down.sem, m_down.at(b, j - WSLOTS + 1))
                    s = j % WSLOTS
                    if j < MT_FULL:
                        sp.dma_start(mgu[s], A["moe_gu"][j]).then_inc(ld_mw[s].sem, 16)
                        sp.dma_start(mdn[s], A["moe_d"][j]).then_inc(ld_mw[s].sem, 16)
                        sp.dma_start(msel[s], A["moe_sel"][:, j * P:(j + 1) * P]).then_inc(ld_mw[s].sem, 16)
                    else:
                        sp.dma_start(mgu[s][:, :, :, 0:MT_TAIL], A["moe_gu_tail"]).then_inc(ld_mw[s].sem, 16)
                        sp.dma_start(mdn[s][0:MT_TAIL, :], A["moe_d_tail"]).then_inc(ld_mw[s].sem, 16)
                        sp.dma_start(msel[s][:, 0:MT_TAIL], A["moe_sel"][:, j * P:j * P + MT_TAIL])\
                          .then_inc(ld_mw[s].sem, 16)
                sp.wait_ge(h_ready.sem, h_ready.at(b, 3))
                for m in range(4):
                    sp.dma_start(wzx[:, m, :, :], scratch_fq[m]).then_inc(ld_sw.sem, 16)
                for m in range(2):
                    sp.dma_start(wout[:, m, :, :], scratch_fq[4 + m]).then_inc(ld_sw.sem, 16)
                sp.dma_start(wm6, scratch_fq[6][:, :, 0:256]).then_inc(ld_sw.sem, 16)
                sp.wait_ge(h_ready.sem, h_ready.at(b, 4))
                for ib in range(FB):
                    s = ib % 2
                    if ib >= 2:
                        sp.wait_ge(f_down.sem, f_down.at(b, ib - 1))
                    sp.dma_start(fw[s], scratch_mx[ib].rearrange("m p c o -> p m c o")).then_inc(ld_fw[s].sem, 16)
                sp.wait_ge(x_ready.sem, x_ready.at(b, LAYERS))
                sp.dma_start(out[b], r3(xT[:, :], T)).then_inc(stored.sem, 16)
                sp.wait_ge(stored.sem, stored.at(b, 1))
                hold(sp)

        @block.tensor
        def _(pe):
            pe.wait_ge(ld_const.sem, 16 * 10)
            pe.matmul(bank(0)[:, 0:NB], cst("ones"), condT, start=True, stop=True).then_inc(setup_pe.sem, 1)
            for i in range(NPREP):
                s = i % 2
                pe.wait_ge(prep_q.sem, i + 1)
                if i >= 2:
                    pe.wait_ge(prep_c.sem, i - 1)
                for c in range(4):
                    mm = pe.transpose(bank(6 + s)[:, c * P:(c + 1) * P], pq[s][:, c * P:(c + 1) * P], cst("ident"))
                mm.then_inc(prep_t.sem, 1)

            with pe.Fori(0, NB) as b:
                pe.wait_ge(h_ready.sem, h_ready.at(b, 1))
                hold(pe)
                with pe.Fori(0, NC) as c:
                    u = b * NC + c
                    pe.wait_ge(ld_gw.sem, (u + 1) * 16)
                    for m in range(4):
                        for k in range(NC):
                            mm = pe.matmul(bank(m), gw[:, m, k, :], ch(hT, k), start=(k == 0), stop=(k == NC - 1))
                    mm.then_inc(g_proj.sem, 1)
                    pe.wait_ge(g_evac.sem, u + 1)
                    for v in range(GK + 1):
                        if v < GK:
                            if v >= 2:
                                pe.wait_ge(g_kv.sem, u * GK + v - 1)
                            selv = cst("selv")[:, v * P:(v + 1) * P]
                            pe.matmul(bank(5 + v % 2), selv, qkva[:, 2, :], start=True, stop=True)\
                              .then_inc(g_bc.sem, 1)
                        if v >= 1:
                            pe.wait_ge(g_prod.sem, u * GK + v)
                            red = cst("red")[:, (GK - v) * HPC:(2 * GK - v) * HPC]
                            pe.matmul(bank(4), red, Pb[:, (v - 1) % 2, :], start=(v == 1), stop=(v == GK))\
                              .then_inc(g_red.sem, 1)
                pe.wait_ge(y_evac.sem, y_evac.at(b, NC))
                for k in range(NC):
                    mm = pe.matmul(bank(0), cst("avg_d"), ch(yT, k), start=(k == 0), stop=(k == NC - 1))
                mm.then_inc(ln_mean.sem, 1)
                pe.wait_ge(ln_sq.sem, ln_sq.at(b, 1))
                for k in range(NC):
                    mm = pe.matmul(bank(1), cst("avg_d"), ch(ysq, k), start=(k == 0), stop=(k == NC - 1))
                mm.then_inc(ln_var.sem, 1)
                pe.wait_ge(ld_wo.sem, ld_wo.at(b, 1))
                pe.wait_ge(ln_out.sem, ln_out.at(b, 1))
                for oc in range(NC):
                    for k in range(NC):
                        mm = pe.matmul(bank(oc), wo[:, k, oc * P:(oc + 1) * P], ch(yT, k),
                                       start=(k == 0), stop=(k == NC - 1))
                mm.then_inc(o_done.sem, 1)

                pe.wait_ge(h_ready.sem, h_ready.at(b, 2))
                for t in range(NT):
                    for k in range(NC):
                        mm = pe.matmul(bank(4)[:, t * NE:(t + 1) * NE], ch(hT, k)[:, t * P:(t + 1) * P],
                                       gwT[:, k * NE:(k + 1) * NE], start=(k == 0), stop=(k == NC - 1))
                mm.then_inc(m_logit.sem, 1)
                pe.wait_ge(m_comb.sem, m_comb.at(b, 1))
                comb = rk[:, 0:NT * NE]
                for t in range(NT):
                    mm = pe.transpose(bank(5)[0:NE, t * P:(t + 1) * P], comb[:, t * NE:(t + 1) * NE], cst("ident"))
                mm.then_inc(m_combT.sem, 1)
                pe.wait_ge(m_combC.sem, m_combC.at(b, 1))

                def down(j):
                    rows = P if j < MT_FULL else MT_TAIL
                    pe.wait_ge(m_inter.sem, m_inter.at(b, j + 1))
                    for oc in range(NC):
                        mm = pe.matmul(bank(oc), mdn[j % WSLOTS][0:rows, oc * P:(oc + 1) * P],
                                       inter[0:rows, j % 2, :], start=(j == 0), stop=(j == MT - 1))
                    mm.then_inc(m_down.sem, 1)

                for j in range(MT):
                    s = j % WSLOTS
                    rows = P if j < MT_FULL else MT_TAIL
                    per = len(range(s, MT, WSLOTS))
                    pe.wait_ge(ld_mw[s].sem, (b * per + j // WSLOTS + 1) * 48)
                    if j:
                        pe.wait_ge(m_silu.sem, m_silu.at(b, j))
                    for k in range(NC):
                        mm = pe.matmul(bank(4, rows), mgu[s][:, 0, k, 0:rows], ch(hT, k),
                                       start=(k == 0), stop=(k == NC - 1))
                    mm.then_inc(m_gate.sem, 1)
                    if j:
                        pe.wait_ge(m_inter.sem, m_inter.at(b, j))
                    pe.matmul(bank(6, rows), msel[s][:, 0:rows], combT[:, :], start=True, stop=True)
                    for k in range(NC):
                        mm = pe.matmul(bank(5, rows), mgu[s][:, 1, k, 0:rows], ch(hT, k),
                                       start=(k == 0), stop=(k == NC - 1))
                    mm.then_inc(m_up.sem, 1)
                    if j:
                        down(j - 1)
                down(MT - 1)

                pe.wait_ge(h_ready.sem, h_ready.at(b, 3))
                pe.wait_ge(ld_sw.sem, ld_sw.at(b, 7))
                for i, (a, n) in enumerate(((0, 64), (64, 64), (128, 64), (192, 16), (208, 16))):
                    for k in range(NC):
                        mm = pe.matmul(bank(i, n), wm6[:, k, a:a + n], ch(hT, k), start=(k == 0), stop=(k == NC - 1))
                mm.then_inc(s_proj.sem, 1)
                pe.wait_ge(s_sq.sem, s_sq.at(b, 1))
                hold(pe)
                for i in range(2):
                    mm = pe.matmul(bank(5 + i, SN), cst("avg_n", SN), bsq[:, i, :], start=True, stop=True)
                mm.then_inc(s_ms.sem, 1)
                pe.wait_ge(s_dt.sem, s_dt.at(b, 1))
                pe.matmul(bank(7, SN), cst("avg_h", SH), dtt, start=True, stop=True).then_inc(s_dtavg.sem, 1)
                pe.wait_ge(s_bcn.sem, s_bcn.at(b, 1))
                hold(pe)
                for i in range(2):
                    mm = pe.matmul(bank(i, SN), cst("rope", SN), BCn[:, i, :], start=True, stop=True)
                mm.then_inc(s_perm.sem, 1)
                pe.wait_ge(s_rope.sem, s_rope.at(b, 1))
                hold(pe)
                idn = cst("ident")
                for k in range(NT):
                    t = slice(k * P, (k + 1) * P)
                    for a, src in enumerate((gmt, bet, cst_)):
                        pe.transpose(bank(2)[:, (k * 3 + a) * SH:(k * 3 + a + 1) * SH], src[:, t], idn[0:SH, 0:SH])
                    pe.transpose(bank(3)[:, k * SN:(k + 1) * SN], BCn[:, 0, t], idn[0:SN, 0:SN])
                pe.matmul(bank(4)[:, 0:NT * SH], cst("ones", SH), dl, start=True, stop=True).then_inc(s_tm.sem, 1)
                for k in range(NT):
                    t = slice(k * P, (k + 1) * P)
                    if k == 0:
                        pe.wait_ge(s_exps.sem, s_exps.at(b, 1))
                    else:
                        pe.wait_ge(s_y.sem, s_y.at(b, k))
                    for m, dst in ((2, 0), (3, 1), (0, 2), (1, 3)):
                        for kk in range(NC):
                            mm = pe.matmul(bank(dst), ch(hT, kk)[:, t], wzx[:, m, kk, :],
                                           start=(kk == 0), stop=(kk == NC - 1))
                    mm.then_inc(s_x.sem, 1)
                    pe.matmul(bank(4)[:, 0:P], BCn[:, 0, t], BCn[:, 1, t], start=True, stop=True).then_inc(s_cb.sem, 1)
                    pe.wait_ge(s_silu.sem, s_silu.at(b, k + 1))
                    for h in range(2):
                        col = slice(h * 512, (h + 1) * 512)
                        mm = pe.matmul(bank(h), cst("shift"), xh[k % 2][:, col], start=True, stop=(k == 0))
                        if k:
                            mm = pe.matmul(bank(h), cst("edge"), xh[(k - 1) % 2][:, col], start=False, stop=True)
                    mm.then_inc(s_shift.sem, 1)
                    for h in range(2):
                        mm = pe.matmul(bank(2 + h), BCn[:, 1, t], state[:, h * 512:(h + 1) * 512],
                                       start=True, stop=True)
                    mm.then_inc(s_yo.sem, 1)
                    for g in range(5):
                        if g < 4:
                            if k == 0 and g < 2:
                                pass
                            elif g < 2:
                                pe.wait_ge(s_ynT.sem, s_ynT.at(b, k))
                            else:
                                pe.wait_ge(s_diff.sem, s_diff.at(b, k * 4 + g - 1))
                            for hh in range(4):
                                h = g * 4 + hh
                                mm = pe.matmul(bank(5 + g % 2)[:, hh * P:(hh + 1) * P],
                                               cst("selh", SH)[:, h * P:(h + 1) * P], cst_[:, t],
                                               start=True, stop=True)
                            mm.then_inc(s_csb.sem, 1)
                        if g == 1:
                            pe.wait_ge(s_xg.sem, s_xg.at(b, k + 1))
                        if g >= 1:
                            pe.wait_ge(s_m.sem, s_m.at(b, k * 4 + g))
                            for hh in range(4):
                                h = (g - 1) * 4 + hh
                                mm = pe.matmul(bank(h // 8)[:, (h % 8) * SP_:(h % 8 + 1) * SP_],
                                               Md[:, (g - 1) % 2, hh * P:(hh + 1) * P],
                                               Xg[:, h * SP_:(h + 1) * SP_], start=True, stop=True)
                            if g == 4:
                                mm.then_inc(s_yd.sem, 1)
                            else:
                                mm.then_inc(s_mu.sem, 1)
                    for h in range(2):
                        mm = pe.matmul(bank(4 + 3 * h, SN), Btm[:, k, :], Xd[:, h * 512:(h + 1) * 512],
                                       start=True, stop=True)
                    mm.then_inc(s_st.sem, 1)
                    pe.wait_ge(s_yn.sem, s_yn.at(b, k + 1))
                    for i in range(8):
                        mm = pe.transpose(bank(5 + i // 4)[:, (i % 4) * P:(i % 4 + 1) * P],
                                          Yt[:, i * P:(i + 1) * P], idn)
                    mm.then_inc(s_tr.sem, 1)
                pe.wait_ge(s_ynT.sem, s_ynT.at(b, NT))
                for oc in range(NC):
                    for i in range(8):
                        mm = pe.matmul(bank(oc), wout[:, i // 4, i % 4, oc * P:(oc + 1) * P], ch(ynT, i),
                                       start=(i == 0), stop=(i == 7))
                mm.then_inc(s_out.sem, 1)

                pe.wait_ge(h_ready.sem, h_ready.at(b, 4))
                for t in range(NT):
                    if t:
                        pe.wait_ge(f_qx.sem, f_qx.at(b, t))
                    for c in range(NC):
                        mm = pe.transpose(bank(4)[:, c * P:(c + 1) * P], ch(hT, c)[:, t * P:(t + 1) * P], idn)
                    mm.then_inc(f_tx.sem, 1)
                    pe.wait_ge(f_qx.sem, f_qx.at(b, t + 1))
                    if t:
                        pe.wait_ge(f_xT.sem, f_xT.at(b, t))
                    for c in range(NC):
                        mm = pe.transpose(bank(5)[:, c * P:(c + 1) * P], fq[t % 2][:, c * P:(c + 1) * P], idn)
                    mm.then_inc(f_tq.sem, 1)
                pe.wait_ge(f_xT.sem, f_xT.at(b, NT))

                def f_transposes(i):
                    pe.wait_ge(f_q.sem, f_q.at(b, i + 1))
                    if i >= 1:
                        pe.wait_ge(f_hT.sem, f_hT.at(b, i))
                    for c in range(4):
                        mm = pe.transpose(bank(6)[:, c * P:(c + 1) * P], fq[i % 2][:, c * P:(c + 1) * P], idn)
                    mm.then_inc(f_tr.sem, 1)

                def f_downs(ib):
                    pe.wait_ge(f_hT.sem, f_hT.at(b, (ib + 1) * NT))
                    for oc in range(NC):
                        for i in range(4):
                            mm = pe.matmul(bank(oc), fw[ib % 2][:, 2, i, oc * P:(oc + 1) * P], hqT[ib % 2][:, i, :],
                                           start=(ib == 0 and i == 0), stop=(ib == FB - 1 and i == 3))
                    mm.then_inc(f_down.sem, 1)

                for ib in range(FB):
                    pe.wait_ge(ld_fw[ib % 2].sem, ld_fw[ib % 2].at(b, ib // 2 + 1))
                    for t in range(NT):
                        i = ib * NT + t
                        if i:
                            pe.wait_ge(f_silu.sem, f_silu.at(b, i))
                        for k in range(NC):
                            mm = pe.matmul(bank(4), xqT[:, k, t * P:(t + 1) * P], fw[ib % 2][:, 0, k, :],
                                           start=(k == 0), stop=(k == NC - 1))
                        mm.then_inc(f_gate.sem, 1)
                        if i:
                            pe.wait_ge(f_mul.sem, f_mul.at(b, i))
                        for k in range(NC):
                            mm = pe.matmul(bank(5), xqT[:, k, t * P:(t + 1) * P], fw[ib % 2][:, 1, k, :],
                                           start=(k == 0), stop=(k == NC - 1))
                        mm.then_inc(f_gu.sem, 1)
                        if i:
                            f_transposes(i - 1)
                        if t == 1 and ib:
                            f_downs(ib - 1)
                f_transposes(FB * NT - 1)
                f_downs(FB - 1)

        @block.scalar
        def _(act):
            act.wait_ge(setup_pe.sem, 1)
            act.activation(tf, bank(0)[:, 0:NB], ACT.Sigmoid)
            act.wait_ge(ld_const.sem, 160)
            act.activation(dec0.rearrange("p (l c) -> p l c", l=LAYERS), wu4[:, :, 0, :], ACT.Exp)
            act.activation(negA, alog, ACT.Exp)
            act.drain()
            act.activation(dec0, dec0, ACT.Exp, scale=-1.0).then_inc(setup_act.sem, 1)
            for i in range(NPREP):
                s = i % 2
                act.wait_ge(prep_t.sem, i + 1)
                if i >= 2:
                    act.wait_ge(prep_st[s].sem, 16 * (i // 2))
                act.activation(pt_[s], bank(6 + s), ACT.Copy).then_inc(prep_c.sem, 1)

            with act.Fori(0, NB) as b:
                act.wait_ge(fmin_ready.sem, fmin_ready.at(b, 1))
                act.activation(r4(ek2)[:, :, 1, :], r3(um, T), ACT.Exp).then_inc(ek_ready.sem, 1)

                def gate(i):
                    act.wait_ge(um_ready.sem, um_ready.at(b, i + 1))
                    act.activation(r4(eu2)[:, :, 1, :], r3(um, T), ACT.Exp).then_inc(euk_ready.sem, 1)
                    if i == 0:
                        act.wait_ge(ld_x.sem, ld_x.at(b, 2))
                    else:
                        act.wait_ge(x_ready.sem, x_ready.at(b, i))
                    act.activation(hT[:, :], xT[:, :], ACT.Sigmoid).then_inc(sig_ready.sem, 1)

                gate(0)
                with act.Fori(0, NC) as c:
                    u = b * NC + c
                    act.wait_ge(g_proj.sem, u + 1)
                    act.activation(qkva[:, 3, :], bank(3), ACT.Sigmoid)
                    act.activation(qkva[:, 2, :], bank(2), ACT.Copy)
                    act.activation(qkva[:, 1, :], bank(1), ACT.Copy)
                    act.activation(qkva[:, 0, :], bank(0), ACT.Copy, scale=float(GK) ** -0.5).then_inc(g_evac.sem, 1)
                    act.wait_ge(g_red.sem, (u + 1) * GK)
                    act.activation(yT.rearrange("p (c t) -> p c t", c=NC)[:, c, :], bank(4), ACT.Copy)\
                       .then_inc(y_evac.sem, 1)
                act.wait_ge(ln_cent.sem, ln_cent.at(b, 1))
                act.activation(ysq, yT, ACT.Square).then_inc(ln_sq.sem, 1)
                act.wait_ge(ln_var.sem, ln_var.at(b, 1))
                act.activation(sdv, bank(1), ACT.Sqrt, bias=eps_ln).then_inc(ln_sd.sem, 1)
                gate(1)
                act.wait_ge(m_logit.sem, m_logit.at(b, 1))
                act.activation(rk[:, 0:NT * NE], bank(4)[:, 0:NT * NE], ACT.Sigmoid).then_inc(m_score.sem, 1)
                act.wait_ge(m_combT.sem, m_combT.at(b, 1))
                act.activation(combT[0:NE, :], bank(5)[0:NE, :], ACT.Copy).then_inc(m_combC.sem, 1)
                for j in range(MT):
                    rows = P if j < MT_FULL else MT_TAIL
                    act.wait_ge(m_gate.sem, m_gate.at(b, j + 1))
                    if j >= 2:
                        act.wait_ge(m_inter.sem, m_inter.at(b, j - 1))
                    act.activation(sgt[0:rows, j % 2, :], bank(4, rows), ACT.Silu).then_inc(m_silu.sem, 1)
                gate(2)
                act.wait_ge(s_proj.sem, s_proj.at(b, 1))
                for i in range(2):
                    q = act.activation(bsq[:, i, :], bank(i, SN), ACT.Square)
                q.then_inc(s_sq.sem, 1)
                act.activation(th, bank(2, SN), ACT.Copy)
                act.activation(lamt, bank(4, SH), ACT.Sigmoid).then_inc(s_th.sem, 1)
                act.wait_ge(s_ms.sem, s_ms.at(b, 1))
                for i in range(2):
                    q = act.activation(brs[:, i, :], bank(5 + i, SN), ACT.Sqrt, bias=eps_rms[0:SN, :])
                q.then_inc(s_rms.sem, 1)
                act.wait_ge(s_v.sem, s_v.at(b, 1))
                act.activation(nab, nab, ACT.Exp)
                act.drain()
                act.activation(nab, nab, ACT.Ln, bias=one[0:SH, :]).then_inc(s_ln.sem, 1)
                act.wait_ge(s_cs.sem, s_cs.at(b, 1))
                act.activation(eat, eat, ACT.Exp).then_inc(s_ea.sem, 1)
                act.wait_ge(s_ang.sem, s_ang.at(b, 1))
                act.activation(trg[:, :, :], nrd[:, :, :], ACT.Sin).then_inc(s_sin.sem, 1)
                act.wait_ge(s_tmc.sem, s_tmc.at(b, 1))
                act.activation(eL, csl, ACT.Exp)
                act.activation(dend, dend, ACT.Exp)
                act.activation(r3(ecs, SH), tm[:, :, 2, :], ACT.Exp).then_inc(s_exps.sem, 1)
                for k in range(NT):
                    act.wait_ge(s_x.sem, s_x.at(b, k + 1))
                    for h in range(2):
                        act.activation(xh[k % 2][:, h * 512:(h + 1) * 512], bank(h), ACT.Silu)
                    for h in range(2):
                        q = act.activation(zs[:, h * 512:(h + 1) * 512], bank(2 + h), ACT.Silu)
                    q.then_inc(s_silu.sem, 1)
                    for g in range(4):
                        act.wait_ge(s_diff.sem, s_diff.at(b, k * 4 + g + 1))
                        act.activation(Md[:, g % 2, :], Md[:, g % 2, :], ACT.Exp).then_inc(s_exp.sem, 1)
                    act.wait_ge(s_y.sem, s_y.at(b, k + 1))
                    act.activation(Xg, Yt, ACT.Square, accum_out=ss[:, 0:1])
                    act.drain()
                    act.activation(ss[:, 1:2], ss[:, 0:1], ACT.Sqrt, bias=eps_rms, scale=1.0 / DI).then_inc(s_yss.sem, 1)
                    act.wait_ge(s_tr.sem, s_tr.at(b, k + 1))
                    for i in range(2):
                        q = act.activation(ynT.rearrange("p (i t) -> p i t", i=8)[:, 4 * i:4 * i + 4, k * P:(k + 1) * P],
                                           r3(bank(5 + i), P), ACT.Copy)
                    q.then_inc(s_ynT.sem, 1)
                gate(3)
                for t in range(NT):
                    act.wait_ge(f_tq.sem, f_tq.at(b, t + 1))
                    act.activation(xqT[:, :, t * P:(t + 1) * P], r3(bank(5), P), ACT.Copy).then_inc(f_xT.sem, 1)
                for i in range(FB * NT + 1):
                    if i < FB * NT:
                        act.wait_ge(f_gate.sem, f_gate.at(b, i + 1))
                        if i >= 2:
                            act.wait_ge(f_mul.sem, f_mul.at(b, i - 1))
                        act.activation(fs[i % 2], bank(4), ACT.Silu).then_inc(f_silu.sem, 1)
                    if i:
                        ib, t = (i - 1) // NT, (i - 1) % NT
                        act.wait_ge(f_tr.sem, f_tr.at(b, i))
                        if t == 0 and ib >= 2:
                            act.wait_ge(f_down.sem, f_down.at(b, ib - 1))
                        act.activation(hqT[ib % 2][:, :, t * P:(t + 1) * P], r3(bank(6), P), ACT.Copy)\
                           .then_inc(f_hT.sem, 1)

        @block.gpsimd
        def _(pool):
            with pool.Fori(0, NB) as b:
                with pool.Fori(0, NC) as c:
                    u = b * NC + c
                    for v in range(GK):
                        pool.wait_ge(g_scan.sem, u * GK + v + 1)
                        if v >= 2:
                            pool.wait_ge(g_red.sem, u * GK + v - 1)
                        pool.tensor_tensor(Pb[:, v % 2, :], Sb[:, v % 2, :], qkva[:, 0, :], ALU.mult)\
                            .then_inc(g_prod.sem, 1)

        @block.vector
        def _(dve):
            tt, ts, stt = dve.tensor_tensor, dve.tensor_scalar, dve.scalar_tensor_tensor

            def bcast(ap, n):
                return ap.unsqueeze(2).to_broadcast([ap.shape[0], ap.shape[1], n])

            def quantise(dst, src, v, m, amx):
                nbk = 512 // QB
                dve.tensor_reduce(amx[:, 0:nbk], r3(src, QB), AX.X, ALU.max, apply_absolute_value=True)
                dve.drain()
                ts(amx[:, nbk:2 * nbk], amx[:, 0:nbk], 1.0 / 448.0, 1e-30, ALU.mult, ALU.max)
                dve.drain()
                dve.reciprocal(amx[:, 0:nbk], amx[:, nbk:2 * nbk])
                dve.drain()
                tt(r3(v, QB), r3(src, QB), bcast(amx[:, 0:nbk], QB), ALU.mult)
                dve.drain()
                ts(m.bitcast(U32), v.bitcast(U32), 0x7F800000, None, ALU.bitwise_and)
                dve.drain()
                ts(m, m, 2.0 ** -6, 1.5 * 2.0 ** 20, ALU.max, ALU.mult)
                dve.drain()
                tt(v, v, m, ALU.add)
                dve.drain()
                tt(v, v, m, ALU.subtract)
                dve.drain()
                return tt(r3(dst, QB), r3(v, QB), bcast(amx[:, nbk:2 * nbk], QB), ALU.mult)

            dve.wait_ge(setup_act.sem, 1)
            ts(dscale, tf, 0.5, 0.5, ALU.mult, ALU.add)
            ts(oscale, tf, 0.2, 0.8, ALU.mult, ALU.add)
            ts(negA, negA, -1.0, None, ALU.mult)
            dve.drain()
            tt(decay.rearrange("p (b n) -> p b n", b=NB), bcast(dscale, LAYERS * NC),
               dec0.unsqueeze(1).to_broadcast([P, NB, LAYERS * NC]), ALU.mult)

            for i in range(NPREP):
                s = i % 2
                dve.wait_ge(prep_ld[s].sem, 16 * (i // 2 + 1))
                if i >= 2:
                    dve.wait_ge(prep_t.sem, i - 1)
                if i >= NFQ:
                    quantise(pq[s], pin[s], ptmp, ptmp2, pamx).then_inc(prep_q.sem, 1)
                    dve.drain()
                    continue
                g3 = r3(pin[s], P)
                dve.tensor_reduce(pamx[:, 0:4], g3, AX.X, ALU.max, apply_absolute_value=True)
                dve.drain()
                ts(pamx[:, 4:8], pamx[:, 0:4], 1e-10, 1.0 / 7.0, ALU.max, ALU.mult)
                dve.drain()
                dve.reciprocal(pamx[:, 0:4], pamx[:, 4:8])
                dve.drain()
                tt(r3(ptmp, P), g3, bcast(pamx[:, 0:4], P), ALU.mult)
                dve.drain()
                ts(ptmp, ptmp, MAGIC, MAGIC, ALU.add, ALU.subtract)
                dve.drain()
                ts(ptmp, ptmp, -8.0, 7.0, ALU.max, ALU.min)
                dve.drain()
                tt(r3(ptmp, P), r3(ptmp, P), bcast(pamx[:, 4:8], P), ALU.mult)
                dve.drain()
                tt(ptmp, ptmp, pin[s], ALU.subtract)
                dve.drain()
                tt(pq[s], ptmp, pin[s], ALU.add).then_inc(prep_q.sem, 1)
                dve.drain()

            dve.wait_ge(prep_c.sem, NPREP)
            dve.wait_ge(prep_st[0].sem, 16 * (NPREP // 2))
            dve.wait_ge(prep_st[1].sem, 16 * (NPREP // 2))
            with dve.Fori(0, NB) as b:
                dve.wait_ge(ld_x.sem, ld_x.at(b, 2))
                dve.tensor_copy(decay_b, decay.rearrange("p (b n) -> p b n", b=NB)[:, b, :])
                dve.tensor_copy(osc_b, oscale.rearrange("p (b n) -> p b n", b=NB)[:, b, :])
                ts(um, fT[:, :], 30.0, None, ALU.min).then_inc(fmin_ready.sem, 1)
                dve.wait_ge(ek_ready.sem, ek_ready.at(b, 1))
                tt(r4(ek2)[:, :, 0, :], r4(ek2)[:, :, 1, :], r3(fT[:, :], T), ALU.mult)

                def gate(i):
                    for c in range(NC):
                        q = ts(ch(um, c), ch(fT, c), wu4[:, i, 1, c:c + 1], 30.0, ALU.add, ALU.min)
                    q.then_inc(um_ready.sem, 1)
                    dve.wait_ge(euk_ready.sem, euk_ready.at(b, i + 1))
                    tt(r4(eu2)[:, :, 0, :], r4(eu2)[:, :, 1, :], r3(fT[:, :], T), ALU.mult)
                    dve.drain()
                    for c in range(NC):
                        dk = decay_b[:, i * NC + c:i * NC + c + 1].to_broadcast([P, T])
                        for a in range(2):
                            src = r4(ek2)[:, c, a, :]
                            dve.tensor_tensor_scan(nf2[:, a * T:(a + 1) * T], dk, src, 0.0, ALU.mult, ALU.add)
                            dve.tensor_tensor_scan(nb2[:, a * T:(a + 1) * T][:, ::-1], dk, src[:, ::-1], 0.0,
                                                   ALU.mult, ALU.add)
                        dve.drain()
                        tt(nf2, nf2, nb2, ALU.add)
                        dve.drain()
                        tt(nf2, nf2, ek2[:, c * 2 * T:(c + 1) * 2 * T], ALU.subtract)
                        dve.drain()
                        e = eu2[:, c * 2 * T:(c + 1) * 2 * T]
                        tt(e, e, nf2, ALU.add)
                        dve.drain()
                    ts(r4(eu2)[:, :, 1, :], r4(eu2)[:, :, 1, :], 1e-8, None, ALU.max)
                    dve.drain()
                    dve.reciprocal(r4(eu2)[:, :, 1, :], r4(eu2)[:, :, 1, :])
                    dve.drain()
                    stt(out=r3(R[:, :], T), in0=r4(eu2)[:, :, 0, :], scalar=osc_b, in1=r4(eu2)[:, :, 1, :],
                        op0=ALU.mult, op1=ALU.mult)
                    dve.drain()
                    dve.wait_ge(sig_ready.sem, sig_ready.at(b, i + 1))
                    tt(hT[:, :], hT[:, :], R[:, :], ALU.mult).then_inc(h_ready.sem, 1)

                def residual(i):
                    for oc in range(NC):
                        q = tt(ch(xT, oc), ch(xT, oc), bank(oc), ALU.add)
                    q.then_inc(x_ready.sem, 1)
                    dve.drain()

                gate(0)
                with dve.Fori(0, NC) as c:
                    u = b * NC + c
                    dve.wait_ge(g_evac.sem, u + 1)
                    for v in range(GK):
                        s = v % 2
                        dve.wait_ge(g_bc.sem, u * GK + v + 1)
                        tt(kvb[:, s, :], bank(5 + s), qkva[:, 1, :], ALU.mult).then_inc(g_kv.sem, 1)
                        dve.drain()
                        if v >= 2:
                            dve.wait_ge(g_prod.sem, u * GK + v - 1)
                        dve.tensor_tensor_scan(Sb[:, s, :], qkva[:, 3, :], kvb[:, s, :], 0.0, ALU.mult, ALU.add)\
                           .then_inc(g_scan.sem, 1)
                dve.wait_ge(ln_mean.sem, ln_mean.at(b, 1))
                mean = bank(0).unsqueeze(1).to_broadcast([P, NC, T])
                tt(r3(yT, T), r3(yT, T), mean, ALU.subtract).then_inc(ln_cent.sem, 1)
                dve.wait_ge(ln_sd.sem, ln_sd.at(b, 1))
                dve.reciprocal(sdv, sdv)
                dve.drain()
                tt(r3(yT, T), r3(yT, T), sdv.unsqueeze(1).to_broadcast([P, NC, T]), ALU.mult)
                dve.drain()
                for c in range(NC):
                    q = ts(ch(yT, c), ch(yT, c), gb[:, c:c + 1], gb[:, NC + c:NC + c + 1], ALU.mult, ALU.add)
                q.then_inc(ln_out.sem, 1)
                dve.wait_ge(o_done.sem, o_done.at(b, 1))
                residual(0)

                gate(1)
                dve.memset(combT[:, :], 1.0)
                sc = rk[:, 0:64]
                sfc, pr, grp, gcm, grk = rk[:, 64:128], rk[:, 128:224], rk[:, 224:240], rk[:, 240:304], rk[:, 304:320]
                gcm2, rnk, wsum = rk[:, 320:384], rk[:, 384:448], rk[:, 448:456]
                cmp, cmp2 = rk[:, 1024:2048], rk[:, 2048:3072]
                dve.wait_ge(m_score.sem, m_score.at(b, 1))
                tt(r3(sfc, NE), r3(sc, NE), gate_bias.unsqueeze(1).to_broadcast([P, NT, NE]), ALU.add)
                dve.drain()
                s4, p6 = r3(sfc, 4), r3(pr, 6)
                tt(p6[:, :, 0:3], s4[:, :, 0:3], s4[:, :, 1:4], ALU.add)
                tt(p6[:, :, 3:5], s4[:, :, 0:2], s4[:, :, 2:4], ALU.add)
                tt(p6[:, :, 5:6], s4[:, :, 0:1], s4[:, :, 3:4], ALU.add)
                dve.drain()
                dve.tensor_reduce(grp, p6, AX.X, ALU.max)
                dve.drain()

                def ranks(val, n, c1, c2, low, rank):
                    v3 = r3(val, n)
                    others = v3.unsqueeze(2).to_broadcast([P, NT, n, n])
                    own = v3.unsqueeze(3).to_broadcast([P, NT, n, n])
                    f4 = [x.rearrange("p (t i j) -> p t i j", t=NT, i=n) for x in (c1, c2)]
                    lw = low.rearrange("p (i j) -> p i j", i=n).unsqueeze(1).to_broadcast([P, NT, n, n])
                    tt(f4[0], others, own, ALU.is_gt)
                    tt(f4[1], others, own, ALU.is_ge)
                    dve.drain()
                    tt(f4[1], f4[1], lw, ALU.mult)
                    dve.drain()
                    tt(c1, c1, c2, ALU.max)
                    dve.drain()
                    dve.tensor_reduce(rank, r3(c1, n), AX.X, ALU.add)
                    dve.drain()

                ranks(grp, 4, gcm, gcm2, cst("low4"), grk)
                ts(grk, grk, 1.5, None, ALU.is_lt)
                dve.drain()
                tt(r3(sfc, 4), r3(sfc, 4), bcast(grk, 4), ALU.mult)
                dve.drain()
                ranks(sfc, NE, cmp, cmp2, cst("low16"), rnk)
                ts(rnk, rnk, 5.5, None, ALU.is_lt)
                dve.drain()
                tt(sc, sc, rnk, ALU.mult)
                dve.drain()
                dve.tensor_reduce(wsum[:, 0:4], r3(sc, NE), AX.X, ALU.add)
                dve.drain()
                ts(wsum[:, 0:4], wsum[:, 0:4], 1e-20, None, ALU.add)
                dve.drain()
                dve.reciprocal(wsum[:, 4:8], wsum[:, 0:4])
                dve.drain()
                stt(out=r3(sc, NE), in0=r3(sc, NE), scalar=2.5, in1=bcast(wsum[:, 4:8], NE),
                    op0=ALU.mult, op1=ALU.mult).then_inc(m_comb.sem, 1)
                for j in range(MT):
                    rows = P if j < MT_FULL else MT_TAIL
                    dve.wait_ge(m_up.sem, m_up.at(b, j + 1))
                    dve.wait_ge(m_silu.sem, m_silu.at(b, j + 1))
                    tt(tcb[0:rows, :], sgt[0:rows, j % 2, :], bank(6, rows), ALU.mult)
                    dve.drain()
                    if j >= 2:
                        dve.wait_ge(m_down.sem, m_down.at(b, j - 1))
                    tt(inter[0:rows, j % 2, :], tcb[0:rows, :], bank(5, rows), ALU.mult).then_inc(m_inter.sem, 1)
                    dve.drain()
                dve.wait_ge(m_down.sem, m_down.at(b, MT))
                residual(1)

                gate(2)
                dve.wait_ge(s_proj.sem, s_proj.at(b, 1))
                ts(vt, bank(3, SH), dtb, None, ALU.add)
                dve.drain()
                stt(out=nab, in0=vt, scalar=-1.0, in1=vt, op0=ALU.mult, op1=ALU.min).then_inc(s_v.sem, 1)
                dve.wait_ge(s_ln.sem, s_ln.at(b, 1))
                stt(out=dtt, in0=vt, scalar=0.0, in1=nab, op0=ALU.max, op1=ALU.add)
                dve.drain()
                ts(eat, dtt, negA, None, ALU.mult).then_inc(s_dt.sem, 1)
                dve.wait_ge(s_th.sem, s_th.at(b, 1))
                tt(gmt, lamt, dtt, ALU.mult)
                dve.drain()
                for k in range(NT):
                    t = slice(k * P, (k + 1) * P)
                    dve.tensor_tensor_scan(cst_[:, t], one[0:SH, :].to_broadcast([SH, P]), eat[:, t], 0.0,
                                           ALU.mult, ALU.add)
                ts(lamt, lamt, -1.0, 1.0, ALU.mult, ALU.add)
                dve.drain()
                tt(lamt, lamt, dtt, ALU.mult)
                for k in range(NT):
                    ts(dl[:, k * SH:(k + 1) * SH], cst("ident")[0:SH, 0:SH], cst_[:, (k + 1) * P - 1:(k + 1) * P],
                       None, ALU.mult)
                dve.drain().then_inc(s_cs.sem, 1)
                dve.wait_ge(s_ea.sem, s_ea.at(b, 1))
                tt(bet, lamt, eat, ALU.mult)
                dve.wait_ge(s_dtavg.sem, s_dtavg.at(b, 1))
                tt(th, th, bank(7, SN), ALU.mult)
                dve.drain()
                dve.tensor_tensor_scan(ang, one[0:SN, :].to_broadcast([SN, T]), th, 0.0, ALU.mult, ALU.add)
                dve.drain()
                inv = 1.0 / (2.0 * np.pi)
                ts(nrd[:, 0, :], ang, inv, None, ALU.mult)
                ts(nrd[:, 1, :], ang, inv, 0.25, ALU.mult, ALU.add)
                dve.drain()
                ts(nrd[:, :, :], nrd[:, :, :], MAGIC, MAGIC, ALU.add, ALU.subtract)
                dve.drain()
                ang2 = ang.unsqueeze(1).to_broadcast([SN, 2, T])
                stt(out=trg[:, :, :], in0=nrd[:, :, :], scalar=-TWO_PI[0], in1=ang2, op0=ALU.mult, op1=ALU.add)
                dve.drain()
                for cpart in TWO_PI[1:]:
                    stt(out=trg[:, :, :], in0=nrd[:, :, :], scalar=-cpart, in1=trg[:, :, :], op0=ALU.mult, op1=ALU.add)
                    dve.drain()
                ts(trg[:, 1, :], trg[:, 1, :], float(np.pi / 2), None, ALU.add)
                dve.drain()
                ts(nrd[:, :, :], trg[:, :, :], 3.1415925, -3.1415925, ALU.min, ALU.max).then_inc(s_ang.sem, 1)
                dve.wait_ge(s_rms.sem, s_rms.at(b, 1))
                dve.reciprocal(brs[:, :, :], brs[:, :, :])
                dve.drain()
                for i in range(2):
                    tt(BCn[:, i, :], bank(i, SN), brs[:, i, :], ALU.mult)
                dve.drain()
                for i in range(2):
                    q = ts(BCn[:, i, :], BCn[:, i, :], bcb[:, i:i + 1], None, ALU.add)
                q.then_inc(s_bcn.sem, 1)
                dve.wait_ge(s_perm.sem, s_perm.at(b, 1))
                dve.wait_ge(s_sin.sem, s_sin.at(b, 1))
                for i in range(2):
                    tt(bsq[:, i, :], bank(i, SN), trg[:, 0, :], ALU.mult)
                    tt(BCn[:, i, :], BCn[:, i, :], trg[:, 1, :], ALU.mult)
                dve.drain()
                tt(BCn[:, :, :], BCn[:, :, :], bsq[:, :, :], ALU.add).then_inc(s_rope.sem, 1)
                dve.wait_ge(s_tm.sem, s_tm.at(b, 1))
                dve.tensor_copy(tm[:, :, :, :], bank(2)[:, 0:NT * 3 * SH].rearrange("p (k a h) -> p k a h", k=NT, a=3))
                dve.tensor_copy(Btm[:, :, :], bank(3)[:, 0:NT * SN].rearrange("p (k n) -> p k n", k=NT))
                dve.tensor_copy(csl, bank(4)[:, 0:NT * SH])
                dve.memset(state[:, :], 0.0)
                dve.drain()
                tt(r3(dend, SH), r3(csl, SH), tm[:, :, 2, :], ALU.subtract).then_inc(s_tmc.sem, 1)

                for k in range(NT):
                    hs = slice(k * SH, (k + 1) * SH)
                    dve.wait_ge(s_cb.sem, s_cb.at(b, k + 1))
                    tt(Gm, bank(4)[:, 0:P], cst("tri"), ALU.mult)
                    dve.drain()
                    dve.wait_ge(s_silu.sem, s_silu.at(b, k + 1))
                    dve.wait_ge(s_exps.sem, s_exps.at(b, 1))
                    if k:
                        dve.wait_ge(s_yss.sem, s_yss.at(b, k))
                    tt(r3(Xg, SP_), r3(xh[k % 2], SP_), bcast(tm[:, k, 0, :], SP_), ALU.mult)
                    dve.wait_ge(s_shift.sem, s_shift.at(b, k + 1))
                    for h in range(2):
                        tt(r3(Xd[:, h * 512:(h + 1) * 512], SP_), r3(bank(h), SP_),
                           bcast(tm[:, k, 1, h * 8:(h + 1) * 8], SP_), ALU.mult)
                    dve.drain()
                    tt(Xg, Xg, Xd, ALU.add)
                    dve.drain()
                    tt(r3(Xd, SP_), r3(Xg, SP_), bcast(dend[:, hs], SP_), ALU.mult).then_inc(s_xg.sem, 1)
                    for g in range(5):
                        if g < 4:
                            dve.wait_ge(s_csb.sem, s_csb.at(b, k * 4 + g + 1))
                            if g >= 2:
                                dve.wait_ge(s_mu.sem, s_mu.at(b, k * 3 + g - 1))
                            tt(r3(Md[:, g % 2, :], P), r3(bank(5 + g % 2), P),
                               bcast(tm[:, k, 2, g * 4:(g + 1) * 4], P), ALU.subtract).then_inc(s_diff.sem, 1)
                        if g >= 1:
                            dve.wait_ge(s_exp.sem, s_exp.at(b, k * 4 + g))
                            m3 = r3(Md[:, (g - 1) % 2, :], P)
                            stt(out=m3, in0=m3, scalar=10000.0, in1=Gm.unsqueeze(1).to_broadcast([P, 4, P]),
                                op0=ALU.min, op1=ALU.mult).then_inc(s_m.sem, 1)
                            dve.drain()
                    dve.wait_ge(s_yo.sem, s_yo.at(b, k + 1))
                    if k:
                        dve.wait_ge(s_tr.sem, s_tr.at(b, k))
                    for h in range(2):
                        tt(r3(Yt[:, h * 512:(h + 1) * 512], SP_), r3(bank(2 + h), SP_),
                           bcast(ecs[:, k * SH + h * 8:k * SH + h * 8 + 8], SP_), ALU.mult)
                    dve.drain()
                    dve.wait_ge(s_yd.sem, s_yd.at(b, k + 1))
                    for h in range(2):
                        y = Yt[:, h * 512:(h + 1) * 512]
                        tt(y, y, bank(h), ALU.add)
                    dve.wait_ge(s_st.sem, s_st.at(b, k + 1))
                    tt(r3(Xd, SP_), r3(xh[k % 2], SP_), bcast(Dbc, SP_), ALU.mult)
                    tt(r3(state, SP_), r3(state, SP_), bcast(eL[0:SN, hs], SP_), ALU.mult)
                    dve.drain()
                    for h in range(2):
                        st = state[:, h * 512:(h + 1) * 512]
                        tt(st, st, bank(4 + 3 * h, SN), ALU.add)
                    tt(Yt, Yt, Xd, ALU.add)
                    dve.drain()
                    tt(Yt, Yt, zs, ALU.mult).then_inc(s_y.sem, 1)
                    dve.wait_ge(s_yss.sem, s_yss.at(b, k + 1))
                    dve.reciprocal(ss[:, 2:3], ss[:, 1:2])
                    dve.drain()
                    ts(Yt, Yt, ss[:, 2:3], None, ALU.mult).then_inc(s_yn.sem, 1)
                dve.wait_ge(s_out.sem, s_out.at(b, 1))
                residual(2)

                gate(3)
                for t in range(NT):
                    dve.wait_ge(f_tx.sem, f_tx.at(b, t + 1))
                    if t >= 2:
                        dve.wait_ge(f_tq.sem, f_tq.at(b, t - 1))
                    quantise(fq[t % 2], bank(4), fv, fm, famx).then_inc(f_qx.sem, 1)
                    dve.drain()
                for i in range(FB * NT):
                    dve.wait_ge(f_silu.sem, f_silu.at(b, i + 1))
                    dve.wait_ge(f_gu.sem, f_gu.at(b, i + 1))
                    tt(fh, fs[i % 2], bank(5), ALU.mult).then_inc(f_mul.sem, 1)
                    dve.drain()
                    if i >= 2:
                        dve.wait_ge(f_tr.sem, f_tr.at(b, i - 1))
                    else:
                        dve.wait_ge(f_tq.sem, f_tq.at(b, NT - 1 + i))
                    quantise(fq[i % 2], fh, fv, fm, famx).then_inc(f_q.sem, 1)
                    dve.drain()
                dve.wait_ge(f_down.sem, f_down.at(b, FB))
                residual(3)


def host_arrays(i):
    ct = np.ascontiguousarray

    def channel_major(x):
        return ct(x.transpose(0, 2, 1).reshape(NB, NC, P, T).transpose(0, 2, 1, 3))

    def per_channel(v):
        return v.reshape(NC, P).T

    def k_major(wt):
        o, k = wt.shape
        return wt.T.reshape(k // P, P, o).transpose(1, 0, 2)

    r = {}
    r["consts"] = constant_table()[1]
    r["moe_sel"] = expert_rows()
    r["xT"] = channel_major(i["x"])
    r["fT"] = channel_major(i["fside_BxSxS_0"])
    r["condT"] = ct(i["cond_512"].T)
    r["wu"] = ct(np.concatenate([per_channel(i[f"{n}_{a}"]) for n in ("L0_cond", "L0_cond2", "L1_cond", "L1_cond2")
                                 for a in "wu"], 1))
    def by_value(v):
        return v.reshape(NC, HPC, GK, *v.shape[1:]).swapaxes(1, 2).reshape(v.shape)

    r["gb"] = ct(np.concatenate([per_channel(by_value(i["L0_attn_gamma"])),
                                 per_channel(by_value(i["L0_attn_beta"]))], 1))
    r["gwT"] = ct(k_major(i["L0_ffn_gate_weight"]).reshape(P, NC * NE))
    r["gate_bias"] = i["L0_ffn_e_score_correction_bias"]
    r["bc_bias"] = ct(np.concatenate([i["L1_attn_B_bias"].T, i["L1_attn_C_bias"].T], 1))
    r["A_log"], r["dt_bias"], r["D_param"] = i["L1_attn_A_log"], i["L1_attn_dt_bias"], i["L1_attn_D_param"]
    qkvg = np.stack([k_major(i[f"L0_attn_W{m}"]) for m in "qkvg"], 1)
    r["w_qkvg"] = ct(qkvg.reshape(P, 4, NC, NC, P).transpose(3, 0, 1, 2, 4))
    r["wo"] = ct(k_major(by_value(i["L0_attn_Wo"].T).T))
    gate = np.concatenate([i["L0_ffn_gate_proj"].reshape(NE * EI, D), i["L0_ffn_shared_gate_w"]])
    up = np.concatenate([i["L0_ffn_up_proj"].reshape(NE * EI, D), i["L0_ffn_shared_up_w"]])
    down = np.concatenate([i["L0_ffn_down_proj"].transpose(0, 2, 1).reshape(NE * EI, D), i["L0_ffn_shared_down_w"].T])
    gu = np.stack([k_major(gate), k_major(up)], 1)
    full = MT_FULL * P
    r["moe_gu"] = ct(gu[..., :full].reshape(P, 2, NC, MT_FULL, P).transpose(3, 0, 1, 2, 4))
    r["moe_gu_tail"] = ct(gu[..., full:])
    r["moe_d"] = ct(down[:full].reshape(MT_FULL, P, D))
    r["moe_d_tail"] = ct(down[full:])
    win, th, lam, wout = (i[f"L1_attn_{n}"] for n in ("W_in", "W_theta", "W_lambda", "W_out"))
    dtw = win[2 * DI + 2 * SN:]
    r["w_fq"] = ct(np.concatenate([win[:2 * DI], wout.reshape(D, 2, 512).transpose(1, 0, 2).reshape(2 * D, 512),
                                   win[2 * DI:2 * DI + 2 * SN], th, th, dtw, lam, dtw, lam]).reshape(-1, P, 512))
    g, u, d = i["L1_ffn_gate_w"], i["L1_ffn_up_w"], i["L1_ffn_down_w"]
    mx = np.stack([g.reshape(FB, 512, D), u.reshape(FB, 512, D), d.reshape(D, FB, 512).transpose(1, 0, 2)], 1)
    r["w_mx"] = ct(mx.reshape(-1, P, 512))
    return r


def kernel(**inputs):
    import concourse.bacc as _bacc
    from concourse.bass_utils import run_bass_kernel_spmd as _run

    nc = _bacc.Bacc("TRN2", target_bir_lowering=False, num_devices=1)
    arrays = host_arrays({k: np.asarray(v) for k, v in inputs.items()})
    A = {k: nc.dram_tensor(k, list(v.shape), F32, kind="ExternalInput").ap() for k, v in arrays.items()}
    out = nc.dram_tensor("out", [NB, P, NC, T], F32, kind="ExternalOutput").ap()
    fq = nc.dram_tensor("scratch_fq", [7, P, 4, 512], F32, kind="Internal").ap()
    mx = nc.dram_tensor("scratch_mx", [FB, 3, P, 4, 512], F32, kind="Internal").ap()
    build(nc, A, out, fq, mx)
    got = _run(nc, [arrays], core_ids=[0]).results[0]["out"]
    return np.ascontiguousarray(got.transpose(0, 2, 1, 3).reshape(NB, D, T).transpose(0, 2, 1))
```

```python
from contextlib import ExitStack

import concourse.bass as bass
from concourse import mybir
import numpy as np

F32 = mybir.dt.float32
F32R = mybir.dt.float32r
U32 = mybir.dt.uint32
ALU = mybir.AluOpType
ACT = mybir.ActivationFunctionType
AX = mybir.AxisListType

P = 128
NB, T, D = 4, 512, 512
NC = D // P
NT = T // P
LAYERS = 4
GH, GK = 16, 32
HPC = P // GK
NE, EI, NSH = 16, 352, 2
ST = -(-NSH * EI // P)
MT = ST + NE * EI // P
GUW, DW = 2 * NC * P, D
WSLOTS = 4
SH, SP_, SN = 16, 64, 64
DI = SH * SP_
FI = 2048
FB = FI // 512
QB = 32

MAGIC = 12582912.0
TWO_PI = (6.28125, float(np.float32(2 * np.pi - 6.28125)),
          2 * np.pi - 6.28125 - float(np.float32(2 * np.pi - 6.28125)))


class Event:

    def __init__(self, sem, per, unit=1, before=0):
        self.sem, self.per, self.unit, self.before = sem, per, unit, before

    def at(self, b, k):
        return (b * self.per + k + self.before) * self.unit


def constant_table():
    parts = {}
    eye = np.eye(P)
    parts["ident"] = eye
    parts["ones"] = np.ones((P, P))
    parts["avg_d"] = np.full((P, P), 1.0 / D)
    parts["shift"] = np.eye(P, k=1)
    edge = np.zeros((P, P))
    edge[P - 1, 0] = 1.0
    parts["edge"] = edge
    red = np.zeros((P, 15, HPC))
    for h in range(HPC):
        red[h * GK:(h + 1) * GK, 7, h] = 1.0
    parts["red"] = red.reshape(P, -1)
    rope = np.zeros((P, SN))
    for m in range(SN // 2):
        rope[m + SN // 2, m] = -1.0
        rope[m, m + SN // 2] = 1.0
    parts["rope"] = rope
    parts["avg_n"] = np.full((P, SN), 1.0 / SN)
    parts["avg_h"] = np.full((P, SN), 1.0 / SH)
    selh = np.zeros((P, SH, P))
    for h in range(SH):
        selh[h, h, :] = 1.0
    parts["selh"] = selh.reshape(P, -1)
    parts["tri"] = np.triu(np.ones((P, P)))
    parts["low16"] = np.tile(np.tril(np.ones((NE, NE)), -1).reshape(1, -1), (P, 1))
    parts["low4"] = np.tile(np.tril(np.ones((4, 4)), -1).reshape(1, -1), (P, 1))
    parts["eps"] = np.tile(np.array([[1e-5, 1.1920929e-07, 1.0, 0.0]]), (P, 1))
    at, n = {}, 0
    for k, v in parts.items():
        at[k] = (n, v.shape[1])
        n += v.shape[1]
    return at, np.concatenate(list(parts.values()), 1).astype(np.float32)


def value_selectors():
    selv = np.zeros((P, GK, HPC, GK), np.float32)
    for h in range(HPC):
        for v in range(GK):
            selv[h * GK + v, v, h, :] = 1.0
    return selv.reshape(P, -1)


def expert_rows():
    sel = np.zeros((NE, NE * EI), np.float32)
    for e in range(NE):
        sel[e, e * EI:(e + 1) * EI] = 1.0
    return sel


def build(nc, A, out, scratch_fq, scratch_mx):
    cat, ctab = constant_table()
    ctx = ExitStack()
    with ctx:
        def sb(name, cols, parts=P):
            return ctx.enter_context(nc.sbuf_tensor("sb_" + name, [parts, cols], F32))

        def ev(name, per, unit=1, before=0):
            return Event(ctx.enter_context(nc.semaphore(name)), per, unit, before)

        banks = [ctx.enter_context(nc.psum_tensor(f"bank{i}", [P, 512], F32)) for i in range(8)]

        def bank(i, rows=P):
            return banks[i][0:rows, :]

        passed = ctx.enter_context(nc.semaphore("passed"))

        def hold(eng):
            eng.sem_inc(passed, 1)

        const = sb("const", ctab.shape[1])

        def cst(name, rows=P):
            a, n = cat[name]
            return const[0:rows, a:a + n]

        eps_ln, eps_rms, one = (const[:, cat["eps"][0] + i:cat["eps"][0] + i + 1] for i in range(3))
        xT = sb("xT", NC * T)
        hT = sb("hT", NC * T)
        R = [sb(f"ratio{i}", NC * T) for i in range(LAYERS)]
        small = sb("small", 1024)
        pos = [0]

        def carve(n, parts=P):
            pos[0] += n
            return small[0:parts, pos[0] - n:pos[0]]

        wu = carve(LAYERS * 2 * NC)
        wu4 = wu.rearrange("p (l a c) -> p l a c", l=LAYERS, a=2)
        condT = carve(NB)
        tf = carve(NB)
        dscale = carve(NB)
        oscale = carve(NB + 1)
        dec0 = carve(LAYERS * NC)
        decay = carve((NB + 1) * LAYERS * NC)
        decay_b = carve(2 * LAYERS * NC)
        osc_b = carve(2)
        comb = carve(NT * NE)
        gb = carve(2 * NC)
        gate_bias = carve(NE)
        gwT = carve(NC * NE)
        bcb = carve(2, SN)
        alog = carve(1, SH)
        negA = carve(1, SH)
        dtb = carve(1, SH)
        Dbc = carve(SH)
        csl = carve(NT * SH)
        eL = carve(NT * SH)
        ecs = carve(NT * SH)
        dend = carve(NT * SH)
        ss = carve(4)

        WCOLS = 17408
        work = sb("work", WCOLS)

        def w(a, n, parts=P):
            assert a + n <= WCOLS, (a, n)
            return work[0:parts, a:a + n]

        RCOLS = 12288
        parts = ctx.enter_context(nc.sbuf_tensor("sb_parts", [P, RCOLS], F32R))
        selv_r = ctx.enter_context(nc.sbuf_tensor("sb_selv_r", [P, GK * P], F32R))
        big = parts[:, :].bitcast(F32)

        ld_const = ev("ld_const", 0, 16)
        ld_selv = ev("ld_selv", 0, 16)
        ld_x = ev("ld_x", 1, 16, 1)
        x_copied = ev("x_copied", 1)
        stored = ev("stored", 1, 16, 1)
        setup_pe = ev("setup_pe", 0)
        setup_act = ev("setup_act", 0)
        setup_dve = ev("setup_dve", 0)
        ld_f = [ev(f"ld_f{i}", 4, 16, 2) for i in range(2)]
        r_min = ev("r_min", 8, 1, 4)
        r_exp = ev("r_exp", 8, 1, 4)
        r_min2 = ev("r_min2", 8, 1, 4)
        r_exp2 = ev("r_exp2", 8, 1, 4)
        r_done = ev("r_done", 8, 1, 4)
        sig_ready = ev("sig_ready", LAYERS * NC)
        h_ready = ev("h_ready", LAYERS)
        x_ready = ev("x_ready", LAYERS * NC)
        prep_ld = [ev(f"prep_ld{i}", 0, 16) for i in range(2)]
        prep_v = ev("prep_v", 0)
        prep_q = ev("prep_q", 0)
        prep_t = ev("prep_t", 0)
        prep_c = ev("prep_c", 0)
        prep_st = [ev(f"prep_st{i}", 0, 16) for i in range(2)]
        ld_gw = ev("ld_gw", NC, 16)
        g_proj = ev("g_proj", NC)
        g_evac = ev("g_evac", NC)
        g_vlo = ev("g_vlo", NC)
        NS = NC * GK
        g_bc = ev("g_bc", NS)
        g_kv = ev("g_kv", NS)
        g_scan = ev("g_scan", NS)
        g_prod = ev("g_prod", NS, 1, 1)
        NG = GK // 4
        g_red = ev("g_red", NC * NG)
        y_evac = ev("y_evac", NC, 1, 1)
        ld_wo = ev("ld_wo", 1, 16)
        ln_mean = ev("ln_mean", 1)
        ln_cent = ev("ln_cent", 1)
        ln_sq = ev("ln_sq", 1)
        ln_var = ev("ln_var", 1)
        ln_sd = ev("ln_sd", 1)
        ln_out = ev("ln_out", 1)
        o_done = ev("o_done", 1)
        m_logit = ev("m_logit", 1)
        m_score = ev("m_score", 1)
        m_comb = ev("m_comb", 1)
        m_combT = ev("m_combT", 1)
        m_combC = ev("m_combC", 1)
        ld_mw = [ev(f"ld_mw{s}", len(range(s, MT, WSLOTS)), 16) for s in range(WSLOTS)]
        ld_ms = [ev(f"ld_ms{s}", len(range(s, MT - ST, WSLOTS)), 16) for s in range(WSLOTS)]
        m_hhi = ev("m_hhi", 1)
        m_hlo = ev("m_hlo", 1)
        m_guhi = ev("m_guhi", MT)
        m_gulo = ev("m_gulo", MT)
        m_dhi = ev("m_dhi", MT)
        m_dlo = ev("m_dlo", MT)
        m_gate = ev("m_gate", MT)
        m_up = ev("m_up", MT)
        m_silu = ev("m_silu", MT)
        m_prod = ev("m_prod", MT)
        m_ihi = ev("m_ihi", MT)
        m_inter = ev("m_inter", MT)
        m_down = ev("m_down", MT)
        ld_sw = ev("ld_sw", 7, 16)
        s_proj = ev("s_proj", 1)
        s_sq = ev("s_sq", 1)
        s_ms = ev("s_ms", 1)
        s_rms = ev("s_rms", 1)
        s_th = ev("s_th", 1)
        s_v = ev("s_v", 1)
        s_ln = ev("s_ln", 1)
        s_dt = ev("s_dt", 1)
        s_dtavg = ev("s_dtavg", 1)
        s_ea = ev("s_ea", 1)
        s_bcn = ev("s_bcn", 1)
        s_perm = ev("s_perm", 1)
        s_ang = ev("s_ang", 1)
        s_sin = ev("s_sin", 1)
        s_rope = ev("s_rope", 1)
        s_tm = ev("s_tm", 1)
        s_tmc = ev("s_tmc", 1)
        s_exps = ev("s_exps", 1)
        s_x = ev("s_x", NT)
        s_silu = ev("s_silu", NT)
        s_shift = ev("s_shift", NT)
        s_xg = ev("s_xg", NT)
        s_cb = ev("s_cb", NT)
        s_gm = ev("s_gm", NT)
        s_csb = ev("s_csb", NT * 4)
        s_diff = ev("s_diff", NT * 4)
        s_exp = ev("s_exp", NT * 4)
        s_m = ev("s_m", NT * 4)
        s_mu = ev("s_mu", NT * 3)
        s_cs = ev("s_cs", 1)
        s_yd = ev("s_yd", NT)
        s_yo = ev("s_yo", NT)
        s_st = ev("s_st", NT)
        s_y = ev("s_y", NT)
        s_yss = ev("s_yss", NT)
        s_yn = ev("s_yn", NT)
        s_tr = ev("s_tr", NT)
        s_ynT = ev("s_ynT", NT)
        s_out = ev("s_out", 1)
        ld_fw = [ev(f"ld_fw{s}", 2, 16) for s in range(2)]
        f_tx = ev("f_tx", NT)
        f_qx = ev("f_qx", NT)
        f_tq = ev("f_tq", NT)
        f_xT = ev("f_xT", NT)
        f_gate = ev("f_gate", NT * FB)
        f_mul = ev("f_mul", NT * FB)
        f_gu = ev("f_gu", NT * FB)
        f_silu = ev("f_silu", NT * FB)
        f_q = ev("f_q", NT * FB)
        f_tr = ev("f_tr", NT * FB)
        f_hT = ev("f_hT", NT * FB)
        f_down = ev("f_down", FB)

        gw = w(0, 4 * NC * P).rearrange("p (m c o) -> p m c o", m=4, c=NC)
        qg, kg, ag = w(2048, T), w(2560, T), w(3072, T)
        NSB, NPB = 3, 6
        Sb = [w(3584 + s * T, T) for s in range(NSB)]
        Pb = [w(5120 + s * T, T) for s in range(NPB)]
        yT = w(8192, NC * T)
        ysq = w(10240, NC * T)
        sdv = w(12288, T)
        wo = w(12800, NC * D).rearrange("p (c o) -> p c o", c=NC)
        vhi, vlo = parts[:, 0:T], parts[:, T:2 * T]
        xnext = w(14848, NC * T)
        mraw = [w(s * (GUW + DW), GUW + DW) for s in range(WSLOTS)]
        msel = [w(6144 + s * P, P, NE) for s in range(WSLOTS)]
        combT = w(6656, T, NE)
        sgt = [w(7168 + s * T, T) for s in range(2)]
        inter = w(8192, T)
        rk = w(8704, 3 * 1024)

        def split_slots(at, n):
            return [[parts[:, at + (2 * s + i) * n:at + (2 * s + i + 1) * n] for i in range(2)] for s in range(2)]

        guw = split_slots(0, GUW)
        dnw = split_slots(4096, DW)
        isp = split_slots(6144, T)
        hsp = [parts[:, 8192 + i * NC * T:8192 + (i + 1) * NC * T] for i in range(2)]
        ekp, eup, nf2, nb2 = (w(8704 + i * 1024, 1024) for i in range(4))
        fmin_e, fmin_u = w(12800, T), w(13312, T)
        fch = [w(13824 + s * T, T) for s in range(2)]

        def ch(ap, c):
            return ap[:, c * T:(c + 1) * T]

        block = ctx.enter_context(nc.Block())

        pin = [w(s * 512, 512) for s in range(2)]
        pq = [w(1024 + s * 512, 512) for s in range(2)]
        pt_ = [w(2048 + s * 512, 512) for s in range(2)]
        pv = [w(3072 + s * 512, 512) for s in range(2)]
        pm = [w(4096 + s * 512, 512) for s in range(2)]
        pamx = [w(5120 + s * 64, 64) for s in range(2)]
        NFQ, NMX = 26, 48
        NPREP = NFQ + NMX

        wzx = big[:, 0:8192].rearrange("p (m c o) -> p m c o", m=4, c=NC)
        wout = big[:, 8192:12288].rearrange("p (m c o) -> p m c o", m=2, c=4)
        wm6 = w(0, 1024).rearrange("p (c o) -> p c o", c=NC)
        ynT = w(0, 8 * T)
        o = 4096
        xh = [w(o + s * 1024, 1024) for s in range(2)]
        zs = w(o + 2048, 1024)
        Xg = w(o + 3072, 1024)
        Xd = w(o + 4096, 1024)
        Yt = w(o + 5120, 1024)
        Md = w(o + 6144, 1024).rearrange("p (s n) -> p s n", s=2)
        state = w(o + 7168, 1024, SN)
        Gm = w(o + 8192, P)
        tm = w(o + 8192 + P, NT * 3 * SH).rearrange("p (k a h) -> p k a h", k=NT, a=3)
        Btm = w(o + 8192 + P + 192, NT * SN).rearrange("p (k n) -> p k n", k=NT)
        small2 = sb("small2", 2 * T + 3 * T)
        BCn = small2[0:SN, 0:2 * T].rearrange("p (a t) -> p a t", a=2)
        dtt = small2[0:SH, 2 * T:3 * T]
        cst_ = small2[0:SH, 3 * T:4 * T]
        gmt = small2[0:SH, 4 * T:5 * T]
        bsq = w(o, 2 * T, SN).rearrange("p (a t) -> p a t", a=2)
        brs = w(o + 1024, 2 * T, SN).rearrange("p (a t) -> p a t", a=2)
        th = w(o + 2048, T, SN)
        ang = w(o + 2560, T, SN)
        trg = w(o + 3072, 2 * T, SN).rearrange("p (a t) -> p a t", a=2)
        nrd = w(o + 4096, 2 * T, SN).rearrange("p (a t) -> p a t", a=2)
        vt = w(o + 5120, T, SH)
        nab = w(o + 5632, T, SH)
        lamt = w(o + 6144, T, SH)
        eat = w(o + 6656, T, SH)
        bet = w(o + 7168, T, SH)
        dl = w(o + 7680, NT * SH, SH)

        fw = [big[:, s * 6144:(s + 1) * 6144].rearrange("p (m c o) -> p m c o", m=3, c=4) for s in range(2)]
        xqT = w(0, NC * T).rearrange("p (c t) -> p c t", c=NC)
        fs = [w(2048 + s * 512, 512) for s in range(2)]
        fh = w(3072, 512)
        fv = w(3584, 512)
        fm = w(4096, 512)
        fq = [w(4608 + s * 512, 512) for s in range(2)]
        hqT = [w(5632 + s * 2048, 2048).rearrange("p (i t) -> p i t", i=4) for s in range(2)]
        famx = w(9728, 64)

        def r3(ap, n):
            return ap.rearrange("p (a n) -> p a n", n=n)

        def store_prepared(sp, i):
            s = i % 2
            sp.wait_ge(prep_c.sem, i + 1)
            src = r3(pt_[s], P)
            if i < NFQ:
                dst = scratch_fq[i // 4][:, :, (i % 4) * P:(i % 4 + 1) * P]
            else:
                k = i - NFQ
                dst = scratch_mx[k // 12][(k // 4) % 3][:, :, (k % 4) * P:(k % 4 + 1) * P]
            sp.dma_start(dst, src).then_inc(prep_st[s].sem, 16)

        def load_f(sp, n, f_row):
            sp.dma_start(fch[n % 2], f_row[n % NC]).then_inc(ld_f[n % 2].sem, 16)

        f_next = A["fT"][1:NB + 1]
        x_next = A["xT"][1:NB + 1]

        @block.sync
        def _(sp):
            sp.sem_inc(stored.sem, 16)
            for dst, src in ((const[:, :], A["consts"]), (condT, A["condT"]),
                             (wu, A["wu"]), (gb, A["gb"]), (gwT, A["gwT"]),
                             (gate_bias, A["gate_bias"].rearrange("(a n) -> a n", a=1).to_broadcast([P, NE])),
                             (bcb, A["bc_bias"]), (alog, A["A_log"].rearrange("(a n) -> a n", n=1)),
                             (dtb, A["dt_bias"].rearrange("(a n) -> a n", n=1)),
                             (Dbc, A["D_param"].rearrange("(a n) -> a n", a=1).to_broadcast([P, SH]))):
                sp.dma_start(dst, src).then_inc(ld_const.sem, 16)
            sp.dma_start(w(8192, GK * P), A["selv"]).then_inc(ld_selv.sem, 16)
            sp.wait_ge(setup_act.sem, 2)
            sp.dma_start(r3(xnext, T), A["xT"][0]).then_inc(ld_x.sem, 16)
            load_f(sp, 4, A["fT"][0])
            load_f(sp, 5, A["fT"][0])
            for n in (6, 7):
                sp.wait_ge(r_done.sem, r_done.at(0, n - 1 - 8))
                load_f(sp, n, A["fT"][0])
            for i in range(NPREP):
                s = i % 2
                if i >= 2:
                    sp.wait_ge(prep_q.sem, i - 1)
                sp.dma_start(pin[s], A["w_fq"][i] if i < NFQ else A["w_mx"][i - NFQ]).then_inc(prep_ld[s].sem, 16)
                if i >= 1:
                    store_prepared(sp, i - 1)
            store_prepared(sp, NPREP - 1)
            sp.wait_ge(prep_st[0].sem, 16 * (NPREP // 2))
            sp.wait_ge(prep_st[1].sem, 16 * (NPREP // 2))

            sp.dma_start(gw, A["w_qkvg"][0]).then_inc(ld_gw.sem, 16)

            with sp.Fori(0, NB) as b:
                sp.wait_ge(h_ready.sem, h_ready.at(b, 1))
                sp.dma_start(wo, A["wo"]).then_inc(ld_wo.sem, 16)
                with sp.Fori(0, NC - 1) as c:
                    sp.wait_ge(g_proj.sem, b * NC + c + 1)
                    sp.dma_start(gw, A["w_qkvg"][1:NC][c]).then_inc(ld_gw.sem, 16)
                sp.wait_ge(y_evac.sem, y_evac.at(b, NC))
                for j in range(MT):
                    s, i = j % WSLOTS, j - ST
                    if j >= WSLOTS:
                        sp.wait_ge(m_down.sem, m_down.at(b, j - WSLOTS + 1))
                    sp.dma_start(mraw[s], A["moe_w"][j]).then_inc(ld_mw[s].sem, 16)
                    if i >= 0:
                        sp.dma_start(msel[i % WSLOTS], A["moe_sel"][:, i * P:(i + 1) * P])\
                          .then_inc(ld_ms[i % WSLOTS].sem, 16)
                    if j == WSLOTS - 1:
                        sp.wait_ge(o_done.sem, o_done.at(b, 1))
                        for n in range(2):
                            load_f(sp, n, A["fT"][b])
                    n = (j - 2) // 6 + 1
                    if j % 6 == 2 and 2 <= n < 8:
                        sp.wait_ge(r_done.sem, r_done.at(b, n - 1))
                        load_f(sp, n, A["fT"][b] if n < NC else f_next[b])
                sp.wait_ge(m_down.sem, m_down.at(b, MT))
                sp.dma_start(wm6, scratch_fq[6][:, :, 0:256]).then_inc(ld_sw.sem, 16)
                for m in range(4):
                    sp.dma_start(wzx[:, m, :, :], scratch_fq[m]).then_inc(ld_sw.sem, 16)
                for m in range(2):
                    sp.dma_start(wout[:, m, :, :], scratch_fq[4 + m]).then_inc(ld_sw.sem, 16)
                for ib in range(FB):
                    s = ib % 2
                    if ib == 0:
                        sp.wait_ge(s_x.sem, s_x.at(b, NT))
                    elif ib == 1:
                        sp.wait_ge(s_out.sem, s_out.at(b, 1))
                    else:
                        sp.wait_ge(f_down.sem, f_down.at(b, ib - 1))
                    sp.dma_start(fw[s], scratch_mx[ib].rearrange("m p c o -> p m c o")).then_inc(ld_fw[s].sem, 16)
                sp.dma_start(r3(xnext, T), x_next[b]).then_inc(ld_x.sem, 16)
                sp.wait_ge(f_gu.sem, f_gu.at(b, NT * FB))
                sp.dma_start(gw, A["w_qkvg"][0]).then_inc(ld_gw.sem, 16)
                sp.wait_ge(x_ready.sem, x_ready.at(b, LAYERS * NC))
                sp.dma_start(out[b], r3(xT[:, :], T)).then_inc(stored.sem, 16)
            sp.wait_ge(stored.sem, 16 * (NB + 1))
            sp.wait_ge(ld_x.sem, 16 * (NB + 1))
            sp.wait_ge(ld_gw.sem, 16 * (NB * NC + 1))

        @block.tensor
        def _(pe):
            pe.wait_ge(ld_const.sem, 16 * 10)
            pe.matmul(bank(0)[:, 0:NB], cst("ones"), condT, start=True, stop=True).then_inc(setup_pe.sem, 1)
            for i in range(NPREP):
                s = i % 2
                pe.wait_ge(prep_q.sem, i + 1)
                if i >= 2:
                    pe.wait_ge(prep_c.sem, i - 1)
                for c in range(4):
                    mm = pe.transpose(bank(6 + s)[:, c * P:(c + 1) * P], pq[s][:, c * P:(c + 1) * P], cst("ident"))
                mm.then_inc(prep_t.sem, 1)

            with pe.Fori(0, NB) as b:
                def project(m, k):
                    return pe.matmul(bank(m), gw[:, m, k, :], ch(hT, k), start=(k == 0), stop=(k == NC - 1))

                def chunk(u, ahead):
                    pe.wait_ge(g_evac.sem, u + 1)
                    pe.wait_ge(g_vlo.sem, u + 1)
                    hold(pe)
                    if ahead:
                        pe.wait_ge(ld_gw.sem, (u + 2) * 16)
                        hold(pe)
                    for v in range(GK):
                        if v >= 3:
                            pe.wait_ge(g_kv.sem, u * GK + v - 2)
                        selv = selv_r[:, v * P:(v + 1) * P]
                        pe.matmul(bank(5 + v % 3), selv, vhi, start=True, stop=False)
                        pe.matmul(bank(5 + v % 3), selv, vlo, start=False, stop=True).then_inc(g_bc.sem, 1)
                        if ahead and v % 2 == 0:
                            mm = project(v // 2 // NC, v // 2 % NC)
                            if v == GK - 2:
                                mm.then_inc(g_proj.sem, 1)
                        if v >= 6 and v % 4 == 2:
                            reduce_group(u, v // 4 - 1)
                    reduce_group(u, NG - 1)

                def reduce_group(u, g):
                    pe.wait_ge(g_prod.sem, u * GK + 4 * g + 5)
                    if g == 0:
                        pe.wait_ge(y_evac.sem, u + 1)
                        hold(pe)
                    red = cst("red")[:, (7 - g) * HPC:(15 - g) * HPC]
                    for j in range(4):
                        mm = pe.matmul(bank(4)[32 * j:32 * j + 32, :], red, Pb[(4 * g + j) % NPB],
                                       start=(g == 0), stop=(g == NG - 1))
                    mm.then_inc(g_red.sem, 1)

                pe.wait_ge(h_ready.sem, h_ready.at(b, 1))
                hold(pe)
                pe.wait_ge(ld_gw.sem, ld_gw.at(b, 1))
                for m in range(4):
                    for k in range(NC):
                        mm = project(m, k)
                mm.then_inc(g_proj.sem, 1)
                with pe.Fori(0, NC - 1) as c:
                    chunk(b * NC + c, True)
                chunk(b * NC + NC - 1, False)
                pe.wait_ge(y_evac.sem, y_evac.at(b, NC))
                for k in range(NC):
                    mm = pe.matmul(bank(0), cst("avg_d"), ch(yT, k), start=(k == 0), stop=(k == NC - 1))
                mm.then_inc(ln_mean.sem, 1)
                pe.wait_ge(ln_sq.sem, ln_sq.at(b, 1))
                for k in range(NC):
                    mm = pe.matmul(bank(1), cst("avg_d"), ch(ysq, k), start=(k == 0), stop=(k == NC - 1))
                mm.then_inc(ln_var.sem, 1)
                pe.wait_ge(ld_wo.sem, ld_wo.at(b, 1))
                pe.wait_ge(ln_out.sem, ln_out.at(b, 1))
                for oc in range(NC):
                    for k in range(NC):
                        mm = pe.matmul(bank(oc), wo[:, k, oc * P:(oc + 1) * P], ch(yT, k),
                                       start=(k == 0), stop=(k == NC - 1))
                mm.then_inc(o_done.sem, 1)

                pe.wait_ge(h_ready.sem, h_ready.at(b, 2))
                for t in range(NT):
                    for k in range(NC):
                        mm = pe.matmul(bank(7)[:, t * NE:(t + 1) * NE], ch(hT, k)[:, t * P:(t + 1) * P],
                                       gwT[:, k * NE:(k + 1) * NE], start=(k == 0), stop=(k == NC - 1))
                mm.then_inc(m_logit.sem, 1)
                pe.wait_ge(m_hlo.sem, m_hlo.at(b, 1))

                def three(dst, lhs, rhs, first, last):
                    pe.matmul(dst, lhs[0], rhs[0], start=first, stop=False)
                    pe.matmul(dst, lhs[0], rhs[1], start=False, stop=False)
                    return pe.matmul(dst, lhs[1], rhs[0], start=False, stop=last)

                def project_in(j, which, dst):
                    for k in range(NC):
                        a = (which * NC + k) * P
                        mm = three(dst, [x[:, a:a + P] for x in guw[j % 2]], [ch(x, k) for x in hsp],
                                   k == 0, k == NC - 1)
                    return mm

                def down(j):
                    pe.wait_ge(m_dlo.sem, m_dlo.at(b, j + 1))
                    pe.wait_ge(m_inter.sem, m_inter.at(b, j + 1))
                    for oc in range(NC):
                        mm = three(bank(oc), [x[:, oc * P:(oc + 1) * P] for x in dnw[j % 2]], isp[j % 2],
                                   j == 0, j == MT - 1)
                    mm.then_inc(m_down.sem, 1)

                for j in range(MT):
                    i = j - ST
                    pe.wait_ge(m_gulo.sem, m_gulo.at(b, j + 1))
                    if j:
                        pe.wait_ge(m_silu.sem, m_silu.at(b, j))
                    project_in(j, 0, bank(4)).then_inc(m_gate.sem, 1)
                    if j:
                        pe.wait_ge(m_prod.sem, m_prod.at(b, j))
                    if i >= 0:
                        s = i % WSLOTS
                        pe.wait_ge(ld_ms[s].sem, ld_ms[s].at(b, i // WSLOTS + 1))
                        pe.matmul(bank(6), msel[s][:, :], combT[:, :], start=True, stop=True)
                    project_in(j, 1, bank(5)).then_inc(m_up.sem, 1)
                    if j:
                        down(j - 1)
                    if j == ST - 2:
                        pe.wait_ge(m_comb.sem, m_comb.at(b, 1))
                        for t in range(NT):
                            mm = pe.transpose(bank(7)[0:NE, t * P:(t + 1) * P], comb[:, t * NE:(t + 1) * NE],
                                              cst("ident"))
                        mm.then_inc(m_combT.sem, 1)
                    if j == ST - 1:
                        pe.wait_ge(m_combC.sem, m_combC.at(b, 1))
                down(MT - 1)

                pe.wait_ge(h_ready.sem, h_ready.at(b, 3))
                pe.wait_ge(ld_sw.sem, ld_sw.at(b, 7))
                for i, (a, n) in enumerate(((0, 64), (64, 64), (128, 64), (192, 16), (208, 16))):
                    for k in range(NC):
                        mm = pe.matmul(bank(i, n), wm6[:, k, a:a + n], ch(hT, k), start=(k == 0), stop=(k == NC - 1))
                mm.then_inc(s_proj.sem, 1)
                pe.wait_ge(s_sq.sem, s_sq.at(b, 1))
                hold(pe)
                for i in range(2):
                    mm = pe.matmul(bank(5 + i, SN), cst("avg_n", SN), bsq[:, i, :], start=True, stop=True)
                mm.then_inc(s_ms.sem, 1)
                pe.wait_ge(s_dt.sem, s_dt.at(b, 1))
                pe.matmul(bank(7, SN), cst("avg_h", SH), dtt, start=True, stop=True).then_inc(s_dtavg.sem, 1)
                pe.wait_ge(s_bcn.sem, s_bcn.at(b, 1))
                hold(pe)
                for i in range(2):
                    mm = pe.matmul(bank(i, SN), cst("rope", SN), BCn[:, i, :], start=True, stop=True)
                mm.then_inc(s_perm.sem, 1)
                pe.wait_ge(s_rope.sem, s_rope.at(b, 1))
                hold(pe)
                idn = cst("ident")
                for k in range(NT):
                    t = slice(k * P, (k + 1) * P)
                    for a, src in enumerate((gmt, bet, cst_)):
                        pe.transpose(bank(2)[:, (k * 3 + a) * SH:(k * 3 + a + 1) * SH], src[:, t], idn[0:SH, 0:SH])
                    pe.transpose(bank(3)[:, k * SN:(k + 1) * SN], BCn[:, 0, t], idn[0:SN, 0:SN])
                pe.matmul(bank(4)[:, 0:NT * SH], cst("ones", SH), dl, start=True, stop=True).then_inc(s_tm.sem, 1)
                for k in range(NT):
                    t = slice(k * P, (k + 1) * P)
                    if k == 0:
                        pe.wait_ge(s_exps.sem, s_exps.at(b, 1))
                    else:
                        pe.wait_ge(s_y.sem, s_y.at(b, k))
                    for m, dst in ((2, 0), (3, 1), (0, 2), (1, 3)):
                        for kk in range(NC):
                            mm = pe.matmul(bank(dst), ch(hT, kk)[:, t], wzx[:, m, kk, :],
                                           start=(kk == 0), stop=(kk == NC - 1))
                    mm.then_inc(s_x.sem, 1)
                    pe.matmul(bank(4)[:, 0:P], BCn[:, 0, t], BCn[:, 1, t], start=True, stop=True).then_inc(s_cb.sem, 1)
                    pe.wait_ge(s_silu.sem, s_silu.at(b, k + 1))
                    for h in range(2):
                        col = slice(h * 512, (h + 1) * 512)
                        mm = pe.matmul(bank(h), cst("shift"), xh[k % 2][:, col], start=True, stop=(k == 0))
                        if k:
                            mm = pe.matmul(bank(h), cst("edge"), xh[(k - 1) % 2][:, col], start=False, stop=True)
                    mm.then_inc(s_shift.sem, 1)
                    for h in range(2):
                        mm = pe.matmul(bank(2 + h), BCn[:, 1, t], state[:, h * 512:(h + 1) * 512],
                                       start=True, stop=True)
                    mm.then_inc(s_yo.sem, 1)
                    for g in range(5):
                        if g < 4:
                            if k == 0 and g < 2:
                                pass
                            elif g < 2:
                                pe.wait_ge(s_ynT.sem, s_ynT.at(b, k))
                            else:
                                pe.wait_ge(s_diff.sem, s_diff.at(b, k * 4 + g - 1))
                            for hh in range(4):
                                h = g * 4 + hh
                                mm = pe.matmul(bank(5 + g % 2)[:, hh * P:(hh + 1) * P],
                                               cst("selh", SH)[:, h * P:(h + 1) * P], cst_[:, t],
                                               start=True, stop=True)
                            mm.then_inc(s_csb.sem, 1)
                        if g == 1:
                            pe.wait_ge(s_xg.sem, s_xg.at(b, k + 1))
                        if g >= 1:
                            pe.wait_ge(s_m.sem, s_m.at(b, k * 4 + g))
                            for hh in range(4):
                                h = (g - 1) * 4 + hh
                                mm = pe.matmul(bank(h // 8)[:, (h % 8) * SP_:(h % 8 + 1) * SP_],
                                               Md[:, (g - 1) % 2, hh * P:(hh + 1) * P],
                                               Xg[:, h * SP_:(h + 1) * SP_], start=True, stop=True)
                            if g == 4:
                                mm.then_inc(s_yd.sem, 1)
                            else:
                                mm.then_inc(s_mu.sem, 1)
                    for h in range(2):
                        mm = pe.matmul(bank(4 + 3 * h, SN), Btm[:, k, :], Xd[:, h * 512:(h + 1) * 512],
                                       start=True, stop=True)
                    mm.then_inc(s_st.sem, 1)
                    pe.wait_ge(s_yn.sem, s_yn.at(b, k + 1))
                    for i in range(8):
                        mm = pe.transpose(bank(5 + i // 4)[:, (i % 4) * P:(i % 4 + 1) * P],
                                          Yt[:, i * P:(i + 1) * P], idn)
                    mm.then_inc(s_tr.sem, 1)
                pe.wait_ge(s_ynT.sem, s_ynT.at(b, NT))
                for oc in range(NC):
                    for i in range(8):
                        mm = pe.matmul(bank(oc), wout[:, i // 4, i % 4, oc * P:(oc + 1) * P], ch(ynT, i),
                                       start=(i == 0), stop=(i == 7))
                mm.then_inc(s_out.sem, 1)

                pe.wait_ge(h_ready.sem, h_ready.at(b, 4))
                for t in range(NT):
                    if t:
                        pe.wait_ge(f_qx.sem, f_qx.at(b, t))
                    for c in range(NC):
                        mm = pe.transpose(bank(4)[:, c * P:(c + 1) * P], ch(hT, c)[:, t * P:(t + 1) * P], idn)
                    mm.then_inc(f_tx.sem, 1)
                    pe.wait_ge(f_qx.sem, f_qx.at(b, t + 1))
                    if t:
                        pe.wait_ge(f_xT.sem, f_xT.at(b, t))
                    for c in range(NC):
                        mm = pe.transpose(bank(5)[:, c * P:(c + 1) * P], fq[t % 2][:, c * P:(c + 1) * P], idn)
                    mm.then_inc(f_tq.sem, 1)
                pe.wait_ge(f_xT.sem, f_xT.at(b, NT))

                def f_transposes(i):
                    pe.wait_ge(f_q.sem, f_q.at(b, i + 1))
                    if i >= 1:
                        pe.wait_ge(f_hT.sem, f_hT.at(b, i))
                    for c in range(4):
                        mm = pe.transpose(bank(6)[:, c * P:(c + 1) * P], fq[i % 2][:, c * P:(c + 1) * P], idn)
                    mm.then_inc(f_tr.sem, 1)

                def f_downs(ib):
                    pe.wait_ge(f_hT.sem, f_hT.at(b, (ib + 1) * NT))
                    for oc in range(NC):
                        for i in range(4):
                            mm = pe.matmul(bank(oc), fw[ib % 2][:, 2, i, oc * P:(oc + 1) * P], hqT[ib % 2][:, i, :],
                                           start=(ib == 0 and i == 0), stop=(ib == FB - 1 and i == 3))
                    mm.then_inc(f_down.sem, 1)

                for ib in range(FB):
                    pe.wait_ge(ld_fw[ib % 2].sem, ld_fw[ib % 2].at(b, ib // 2 + 1))
                    for t in range(NT):
                        i = ib * NT + t
                        if i:
                            pe.wait_ge(f_silu.sem, f_silu.at(b, i))
                        for k in range(NC):
                            mm = pe.matmul(bank(4), xqT[:, k, t * P:(t + 1) * P], fw[ib % 2][:, 0, k, :],
                                           start=(k == 0), stop=(k == NC - 1))
                        mm.then_inc(f_gate.sem, 1)
                        if i:
                            pe.wait_ge(f_mul.sem, f_mul.at(b, i))
                        for k in range(NC):
                            mm = pe.matmul(bank(5), xqT[:, k, t * P:(t + 1) * P], fw[ib % 2][:, 1, k, :],
                                           start=(k == 0), stop=(k == NC - 1))
                        mm.then_inc(f_gu.sem, 1)
                        if i:
                            f_transposes(i - 1)
                        if t == 1 and ib:
                            f_downs(ib - 1)
                f_transposes(FB * NT - 1)
                f_downs(FB - 1)

        def ratio_exps(act, b, n, second):
            if second:
                act.wait_ge(r_min2.sem, r_min2.at(b, n + 1))
                act.activation(eup[:, T:2 * T], fmin_u, ACT.Exp).then_inc(r_exp2.sem, 1)
            else:
                act.wait_ge(r_min.sem, r_min.at(b, n + 1))
                act.activation(ekp[:, T:2 * T], fmin_e, ACT.Exp)
                act.activation(eup[:, T:2 * T], fmin_u, ACT.Exp).then_inc(r_exp.sem, 1)

        @block.scalar
        def _(act):
            act.sem_inc(y_evac.sem, 1)
            act.wait_ge(setup_pe.sem, 1)
            act.activation(tf, bank(0)[:, 0:NB], ACT.Sigmoid)
            act.wait_ge(ld_const.sem, 16 * 10)
            act.activation(dec0.rearrange("p (l c) -> p l c", l=LAYERS), wu4[:, :, 0, :], ACT.Exp)
            act.activation(negA, alog, ACT.Exp)
            act.drain()
            act.activation(dec0, dec0, ACT.Exp, scale=-1.0).then_inc(setup_act.sem, 1)
            act.wait_ge(ld_selv.sem, 16)
            act.activation(selv_r[:, :], w(8192, GK * P), ACT.Copy).then_inc(setup_act.sem, 1)
            for n in range(4, 8):
                ratio_exps(act, 0, n - 8, 0)
                ratio_exps(act, 0, n - 8, 1)
            for i in range(NPREP):
                s = i % 2
                act.wait_ge(prep_t.sem, i + 1)
                if i >= 2:
                    act.wait_ge(prep_st[s].sem, 16 * (i // 2))
                act.activation(pt_[s], bank(6 + s), ACT.Copy).then_inc(prep_c.sem, 1)

            with act.Fori(0, NB) as b:
                def sigmoids(i, src):
                    for c in range(NC):
                        if i:
                            act.wait_ge(x_ready.sem, x_ready.at(b, (i - 1) * NC + c + 1))
                        act.activation(ch(hT, c), ch(src, c), ACT.Sigmoid).then_inc(sig_ready.sem, 1)

                act.wait_ge(ld_x.sem, ld_x.at(b, 0))
                sigmoids(0, xnext)
                act.wait_ge(stored.sem, stored.at(b, 0))
                act.activation(xT[:, :], xnext, ACT.Copy).then_inc(x_copied.sem, 1)
                with act.Fori(0, NC) as c:
                    u = b * NC + c
                    act.wait_ge(g_proj.sem, u + 1)
                    act.wait_ge(g_prod.sem, u * GK + 1)
                    act.activation(vhi, bank(2), ACT.Copy)
                    act.activation(ag, bank(3), ACT.Sigmoid)
                    act.activation(kg, bank(1), ACT.Copy)
                    act.activation(qg, bank(0), ACT.Copy, scale=float(GK) ** -0.5).then_inc(g_evac.sem, 1)
                    act.wait_ge(g_red.sem, (u + 1) * NG)
                    act.activation(yT.rearrange("p (c t) -> p c t", c=NC)[:, c, :], bank(4), ACT.Copy)\
                       .then_inc(y_evac.sem, 1)
                act.wait_ge(ln_cent.sem, ln_cent.at(b, 1))
                act.activation(ysq, yT, ACT.Square).then_inc(ln_sq.sem, 1)
                act.wait_ge(ln_var.sem, ln_var.at(b, 1))
                act.activation(sdv, bank(1), ACT.Sqrt, bias=eps_ln).then_inc(ln_sd.sem, 1)
                sigmoids(1, xT)
                def gu_hi(j):
                    act.wait_ge(ld_mw[j % WSLOTS].sem, ld_mw[j % WSLOTS].at(b, j // WSLOTS + 1))
                    if j >= 2:
                        act.wait_ge(m_up.sem, m_up.at(b, j - 1))
                    act.activation(guw[j % 2][0], mraw[j % WSLOTS][:, 0:GUW], ACT.Copy).then_inc(m_guhi.sem, 1)

                gu_hi(0)
                act.wait_ge(h_ready.sem, h_ready.at(b, 2))
                act.activation(hsp[0], hT[:, :], ACT.Copy).then_inc(m_hhi.sem, 1)
                act.wait_ge(m_logit.sem, m_logit.at(b, 1))
                act.activation(comb, bank(7)[:, 0:NT * NE], ACT.Sigmoid).then_inc(m_score.sem, 1)
                for j in range(MT):
                    act.wait_ge(m_gate.sem, m_gate.at(b, j + 1))
                    if j >= 2:
                        act.wait_ge(m_prod.sem, m_prod.at(b, j - 1))
                    act.activation(sgt[j % 2], bank(4), ACT.Silu).then_inc(m_silu.sem, 1)
                    if j + 1 < MT:
                        gu_hi(j + 1)
                    if j >= 2:
                        act.wait_ge(m_down.sem, m_down.at(b, j - 1))
                    act.activation(dnw[j % 2][0], mraw[j % WSLOTS][:, GUW:GUW + DW], ACT.Copy).then_inc(m_dhi.sem, 1)
                    if j == ST - 1:
                        act.wait_ge(m_combT.sem, m_combT.at(b, 1))
                        act.activation(combT, bank(7, NE), ACT.Copy).then_inc(m_combC.sem, 1)
                    act.wait_ge(m_prod.sem, m_prod.at(b, j + 1))
                    act.activation(isp[j % 2][0], inter, ACT.Copy).then_inc(m_ihi.sem, 1)
                    n, step = (j - 2) // 6, (j - 2) % 6
                    if step == 5 and n < 7:
                        ratio_exps(act, b, n + 1, 0)
                    if step == 2:
                        ratio_exps(act, b, n, 1)
                sigmoids(2, xT)
                act.wait_ge(s_proj.sem, s_proj.at(b, 1))
                for i in range(2):
                    q = act.activation(bsq[:, i, :], bank(i, SN), ACT.Square)
                q.then_inc(s_sq.sem, 1)
                act.activation(th, bank(2, SN), ACT.Copy)
                act.activation(lamt, bank(4, SH), ACT.Sigmoid).then_inc(s_th.sem, 1)
                act.wait_ge(s_ms.sem, s_ms.at(b, 1))
                for i in range(2):
                    q = act.activation(brs[:, i, :], bank(5 + i, SN), ACT.Sqrt, bias=eps_rms[0:SN, :])
                q.then_inc(s_rms.sem, 1)
                act.wait_ge(s_v.sem, s_v.at(b, 1))
                act.activation(nab, nab, ACT.Exp)
                act.drain()
                act.activation(nab, nab, ACT.Ln, bias=one[0:SH, :]).then_inc(s_ln.sem, 1)
                act.wait_ge(s_cs.sem, s_cs.at(b, 1))
                act.activation(eat, eat, ACT.Exp).then_inc(s_ea.sem, 1)
                act.wait_ge(s_ang.sem, s_ang.at(b, 1))
                act.activation(trg[:, :, :], nrd[:, :, :], ACT.Sin).then_inc(s_sin.sem, 1)
                act.wait_ge(s_tmc.sem, s_tmc.at(b, 1))
                act.activation(eL, csl, ACT.Exp)
                act.activation(dend, dend, ACT.Exp)
                act.activation(r3(ecs, SH), tm[:, :, 2, :], ACT.Exp).then_inc(s_exps.sem, 1)
                for k in range(NT):
                    act.wait_ge(s_x.sem, s_x.at(b, k + 1))
                    for h in range(2):
                        act.activation(xh[k % 2][:, h * 512:(h + 1) * 512], bank(h), ACT.Silu)
                    for h in range(2):
                        q = act.activation(zs[:, h * 512:(h + 1) * 512], bank(2 + h), ACT.Silu)
                    q.then_inc(s_silu.sem, 1)
                    for g in range(4):
                        act.wait_ge(s_diff.sem, s_diff.at(b, k * 4 + g + 1))
                        act.activation(Md[:, g % 2, :], Md[:, g % 2, :], ACT.Exp).then_inc(s_exp.sem, 1)
                    act.wait_ge(s_y.sem, s_y.at(b, k + 1))
                    act.activation(Xg, Yt, ACT.Square, accum_out=ss[:, 0:1])
                    act.drain()
                    act.activation(ss[:, 1:2], ss[:, 0:1], ACT.Sqrt, bias=eps_rms, scale=1.0 / DI).then_inc(s_yss.sem, 1)
                    act.wait_ge(s_tr.sem, s_tr.at(b, k + 1))
                    for i in range(2):
                        q = act.activation(ynT.rearrange("p (i t) -> p i t", i=8)[:, 4 * i:4 * i + 4, k * P:(k + 1) * P],
                                           r3(bank(5 + i), P), ACT.Copy)
                    q.then_inc(s_ynT.sem, 1)
                sigmoids(3, xT)
                for t in range(NT):
                    act.wait_ge(f_tq.sem, f_tq.at(b, t + 1))
                    act.activation(xqT[:, :, t * P:(t + 1) * P], r3(bank(5), P), ACT.Copy).then_inc(f_xT.sem, 1)
                for i in range(FB * NT + 1):
                    if i < FB * NT:
                        act.wait_ge(f_gate.sem, f_gate.at(b, i + 1))
                        if i >= 2:
                            act.wait_ge(f_mul.sem, f_mul.at(b, i - 1))
                        act.activation(fs[i % 2], bank(4), ACT.Silu).then_inc(f_silu.sem, 1)
                    if i:
                        ib, t = (i - 1) // NT, (i - 1) % NT
                        act.wait_ge(f_tr.sem, f_tr.at(b, i))
                        if t == 0 and ib >= 2:
                            act.wait_ge(f_down.sem, f_down.at(b, ib - 1))
                        act.activation(hqT[ib % 2][:, :, t * P:(t + 1) * P], r3(bank(6), P), ACT.Copy)\
                           .then_inc(f_hT.sem, 1)

        @block.gpsimd
        def _(pool):
            pool.sem_inc(g_prod.sem, 1)
            for i in range(NPREP):
                s = i % 2
                pool.wait_ge(prep_v.sem, i + 1)
                if i >= 2:
                    pool.wait_ge(prep_t.sem, i - 1)
                if i >= NFQ:
                    pool.tensor_tensor(pv[s], pv[s], pm[s], ALU.subtract)
                    pool.drain()
                    sc = pamx[s][:, 16:32].unsqueeze(2).to_broadcast([P, 16, QB])
                    pool.tensor_tensor(r3(pq[s], QB), r3(pv[s], QB), sc, ALU.mult).then_inc(prep_q.sem, 1)
                else:
                    pool.tensor_tensor(pv[s], pv[s], pin[s], ALU.subtract)
                    pool.drain()
                    pool.tensor_tensor(pq[s], pv[s], pin[s], ALU.add).then_inc(prep_q.sem, 1)

            with pool.Fori(0, NB) as b:
                with pool.Fori(0, NC) as c:
                    u = b * NC + c
                    for v in range(GK):
                        pool.wait_ge(g_scan.sem, u * GK + v + 1)
                        if v >= NPB:
                            pool.wait_ge(g_red.sem, u * NG + (v - NPB) // 4 + 1)
                        pool.tensor_tensor(Pb[v % NPB], Sb[v % NSB], qg, ALU.mult).then_inc(g_prod.sem, 1)

                def low(dst, src, hi):
                    return pool.tensor_tensor(dst, src, hi.bitcast(F32), ALU.subtract)

                def gu_lo(j):
                    pool.wait_ge(m_guhi.sem, m_guhi.at(b, j + 1))
                    low(guw[j % 2][1], mraw[j % WSLOTS][:, 0:GUW], guw[j % 2][0]).then_inc(m_gulo.sem, 1)

                gu_lo(0)
                pool.wait_ge(m_hhi.sem, m_hhi.at(b, 1))
                low(hsp[1], hT[:, :], hsp[0]).then_inc(m_hlo.sem, 1)
                for j in range(MT):
                    if j + 1 < MT:
                        gu_lo(j + 1)
                    pool.wait_ge(m_dhi.sem, m_dhi.at(b, j + 1))
                    low(dnw[j % 2][1], mraw[j % WSLOTS][:, GUW:GUW + DW], dnw[j % 2][0]).then_inc(m_dlo.sem, 1)

        @block.vector
        def _(dve):
            tt, ts, stt = dve.tensor_tensor, dve.tensor_scalar, dve.scalar_tensor_tensor

            def bcast(ap, n):
                return ap.unsqueeze(2).to_broadcast([ap.shape[0], ap.shape[1], n])

            def quantise_head(src, v, m, amx):
                nbk = 512 // QB
                dve.tensor_reduce(amx[:, 0:nbk], r3(src, QB), AX.X, ALU.max, apply_absolute_value=True)
                dve.drain()
                ts(amx[:, nbk:2 * nbk], amx[:, 0:nbk], 1.0 / 448.0, 1e-30, ALU.mult, ALU.max)
                dve.drain()
                dve.reciprocal(amx[:, 0:nbk], amx[:, nbk:2 * nbk])
                dve.drain()
                tt(r3(v, QB), r3(src, QB), bcast(amx[:, 0:nbk], QB), ALU.mult)
                dve.drain()
                ts(m.bitcast(U32), v.bitcast(U32), 0x7F800000, None, ALU.bitwise_and)
                dve.drain()
                ts(m, m, 2.0 ** -6, 1.5 * 2.0 ** 20, ALU.max, ALU.mult)
                dve.drain()
                return tt(v, v, m, ALU.add)

            def quantise(dst, src, v, m, amx):
                nbk = 512 // QB
                quantise_head(src, v, m, amx)
                dve.drain()
                tt(v, v, m, ALU.subtract)
                dve.drain()
                return tt(r3(dst, QB), r3(v, QB), bcast(amx[:, nbk:2 * nbk], QB), ALU.mult)

            dve.wait_ge(setup_act.sem, 1)
            ts(dscale, tf, 0.5, 0.5, ALU.mult, ALU.add)
            ts(oscale[:, 0:NB], tf, 0.2, 0.8, ALU.mult, ALU.add)
            ts(negA, negA, -1.0, None, ALU.mult)
            dve.drain()
            decay3 = decay.rearrange("p (b n) -> p b n", n=LAYERS * NC)
            tt(decay3[:, 0:NB, :], bcast(dscale, LAYERS * NC),
               dec0.unsqueeze(1).to_broadcast([P, NB, LAYERS * NC]), ALU.mult)
            dve.tensor_copy(oscale[:, NB:NB + 1], oscale[:, 0:1])
            dve.drain()
            dve.tensor_copy(decay3[:, NB, :], decay3[:, 0, :])
            osc3 = oscale.rearrange("p (b n) -> p b n", n=1)
            LC = LAYERS * NC
            dve.tensor_copy(decay_b[:, LC:2 * LC], decay3[:, 0, :])
            dve.tensor_copy(osc_b[:, 1:2], oscale[:, 0:1])
            dve.drain()

            def ratio_start(b, n):
                g0, c = (2, n) if 0 <= n < NC else (0, n % NC)
                f = fch[n % 2]
                dve.wait_ge(ld_f[n % 2].sem, ld_f[n % 2].at(b, n // 2 + 1))
                ts(fmin_e, f, 30.0, None, ALU.min)
                ts(fmin_u, f, wu4[:, g0, 1, c:c + 1], 30.0, ALU.add, ALU.min).then_inc(r_min.sem, 1)

            def ratio_step(b, n, step):
                g0, c, nxt = (2, n, 0) if 0 <= n < NC else (0, n % NC, 1)
                g, f = g0 + step // 3, fch[n % 2]
                if step % 3 == 0:
                    done = r_exp if step == 0 else r_exp2
                    dve.wait_ge(done.sem, done.at(b, n + 1))
                    if step == 0:
                        tt(ekp[:, 0:T], ekp[:, T:2 * T], f, ALU.mult)
                    tt(eup[:, 0:T], eup[:, T:2 * T], f, ALU.mult)
                    dve.drain()
                    dk = decay_b[:, nxt * LC + g * NC + c:nxt * LC + g * NC + c + 1].to_broadcast([P, T])
                    for a in range(2):
                        src = ekp[:, a * T:(a + 1) * T]
                        dve.tensor_tensor_scan(nf2[:, a * T:(a + 1) * T], dk, src, 0.0, ALU.mult, ALU.add)
                        dve.tensor_tensor_scan(nb2[:, a * T:(a + 1) * T][:, ::-1], dk, src[:, ::-1], 0.0,
                                               ALU.mult, ALU.add)
                elif step % 3 == 1:
                    tt(nf2, nf2, nb2, ALU.add)
                    dve.drain()
                    tt(nf2, nf2, ekp, ALU.subtract)
                    dve.drain()
                    tt(eup, eup, nf2, ALU.add)
                    dve.drain()
                    ts(eup[:, T:2 * T], eup[:, T:2 * T], 1e-8, None, ALU.max)
                else:
                    dve.reciprocal(nb2[:, 0:T], eup[:, T:2 * T])
                    dve.drain()
                    q = stt(out=ch(R[g], c), in0=eup[:, 0:T], scalar=osc_b[:, nxt:nxt + 1], in1=nb2[:, 0:T],
                            op0=ALU.mult, op1=ALU.mult)
                    if step == 5:
                        q.then_inc(r_done.sem, 1)
                    else:
                        dve.drain()
                        ts(fmin_u, f, wu4[:, g0 + 1, 1, c:c + 1], 30.0, ALU.add, ALU.min).then_inc(r_min2.sem, 1)
                dve.drain()

            for n in range(4, 8):
                ratio_start(0, n - 8)
                for step in range(6):
                    ratio_step(0, n - 8, step)

            for i in range(NPREP):
                s = i % 2
                dve.wait_ge(prep_ld[s].sem, 16 * (i // 2 + 1))
                if i >= 2:
                    dve.wait_ge(prep_q.sem, i - 1)
                v, m, amx = pv[s], pm[s], pamx[s]
                if i >= NFQ:
                    quantise_head(pin[s], v, m, amx).then_inc(prep_v.sem, 1)
                    dve.drain()
                    continue
                g3 = r3(pin[s], P)
                dve.tensor_reduce(amx[:, 0:4], g3, AX.X, ALU.max, apply_absolute_value=True)
                dve.drain()
                ts(amx[:, 4:8], amx[:, 0:4], 1e-10, 1.0 / 7.0, ALU.max, ALU.mult)
                dve.drain()
                dve.reciprocal(amx[:, 0:4], amx[:, 4:8])
                dve.drain()
                tt(r3(v, P), g3, bcast(amx[:, 0:4], P), ALU.mult)
                dve.drain()
                ts(v, v, MAGIC, MAGIC, ALU.add, ALU.subtract)
                dve.drain()
                ts(v, v, -8.0, 7.0, ALU.max, ALU.min)
                dve.drain()
                tt(r3(v, P), r3(v, P), bcast(amx[:, 4:8], P), ALU.mult).then_inc(prep_v.sem, 1)
                dve.drain()

            dve.wait_ge(prep_c.sem, NPREP)
            dve.wait_ge(prep_st[0].sem, 16 * (NPREP // 2))
            dve.wait_ge(prep_st[1].sem, 16 * (NPREP // 2))
            with dve.Fori(0, NB) as b:
                def gate(i):
                    for c in range(NC):
                        dve.wait_ge(sig_ready.sem, sig_ready.at(b, i * NC + c + 1))
                        q = tt(ch(hT, c), ch(hT, c), ch(R[i], c), ALU.mult)
                    q.then_inc(h_ready.sem, 1)

                def residual(i):
                    for oc in range(NC):
                        tt(ch(xT, oc), ch(xT, oc), bank(oc), ALU.add).then_inc(x_ready.sem, 1)
                    dve.drain()

                gate(0)
                with dve.Fori(0, NC) as c:
                    u = b * NC + c
                    dve.wait_ge(g_evac.sem, u + 1)
                    tt(vlo, bank(2), vhi.bitcast(F32), ALU.subtract).then_inc(g_vlo.sem, 1)
                    for v in range(GK):
                        s = v % NSB
                        if v >= NSB:
                            dve.wait_ge(g_prod.sem, u * GK + v - NSB + 2)
                        dve.wait_ge(g_bc.sem, u * GK + v + 1)
                        tt(Sb[s], bank(5 + v % 3), kg, ALU.mult).then_inc(g_kv.sem, 1)
                        dve.drain()
                        dve.tensor_tensor_scan(Sb[s], ag, Sb[s], 0.0, ALU.mult, ALU.add)\
                           .then_inc(g_scan.sem, 1)
                dve.wait_ge(ln_mean.sem, ln_mean.at(b, 1))
                mean = bank(0).unsqueeze(1).to_broadcast([P, NC, T])
                tt(r3(yT, T), r3(yT, T), mean, ALU.subtract).then_inc(ln_cent.sem, 1)
                dve.wait_ge(ln_sd.sem, ln_sd.at(b, 1))
                dve.reciprocal(sdv, sdv)
                dve.drain()
                tt(r3(yT, T), r3(yT, T), sdv.unsqueeze(1).to_broadcast([P, NC, T]), ALU.mult)
                dve.drain()
                for c in range(NC):
                    q = ts(ch(yT, c), ch(yT, c), gb[:, c:c + 1], gb[:, NC + c:NC + c + 1], ALU.mult, ALU.add)
                q.then_inc(ln_out.sem, 1)
                dve.wait_ge(o_done.sem, o_done.at(b, 1))
                dve.wait_ge(x_copied.sem, x_copied.at(b, 1))
                residual(0)

                gate(1)
                sc = comb
                sfc, pr, grp, gcm, grk = rk[:, 64:128], rk[:, 128:224], rk[:, 224:240], rk[:, 240:304], rk[:, 304:320]
                gcm2, rnk, wsum = rk[:, 320:384], rk[:, 384:448], rk[:, 448:456]
                cmp, cmp2 = rk[:, 1024:2048], rk[:, 2048:3072]
                dve.wait_ge(m_score.sem, m_score.at(b, 1))
                tt(r3(sfc, NE), r3(sc, NE), gate_bias.unsqueeze(1).to_broadcast([P, NT, NE]), ALU.add)
                dve.drain()
                s4, p6 = r3(sfc, 4), r3(pr, 6)
                tt(p6[:, :, 0:3], s4[:, :, 0:3], s4[:, :, 1:4], ALU.add)
                tt(p6[:, :, 3:5], s4[:, :, 0:2], s4[:, :, 2:4], ALU.add)
                tt(p6[:, :, 5:6], s4[:, :, 0:1], s4[:, :, 3:4], ALU.add)
                dve.drain()
                dve.tensor_reduce(grp, p6, AX.X, ALU.max)
                dve.drain()

                def ranks(val, n, c1, c2, low, rank):
                    v3 = r3(val, n)
                    others = v3.unsqueeze(2).to_broadcast([P, NT, n, n])
                    own = v3.unsqueeze(3).to_broadcast([P, NT, n, n])
                    f4 = [x.rearrange("p (t i j) -> p t i j", t=NT, i=n) for x in (c1, c2)]
                    lw = low.rearrange("p (i j) -> p i j", i=n).unsqueeze(1).to_broadcast([P, NT, n, n])
                    tt(f4[0], others, own, ALU.is_gt)
                    tt(f4[1], others, own, ALU.is_ge)
                    dve.drain()
                    tt(f4[1], f4[1], lw, ALU.mult)
                    dve.drain()
                    tt(c1, c1, c2, ALU.max)
                    dve.drain()
                    dve.tensor_reduce(rank, r3(c1, n), AX.X, ALU.add)
                    dve.drain()

                ranks(grp, 4, gcm, gcm2, cst("low4"), grk)
                ts(grk, grk, 1.5, None, ALU.is_lt)
                dve.drain()
                tt(r3(sfc, 4), r3(sfc, 4), bcast(grk, 4), ALU.mult)
                dve.drain()
                ranks(sfc, NE, cmp, cmp2, cst("low16"), rnk)
                ts(rnk, rnk, 5.5, None, ALU.is_lt)
                dve.drain()
                tt(sc, sc, rnk, ALU.mult)
                dve.drain()
                dve.tensor_reduce(wsum[:, 0:4], r3(sc, NE), AX.X, ALU.add)
                dve.drain()
                ts(wsum[:, 0:4], wsum[:, 0:4], 1e-20, None, ALU.add)
                dve.drain()
                dve.reciprocal(wsum[:, 4:8], wsum[:, 0:4])
                dve.drain()
                stt(out=r3(sc, NE), in0=r3(sc, NE), scalar=2.5, in1=bcast(wsum[:, 4:8], NE),
                    op0=ALU.mult, op1=ALU.mult).then_inc(m_comb.sem, 1)
                dve.tensor_copy(decay_b[:, 0:LC], decay3[:, 0:NB, :][:, b, :])
                dve.tensor_copy(decay_b[:, LC:2 * LC], decay3[:, 1:NB + 1, :][:, b, :])
                dve.tensor_copy(osc_b[:, 0:1], osc3[:, 0:NB, :][:, b, :])
                dve.tensor_copy(osc_b[:, 1:2], osc3[:, 1:NB + 1, :][:, b, :])
                dve.drain()
                for j in range(MT):
                    sg = sgt[j % 2]
                    dve.wait_ge(m_silu.sem, m_silu.at(b, j + 1))
                    dve.wait_ge(m_up.sem, m_up.at(b, j + 1))
                    if j >= ST:
                        tt(sg, sg, bank(6), ALU.mult)
                        dve.drain()
                    tt(inter, sg, bank(5), ALU.mult).then_inc(m_prod.sem, 1)
                    dve.drain()
                    n, step = (j - 2) // 6, (j - 2) % 6
                    if j >= 2:
                        ratio_step(b, n, step)
                    if step == 5 and n < 7:
                        ratio_start(b, n + 1)
                    dve.wait_ge(m_ihi.sem, m_ihi.at(b, j + 1))
                    tt(isp[j % 2][1], inter, isp[j % 2][0].bitcast(F32), ALU.subtract).then_inc(m_inter.sem, 1)
                    dve.drain()
                dve.wait_ge(m_down.sem, m_down.at(b, MT))
                residual(1)

                gate(2)
                dve.wait_ge(s_proj.sem, s_proj.at(b, 1))
                ts(vt, bank(3, SH), dtb, None, ALU.add)
                dve.drain()
                stt(out=nab, in0=vt, scalar=-1.0, in1=vt, op0=ALU.mult, op1=ALU.min).then_inc(s_v.sem, 1)
                dve.wait_ge(s_ln.sem, s_ln.at(b, 1))
                stt(out=dtt, in0=vt, scalar=0.0, in1=nab, op0=ALU.max, op1=ALU.add)
                dve.drain()
                ts(eat, dtt, negA, None, ALU.mult).then_inc(s_dt.sem, 1)
                dve.wait_ge(s_th.sem, s_th.at(b, 1))
                tt(gmt, lamt, dtt, ALU.mult)
                dve.drain()
                for k in range(NT):
                    t = slice(k * P, (k + 1) * P)
                    dve.tensor_tensor_scan(cst_[:, t], one[0:SH, :].to_broadcast([SH, P]), eat[:, t], 0.0,
                                           ALU.mult, ALU.add)
                ts(lamt, lamt, -1.0, 1.0, ALU.mult, ALU.add)
                dve.drain()
                tt(lamt, lamt, dtt, ALU.mult)
                for k in range(NT):
                    ts(dl[:, k * SH:(k + 1) * SH], cst("ident")[0:SH, 0:SH], cst_[:, (k + 1) * P - 1:(k + 1) * P],
                       None, ALU.mult)
                dve.drain().then_inc(s_cs.sem, 1)
                dve.wait_ge(s_ea.sem, s_ea.at(b, 1))
                tt(bet, lamt, eat, ALU.mult)
                dve.wait_ge(s_dtavg.sem, s_dtavg.at(b, 1))
                tt(th, th, bank(7, SN), ALU.mult)
                dve.drain()
                dve.tensor_tensor_scan(ang, one[0:SN, :].to_broadcast([SN, T]), th, 0.0, ALU.mult, ALU.add)
                dve.drain()
                inv = 1.0 / (2.0 * np.pi)
                ts(nrd[:, 0, :], ang, inv, None, ALU.mult)
                ts(nrd[:, 1, :], ang, inv, 0.25, ALU.mult, ALU.add)
                dve.drain()
                ts(nrd[:, :, :], nrd[:, :, :], MAGIC, MAGIC, ALU.add, ALU.subtract)
                dve.drain()
                ang2 = ang.unsqueeze(1).to_broadcast([SN, 2, T])
                stt(out=trg[:, :, :], in0=nrd[:, :, :], scalar=-TWO_PI[0], in1=ang2, op0=ALU.mult, op1=ALU.add)
                dve.drain()
                for cpart in TWO_PI[1:]:
                    stt(out=trg[:, :, :], in0=nrd[:, :, :], scalar=-cpart, in1=trg[:, :, :], op0=ALU.mult, op1=ALU.add)
                    dve.drain()
                ts(trg[:, 1, :], trg[:, 1, :], float(np.pi / 2), None, ALU.add)
                dve.drain()
                ts(nrd[:, :, :], trg[:, :, :], 3.1415925, -3.1415925, ALU.min, ALU.max).then_inc(s_ang.sem, 1)
                dve.wait_ge(s_rms.sem, s_rms.at(b, 1))
                dve.reciprocal(brs[:, :, :], brs[:, :, :])
                dve.drain()
                for i in range(2):
                    tt(BCn[:, i, :], bank(i, SN), brs[:, i, :], ALU.mult)
                dve.drain()
                for i in range(2):
                    q = ts(BCn[:, i, :], BCn[:, i, :], bcb[:, i:i + 1], None, ALU.add)
                q.then_inc(s_bcn.sem, 1)
                dve.wait_ge(s_perm.sem, s_perm.at(b, 1))
                dve.wait_ge(s_sin.sem, s_sin.at(b, 1))
                for i in range(2):
                    tt(bsq[:, i, :], bank(i, SN), trg[:, 0, :], ALU.mult)
                    tt(BCn[:, i, :], BCn[:, i, :], trg[:, 1, :], ALU.mult)
                dve.drain()
                tt(BCn[:, :, :], BCn[:, :, :], bsq[:, :, :], ALU.add).then_inc(s_rope.sem, 1)
                dve.wait_ge(s_tm.sem, s_tm.at(b, 1))
                dve.tensor_copy(tm[:, :, :, :], bank(2)[:, 0:NT * 3 * SH].rearrange("p (k a h) -> p k a h", k=NT, a=3))
                dve.tensor_copy(Btm[:, :, :], bank(3)[:, 0:NT * SN].rearrange("p (k n) -> p k n", k=NT))
                dve.tensor_copy(csl, bank(4)[:, 0:NT * SH])
                dve.memset(state[:, :], 0.0)
                dve.drain()
                tt(r3(dend, SH), r3(csl, SH), tm[:, :, 2, :], ALU.subtract).then_inc(s_tmc.sem, 1)

                for k in range(NT):
                    hs = slice(k * SH, (k + 1) * SH)
                    dve.wait_ge(s_cb.sem, s_cb.at(b, k + 1))
                    tt(Gm, bank(4)[:, 0:P], cst("tri"), ALU.mult)
                    dve.drain()
                    dve.wait_ge(s_silu.sem, s_silu.at(b, k + 1))
                    dve.wait_ge(s_exps.sem, s_exps.at(b, 1))
                    if k:
                        dve.wait_ge(s_yss.sem, s_yss.at(b, k))
                    tt(r3(Xg, SP_), r3(xh[k % 2], SP_), bcast(tm[:, k, 0, :], SP_), ALU.mult)
                    dve.wait_ge(s_shift.sem, s_shift.at(b, k + 1))
                    for h in range(2):
                        tt(r3(Xd[:, h * 512:(h + 1) * 512], SP_), r3(bank(h), SP_),
                           bcast(tm[:, k, 1, h * 8:(h + 1) * 8], SP_), ALU.mult)
                    dve.drain()
                    tt(Xg, Xg, Xd, ALU.add)
                    dve.drain()
                    tt(r3(Xd, SP_), r3(Xg, SP_), bcast(dend[:, hs], SP_), ALU.mult).then_inc(s_xg.sem, 1)
                    for g in range(5):
                        if g < 4:
                            dve.wait_ge(s_csb.sem, s_csb.at(b, k * 4 + g + 1))
                            if g >= 2:
                                dve.wait_ge(s_mu.sem, s_mu.at(b, k * 3 + g - 1))
                            tt(r3(Md[:, g % 2, :], P), r3(bank(5 + g % 2), P),
                               bcast(tm[:, k, 2, g * 4:(g + 1) * 4], P), ALU.subtract).then_inc(s_diff.sem, 1)
                        if g >= 1:
                            dve.wait_ge(s_exp.sem, s_exp.at(b, k * 4 + g))
                            m3 = r3(Md[:, (g - 1) % 2, :], P)
                            stt(out=m3, in0=m3, scalar=10000.0, in1=Gm.unsqueeze(1).to_broadcast([P, 4, P]),
                                op0=ALU.min, op1=ALU.mult).then_inc(s_m.sem, 1)
                            dve.drain()
                    dve.wait_ge(s_yo.sem, s_yo.at(b, k + 1))
                    if k:
                        dve.wait_ge(s_tr.sem, s_tr.at(b, k))
                    for h in range(2):
                        tt(r3(Yt[:, h * 512:(h + 1) * 512], SP_), r3(bank(2 + h), SP_),
                           bcast(ecs[:, k * SH + h * 8:k * SH + h * 8 + 8], SP_), ALU.mult)
                    dve.drain()
                    dve.wait_ge(s_yd.sem, s_yd.at(b, k + 1))
                    for h in range(2):
                        y = Yt[:, h * 512:(h + 1) * 512]
                        tt(y, y, bank(h), ALU.add)
                    dve.wait_ge(s_st.sem, s_st.at(b, k + 1))
                    tt(r3(Xd, SP_), r3(xh[k % 2], SP_), bcast(Dbc, SP_), ALU.mult)
                    tt(r3(state, SP_), r3(state, SP_), bcast(eL[0:SN, hs], SP_), ALU.mult)
                    dve.drain()
                    for h in range(2):
                        st = state[:, h * 512:(h + 1) * 512]
                        tt(st, st, bank(4 + 3 * h, SN), ALU.add)
                    tt(Yt, Yt, Xd, ALU.add)
                    dve.drain()
                    tt(Yt, Yt, zs, ALU.mult).then_inc(s_y.sem, 1)
                    dve.wait_ge(s_yss.sem, s_yss.at(b, k + 1))
                    dve.reciprocal(ss[:, 2:3], ss[:, 1:2])
                    dve.drain()
                    ts(Yt, Yt, ss[:, 2:3], None, ALU.mult).then_inc(s_yn.sem, 1)
                dve.wait_ge(s_out.sem, s_out.at(b, 1))
                residual(2)

                gate(3)
                for t in range(NT):
                    dve.wait_ge(f_tx.sem, f_tx.at(b, t + 1))
                    if t >= 2:
                        dve.wait_ge(f_tq.sem, f_tq.at(b, t - 1))
                    quantise(fq[t % 2], bank(4), fv, fm, famx).then_inc(f_qx.sem, 1)
                    dve.drain()
                for i in range(FB * NT):
                    dve.wait_ge(f_silu.sem, f_silu.at(b, i + 1))
                    dve.wait_ge(f_gu.sem, f_gu.at(b, i + 1))
                    tt(fh, fs[i % 2], bank(5), ALU.mult).then_inc(f_mul.sem, 1)
                    dve.drain()
                    if i >= 2:
                        dve.wait_ge(f_tr.sem, f_tr.at(b, i - 1))
                    else:
                        dve.wait_ge(f_tq.sem, f_tq.at(b, NT - 1 + i))
                    quantise(fq[i % 2], fh, fv, fm, famx).then_inc(f_q.sem, 1)
                    dve.drain()
                dve.wait_ge(f_down.sem, f_down.at(b, FB))
                residual(3)


def host_arrays(i):
    ct = np.ascontiguousarray

    def channel_major(x):
        return ct(x.transpose(0, 2, 1).reshape(NB, NC, P, T).transpose(0, 2, 1, 3))

    def per_channel(v):
        return v.reshape(NC, P).T

    def k_major(wt):
        o, k = wt.shape
        return wt.T.reshape(k // P, P, o).transpose(1, 0, 2)

    r = {}
    r["consts"] = constant_table()[1]
    r["moe_sel"] = expert_rows()
    rows = np.arange(NB + 1) % NB
    r["xT"] = ct(channel_major(i["x"])[rows])
    r["fT"] = ct(channel_major(i["fside_BxSxS_0"])[rows].transpose(0, 2, 1, 3))
    r["selv"] = value_selectors()
    r["condT"] = ct(i["cond_512"].T)
    r["wu"] = ct(np.concatenate([per_channel(i[f"{n}_{a}"]) for n in ("L0_cond", "L0_cond2", "L1_cond", "L1_cond2")
                                 for a in "wu"], 1))
    def by_value(v):
        return v.reshape(NC, HPC, GK // 4, 4, *v.shape[1:]).swapaxes(1, 3).reshape(v.shape)

    r["gb"] = ct(np.concatenate([per_channel(by_value(i["L0_attn_gamma"])),
                                 per_channel(by_value(i["L0_attn_beta"]))], 1))
    r["gwT"] = ct(k_major(i["L0_ffn_gate_weight"]).reshape(P, NC * NE))
    r["gate_bias"] = i["L0_ffn_e_score_correction_bias"]
    r["bc_bias"] = ct(np.concatenate([i["L1_attn_B_bias"].T, i["L1_attn_C_bias"].T], 1))
    r["A_log"], r["dt_bias"], r["D_param"] = i["L1_attn_A_log"], i["L1_attn_dt_bias"], i["L1_attn_D_param"]
    qkvg = np.stack([k_major(i[f"L0_attn_W{m}"]) for m in "qkvg"], 1)
    r["w_qkvg"] = ct(qkvg.reshape(P, 4, NC, NC, P).transpose(3, 0, 1, 2, 4))
    r["wo"] = ct(k_major(by_value(i["L0_attn_Wo"].T).T))
    pad = np.zeros((ST * P - NSH * EI, D), np.float32)
    gate = np.concatenate([i["L0_ffn_shared_gate_w"], pad, i["L0_ffn_gate_proj"].reshape(NE * EI, D)])
    up = np.concatenate([i["L0_ffn_shared_up_w"], pad, i["L0_ffn_up_proj"].reshape(NE * EI, D)])
    down = np.concatenate([i["L0_ffn_shared_down_w"].T, pad,
                           i["L0_ffn_down_proj"].transpose(0, 2, 1).reshape(NE * EI, D)])
    gu = np.stack([k_major(gate), k_major(up)], 1).reshape(P, 2, NC, MT, P)
    r["moe_w"] = ct(np.concatenate([gu.transpose(3, 0, 1, 2, 4).reshape(MT, P, GUW), down.reshape(MT, P, D)], 2))
    win, th, lam, wout = (i[f"L1_attn_{n}"] for n in ("W_in", "W_theta", "W_lambda", "W_out"))
    dtw = win[2 * DI + 2 * SN:]
    r["w_fq"] = ct(np.concatenate([win[:2 * DI], wout.reshape(D, 2, 512).transpose(1, 0, 2).reshape(2 * D, 512),
                                   win[2 * DI:2 * DI + 2 * SN], th, th, dtw, lam, dtw, lam]).reshape(-1, P, 512))
    g, u, d = i["L1_ffn_gate_w"], i["L1_ffn_up_w"], i["L1_ffn_down_w"]
    mx = np.stack([g.reshape(FB, 512, D), u.reshape(FB, 512, D), d.reshape(D, FB, 512).transpose(1, 0, 2)], 1)
    r["w_mx"] = ct(mx.reshape(-1, P, 512))
    return r


def kernel(**inputs):
    import concourse.bacc as _bacc
    from concourse.bass_utils import run_bass_kernel_spmd as _run

    nc = _bacc.Bacc("TRN2", target_bir_lowering=False, num_devices=1)
    arrays = host_arrays({k: np.asarray(v) for k, v in inputs.items()})
    A = {k: nc.dram_tensor(k, list(v.shape), F32, kind="ExternalInput").ap() for k, v in arrays.items()}
    out = nc.dram_tensor("out", [NB, P, NC, T], F32, kind="ExternalOutput").ap()
    fq = nc.dram_tensor("scratch_fq", [7, P, 4, 512], F32, kind="Internal").ap()
    mx = nc.dram_tensor("scratch_mx", [FB, 3, P, 4, 512], F32, kind="Internal").ap()
    build(nc, A, out, fq, mx)
    got = _run(nc, [arrays], core_ids=[0]).results[0]["out"]
    return np.ascontiguousarray(got.transpose(0, 2, 1, 3).reshape(NB, D, T).transpose(0, 2, 1))
```

```python
from contextlib import ExitStack

import concourse.bass as bass
from concourse import mybir
import numpy as np

F32 = mybir.dt.float32
F32R = mybir.dt.float32r
BF16 = mybir.dt.bfloat16
U32 = mybir.dt.uint32
ALU = mybir.AluOpType
ACT = mybir.ActivationFunctionType
AX = mybir.AxisListType

P = 128
NB, T, D = 4, 512, 512
NC = D // P
NT = T // P
LAYERS = 4
GH, GK = 16, 32
HPC = P // GK
NE, EI, NSH = 16, 352, 2
ST = -(-NSH * EI // P)
MT = ST + NE * EI // P
GUW, DW = 2 * NC * P, D
WSLOTS = 4
SH, SP_, SN = 16, 64, 64
DI = SH * SP_
FI = 2048
FB = FI // 512
QB = 32

MAGIC = 12582912.0
TWO_PI = (6.28125, float(np.float32(2 * np.pi - 6.28125)),
          2 * np.pi - 6.28125 - float(np.float32(2 * np.pi - 6.28125)))


class Event:

    def __init__(self, sem, per, unit=1, before=0):
        self.sem, self.per, self.unit, self.before = sem, per, unit, before

    def at(self, b, k):
        return (b * self.per + k + self.before) * self.unit


def constant_table():
    parts = {}
    eye = np.eye(P)
    parts["ident"] = eye
    parts["ones"] = np.ones((P, P))
    parts["avg_d"] = np.full((P, P), 1.0 / D)
    parts["shift"] = np.eye(P, k=1)
    edge = np.zeros((P, P))
    edge[P - 1, 0] = 1.0
    parts["edge"] = edge
    red = np.zeros((P, 15, HPC))
    for h in range(HPC):
        red[h * GK:(h + 1) * GK, 7, h] = 1.0
    parts["red"] = red.reshape(P, -1)
    rope = np.zeros((P, SN))
    for m in range(SN // 2):
        rope[m + SN // 2, m] = -1.0
        rope[m, m + SN // 2] = 1.0
    parts["rope"] = rope
    parts["avg_n"] = np.full((P, SN), 1.0 / SN)
    parts["avg_h"] = np.full((P, SN), 1.0 / SH)
    selh = np.zeros((P, SH, P))
    for h in range(SH):
        selh[h, h, :] = 1.0
    parts["selh"] = selh.reshape(P, -1)
    parts["tri"] = np.triu(np.ones((P, P)))
    parts["low16"] = np.tile(np.tril(np.ones((NE, NE)), -1).reshape(1, -1), (P, 1))
    parts["low4"] = np.tile(np.tril(np.ones((4, 4)), -1).reshape(1, -1), (P, 1))
    parts["eps"] = np.tile(np.array([[1e-5, 1.1920929e-07, 1.0, 0.0]]), (P, 1))
    at, n = {}, 0
    for k, v in parts.items():
        at[k] = (n, v.shape[1])
        n += v.shape[1]
    return at, np.concatenate(list(parts.values()), 1).astype(np.float32)


def value_selectors():
    selv = np.zeros((P, GK, HPC, GK), np.float32)
    for h in range(HPC):
        for v in range(GK):
            selv[h * GK + v, v, h, :] = 1.0
    return selv.reshape(P, -1)


def expert_rows():
    sel = np.zeros((3, NE, NE * EI), np.float32)
    for e in range(NE):
        sel[:, e, e * EI:(e + 1) * EI] = 1.0
    return sel.reshape(3 * NE, -1)


def build(nc, A, out, scratch_fq, scratch_mx):
    cat, ctab = constant_table()
    ctx = ExitStack()
    with ctx:
        def sb(name, cols, parts=P):
            return ctx.enter_context(nc.sbuf_tensor("sb_" + name, [parts, cols], F32))

        def ev(name, per, unit=1, before=0):
            return Event(ctx.enter_context(nc.semaphore(name)), per, unit, before)

        banks = [ctx.enter_context(nc.psum_tensor(f"bank{i}", [P, 512], F32)) for i in range(8)]

        def bank(i, rows=P):
            return banks[i][0:rows, :]

        passed = ctx.enter_context(nc.semaphore("passed"))

        def hold(eng):
            eng.sem_inc(passed, 1)

        const = sb("const", ctab.shape[1])

        def cst(name, rows=P):
            a, n = cat[name]
            return const[0:rows, a:a + n]

        eps_ln, eps_rms, one = (const[:, cat["eps"][0] + i:cat["eps"][0] + i + 1] for i in range(3))
        xT = sb("xT", NC * T)
        hT = sb("hT", NC * T)
        R = [sb(f"ratio{i}", NC * T) for i in range(LAYERS)]
        small = sb("small", 1024)
        pos = [0]

        def carve(n, parts=P):
            pos[0] += n
            return small[0:parts, pos[0] - n:pos[0]]

        wu = carve(LAYERS * 2 * NC)
        wu4 = wu.rearrange("p (l a c) -> p l a c", l=LAYERS, a=2)
        condT = carve(NB)
        tf = carve(NB)
        dscale = carve(NB)
        oscale = carve(NB + 1)
        dec0 = carve(LAYERS * NC)
        decay = carve((NB + 1) * LAYERS * NC)
        decay_b = carve(2 * LAYERS * NC)
        osc_b = carve(2)
        comb = carve(NT * NE)
        gb = carve(2 * NC)
        gate_bias = carve(NE)
        gwT = carve(NC * NE)
        bcb = carve(2, SN)
        alog = carve(1, SH)
        negA = carve(1, SH)
        dtb = carve(1, SH)
        Dbc = carve(SH)
        csl = carve(NT * SH)
        eL = carve(NT * SH)
        ecs = carve(NT * SH)
        dend = carve(NT * SH)
        ss = carve(4)
        wob = carve(NC)

        WCOLS = 17408
        work = sb("work", WCOLS)

        def w(a, n, parts=P):
            assert a + n <= WCOLS, (a, n)
            return work[0:parts, a:a + n]

        RCOLS = 12288
        parts = ctx.enter_context(nc.sbuf_tensor("sb_parts", [P, RCOLS], F32R))
        selv_r = ctx.enter_context(nc.sbuf_tensor("sb_selv_r", [P, GK * P], F32R))
        big = parts[:, :].bitcast(F32)

        ld_const = ev("ld_const", 0, 16)
        ld_selv = ev("ld_selv", 0, 16)
        ld_x = ev("ld_x", 1, 16, 1)
        x_copied = ev("x_copied", 1)
        stored = ev("stored", 1, 16, 1)
        setup_pe = ev("setup_pe", 0)
        setup_act = ev("setup_act", 0)
        setup_dve = ev("setup_dve", 0)
        ld_f = [ev(f"ld_f{i}", 4, 16, 2) for i in range(2)]
        r_min = ev("r_min", 8, 1, 4)
        r_exp = ev("r_exp", 8, 1, 4)
        r_min2 = ev("r_min2", 8, 1, 4)
        r_exp2 = ev("r_exp2", 8, 1, 4)
        r_done = ev("r_done", 8, 1, 4)
        sig_ready = ev("sig_ready", LAYERS * NC)
        h_ready = ev("h_ready", LAYERS - 1)
        x_ready = ev("x_ready", LAYERS * NC, 1, 1)
        prep_ld = [ev(f"prep_ld{i}", 0, 16) for i in range(4)]
        prep_v = ev("prep_v", 0)
        prep_q = ev("prep_q", 0)
        prep_t = ev("prep_t", 0)
        prep_c = ev("prep_c", 0)
        prep_st = [ev(f"prep_st{i}", 0, 16) for i in range(2)]
        ld_gw = ev("ld_gw", NC, 16)
        g_proj = ev("g_proj", NC)
        g_evac = ev("g_evac", NC)
        g_vlo = ev("g_vlo", NC)
        NS = NC * GK
        g_bc = ev("g_bc", NS)
        g_kv = ev("g_kv", NS)
        g_scan = ev("g_scan", NS)
        g_prod = ev("g_prod", NS, 1, 1)
        NG = GK // 4
        g_red = ev("g_red", NC * NG)
        y_evac = ev("y_evac", NC, 1, 1)
        ld_wo = ev("ld_wo", 1, 16)
        ln_mean = ev("ln_mean", 1)
        ln_cent = ev("ln_cent", NC)
        ln_sq = ev("ln_sq", NC)
        ln_var = ev("ln_var", 1)
        ln_sd = ev("ln_sd", 1)
        wo_beta = ev("wo_beta", 1)
        wo_scaled = ev("wo_scaled", 1)
        o_done = ev("o_done", NC)
        m_logit = ev("m_logit", 1)
        m_score = ev("m_score", 1)
        m_comb = ev("m_comb", 1)
        m_combT = ev("m_combT", 1)
        m_combC = ev("m_combC", 1)
        ld_mw = [ev(f"ld_mw{s}", len(range(s, MT, WSLOTS)), 16) for s in range(WSLOTS)]
        ld_ms = [ev(f"ld_ms{s}", len(range(s, MT - ST, WSLOTS)), 16) for s in range(WSLOTS)]
        m_hhi = ev("m_hhi", NC)
        m_hlo = ev("m_hlo", 1)
        m_guhi = ev("m_guhi", MT)
        m_gulo = ev("m_gulo", MT)
        m_dhi = ev("m_dhi", MT)
        m_dlo = ev("m_dlo", MT)
        m_gate = ev("m_gate", MT)
        m_up = ev("m_up", MT)
        m_silu = ev("m_silu", MT)
        m_prod = ev("m_prod", MT)
        m_ihi = ev("m_ihi", MT)
        m_inter = ev("m_inter", MT)
        m_down = ev("m_down", MT)
        ld_sm = ev("ld_sm", 1, 16)
        ld_sw = ev("ld_sw", 4, 16)
        ld_so = ev("ld_so", 2, 16)
        s_proj = ev("s_proj", 1)
        s_sq = ev("s_sq", 1)
        s_ms = ev("s_ms", 1)
        s_rms = ev("s_rms", 1)
        s_raw = ev("s_raw", 1)
        s_th = ev("s_th", 1)
        s_v = ev("s_v", 1)
        s_ln = ev("s_ln", 1)
        s_dt = ev("s_dt", 1)
        s_dtavg = ev("s_dtavg", 1)
        s_ea = ev("s_ea", 1)
        s_bcn = ev("s_bcn", 1)
        s_perm = ev("s_perm", 1)
        s_ang = ev("s_ang", 1)
        s_sin = ev("s_sin", 1)
        s_rope = ev("s_rope", 1)
        s_tm = ev("s_tm", 1)
        s_tmc = ev("s_tmc", 1)
        s_exps = ev("s_exps", 1)
        s_xz = ev("s_xz", NT * 4)
        s_silu = ev("s_silu", NT * 4)
        s_shift = ev("s_shift", NT)
        s_xg = ev("s_xg", NT)
        s_cb = ev("s_cb", 1)
        s_gm = ev("s_gm", 1)
        s_csb = ev("s_csb", NT * 4)
        s_diff = ev("s_diff", NT * 4)
        s_exp = ev("s_exp", NT * 4)
        s_m = ev("s_m", NT * 4)
        s_mu = ev("s_mu", NT * 3)
        s_cs = ev("s_cs", 1)
        s_yd = ev("s_yd", NT)
        s_yo = ev("s_yo", NT)
        s_st = ev("s_st", NT - 1)
        s_state = ev("s_state", NT - 1)
        s_gx = ev("s_gx", NT)
        s_dx = ev("s_dx", NT)
        s_xdec = ev("s_xdec", NT - 1)
        s_sdec = ev("s_sdec", NT - 1)
        s_y = ev("s_y", NT)
        s_yss = ev("s_yss", NT)
        s_yr = ev("s_yr", NT)
        s_yn = ev("s_yn", NT)
        s_tr = ev("s_tr", NT)
        s_ynT = ev("s_ynT", NT)
        s_out = ev("s_out", NT)
        h_tile = ev("h_tile", NT)
        ld_fw = [ev(f"ld_fw{s}", 2, 16) for s in range(2)]
        f_tx = ev("f_tx", NT)
        f_vx = ev("f_vx", NT)
        f_qx = ev("f_qx", NT)
        f_tq = ev("f_tq", NT)
        f_xT = ev("f_xT", NT)
        f_gate = ev("f_gate", NT * FB)
        f_mul = ev("f_mul", NT * FB)
        f_gu = ev("f_gu", NT * FB)
        f_silu = ev("f_silu", NT * FB)
        f_q = ev("f_q", NT * FB)
        f_tr = ev("f_tr", NT * FB)
        f_hT = ev("f_hT", NT * FB)
        f_down = ev("f_down", FB)

        gw = w(0, 4 * NC * P).rearrange("p (m c o) -> p m c o", m=4, c=NC)
        qg, kg, ag = [[w(a + i * T, T) for a in (2048, 10240)] for i in range(3)]
        NSB, NPB = 3, 6
        OB = (1, 2, 3, 7)
        Sb = [w(3584 + s * T, T) for s in range(NSB)]
        Pb = [w(5120 + s * T, T) for s in range(NPB)]
        yT = w(8192, NC * T)
        ysq = w(10240, NC * T)
        sdv = w(12288, T)
        wo = w(12800, NC * D).rearrange("p (c o) -> p c o", c=NC)
        PB0, PB = (6, 5, 4, 7), (0, 1, 2, 3)
        vhi, vlo = [[parts[:, (2 * s + i) * T:(2 * s + i + 1) * T] for s in range(2)] for i in range(2)]
        xnext = w(14848, NC * T)
        mraw = [w(s * (GUW + DW), GUW + DW) for s in range(WSLOTS)]
        msel = [w(6144 + s * P, P, 3 * NE) for s in range(WSLOTS)]
        combT = w(6656, T // 2, 3 * NE).bitcast(BF16)
        mselb = [w(6912 + s * P // 2, P // 2, 3 * NE).bitcast(BF16) for s in range(2)]
        sgt = [w(7168 + s * T, T) for s in range(2)]
        inter = w(8192, T)
        rk = w(8704, 3 * 1024)
        cparts = w(14848 + 1088, NT * 3 * NE).rearrange("p (t n) -> p t n", t=NT)
        cpart_b = [w(14848 + 1088 + 192 + i * 32, 32).bitcast(BF16) for i in range(3)]

        def split_slots(at, n):
            return [[parts[:, at + (2 * s + i) * n:at + (2 * s + i + 1) * n] for i in range(2)] for s in range(2)]

        guw = split_slots(0, GUW)
        dnw = split_slots(4096, DW)
        isp = split_slots(6144, T)
        hsp = [parts[:, 8192 + i * NC * T:8192 + (i + 1) * NC * T] for i in range(2)]
        ekp, eup, nf2, nb2 = (w(8704 + i * 1024, 1024) for i in range(4))
        fmin_e, fmin_u = w(12800, T), w(13312, T)
        fch = [w(13824 + s * T, T) for s in range(2)]

        def ch(ap, c):
            return ap[:, c * T:(c + 1) * T]

        block = ctx.enter_context(nc.Block())

        NIN, NQV = 4, 3
        pin = [w(s * 512, 512) for s in range(NIN)]
        pq = [w(2048 + s * 512, 512) for s in range(2)]
        pt_ = [w(3072 + s * 512, 512) for s in range(2)]
        pv = [w(4096 + s * 512, 512) for s in range(NQV)]
        pm = [w(5632 + s * 512, 512) for s in range(NQV)]
        pamx = [w(7168 + s * 64, 64) for s in range(NQV)]
        NFQ, NMX = 26, 48
        NPREP = NFQ + NMX

        wzx = big[:, 0:8192].rearrange("p (m c o) -> p m c o", m=4, c=NC)
        wout = big[:, 8192:12288].rearrange("p (m c o) -> p m c o", m=2, c=4)
        wm6 = w(14912, 1024).rearrange("p (c o) -> p c o", c=NC)
        ynT = w(0, 8 * T)
        ynT8 = ynT.rearrange("p (i t) -> p i t", i=8)
        xh = [w(4096 + k * 1024, 1024) for k in range(NT)]
        o = 8192
        Xd = w(o, 1024)
        Md = w(o + 1024, 1024).rearrange("p (s n) -> p s n", s=2)
        Xg = [w(o + 2048, 1024), w(14272, 1024)]
        Yt = [w(o + 3072, 1024), w(15296, 1024)]
        state = w(o + 4096, 1024, SN)
        tm = w(13312, NT * 3 * SH).rearrange("p (k a h) -> p k a h", k=NT, a=3)
        Btm = w(13504, NT * SN).rearrange("p (k n) -> p k n", k=NT)
        Gm = w(13760, NT * P).rearrange("p (k n) -> p k n", k=NT)
        Dx = w(16320, 1024)
        small2 = sb("small2", 2 * T + 3 * T)
        BCn = small2[0:SN, 0:2 * T].rearrange("p (a t) -> p a t", a=2)
        dtt = small2[0:SH, 2 * T:3 * T]
        cst_ = small2[0:SH, 3 * T:4 * T]
        gmt = small2[0:SH, 4 * T:5 * T]
        bsq = w(o, 2 * T, SN).rearrange("p (a t) -> p a t", a=2)
        brs = w(14912, 2 * T, SN).rearrange("p (a t) -> p a t", a=2)
        th = w(o + 1024, T, SN)
        ang = w(o + 1536, T, SN)
        trg = w(o + 2048, 2 * T, SN).rearrange("p (a t) -> p a t", a=2)
        nrd = w(o + 3072, 2 * T, SN).rearrange("p (a t) -> p a t", a=2)
        vt = w(o + 4096, T, SH)
        nab = w(o + 4608, T, SH)
        lamt = w(14400, T, SH)
        bet = w(15936, T, SH)
        eat = w(16448, T, SH)
        dl = w(16960, NT * SH, SH)

        fw = [big[:, s * 6144:(s + 1) * 6144].rearrange("p (m c o) -> p m c o", m=3, c=4) for s in range(2)]
        xqT = small2[:, 0:NC * T].rearrange("p (c t) -> p c t", c=NC)
        fs = [w(2048 + s * 512, 512) for s in range(2)]
        fh = w(3072, 512)
        fv = w(3584, 512)
        fm = w(4096, 512)
        fq = [w(4608 + s * 512, 512) for s in range(2)]
        hqT = [w(5632 + s * 2048, 2048).rearrange("p (i t) -> p i t", i=4) for s in range(2)]
        fqx = [w(9856 + s * 512, 512) for s in range(2)]
        fxv = [w(10944 + s * 512, 512) for s in range(2)]
        fxm = [w(11968 + s * 512, 512) for s in range(2)]
        fxamx = [w(12992 + s * 64, 64) for s in range(2)]
        famx = w(9728, 64)

        def r3(ap, n):
            return ap.rearrange("p (a n) -> p a n", n=n)

        def store_prepared(sp, i):
            s = i % 2
            sp.wait_ge(prep_c.sem, i + 1)
            src = r3(pt_[s], P)
            if i < NFQ:
                dst = scratch_fq[i // 4][:, :, (i % 4) * P:(i % 4 + 1) * P]
            else:
                k = i - NFQ
                dst = scratch_mx[k // 12][(k // 4) % 3][:, :, (k % 4) * P:(k % 4 + 1) * P]
            sp.dma_start(dst, src).then_inc(prep_st[s].sem, 16)

        def load_f(sp, n, f_row):
            sp.dma_start(fch[n % 2], f_row[n % NC]).then_inc(ld_f[n % 2].sem, 16)

        def tile_of(x, k):
            return x[:, :].rearrange("p (c t) -> p c t", c=NC)[:, :, k * P:(k + 1) * P]

        f_next = A["fT"][1:NB + 1]
        x_next = A["xT"][1:NB + 1]

        @block.sync
        def _(sp):
            sp.sem_inc(stored.sem, 16)
            for dst, src in ((const[:, :], A["consts"]), (condT, A["condT"]),
                             (wu, A["wu"]), (gb, A["gb"]), (gwT, A["gwT"]),
                             (gate_bias, A["gate_bias"].rearrange("(a n) -> a n", a=1).to_broadcast([P, NE])),
                             (bcb, A["bc_bias"]), (alog, A["A_log"].rearrange("(a n) -> a n", n=1)),
                             (dtb, A["dt_bias"].rearrange("(a n) -> a n", n=1)),
                             (Dbc, A["D_param"].rearrange("(a n) -> a n", a=1).to_broadcast([P, SH]))):
                sp.dma_start(dst, src).then_inc(ld_const.sem, 16)
            load_f(sp, 4, A["fT"][0])
            load_f(sp, 5, A["fT"][0])
            for i in range(NPREP):
                s = i % NIN
                if i >= NIN:
                    sp.wait_ge(prep_q.sem, i - NIN + 1)
                sp.dma_start(pin[s], A["w_fq"][i] if i < NFQ else A["w_mx"][i - NFQ]).then_inc(prep_ld[s].sem, 16)
                if i >= 3:
                    store_prepared(sp, i - 3)
                if i == NFQ:
                    sp.dma_start(r3(xnext, T), A["xT"][0]).then_inc(ld_x.sem, 16)
                    for h in range(2):
                        sp.dma_start(R[2 + h][:, :], A["selv"][:, h * 2048:(h + 1) * 2048]).then_inc(ld_selv.sem, 16)
                for n in (6, 7):
                    if i == 18 * (n - 5) + 4:
                        sp.wait_ge(r_done.sem, r_done.at(0, n - 1 - 8))
                        load_f(sp, n, A["fT"][0])
            sp.wait_ge(prep_q.sem, NPREP)
            sp.dma_start(gw, A["w_qkvg"][0]).then_inc(ld_gw.sem, 16)
            for i in range(NPREP - 3, NPREP):
                store_prepared(sp, i)
            sp.wait_ge(prep_st[0].sem, 16 * (NPREP // 2))
            sp.wait_ge(prep_st[1].sem, 16 * (NPREP // 2))

            with sp.Fori(0, NB) as b:
                sp.wait_ge(h_ready.sem, h_ready.at(b, 1))
                sp.dma_start(wo, A["wo"]).then_inc(ld_wo.sem, 16)
                for c in range(1, NC):
                    sp.wait_ge(g_proj.sem, g_proj.at(b, c))
                    sp.dma_start(gw, A["w_qkvg"][c]).then_inc(ld_gw.sem, 16)
                sp.wait_ge(y_evac.sem, y_evac.at(b, NC))
                for j in range(MT):
                    s, i = j % WSLOTS, j - ST
                    if j >= WSLOTS:
                        sp.wait_ge(m_down.sem, m_down.at(b, j - WSLOTS + 1))
                    sp.dma_start(mraw[s], A["moe_w"][j]).then_inc(ld_mw[s].sem, 16)
                    if i >= 0:
                        sp.dma_start(msel[i % WSLOTS], A["moe_sel"][:, i * P:(i + 1) * P])\
                          .then_inc(ld_ms[i % WSLOTS].sem, 16)
                    if j == WSLOTS - 1:
                        sp.wait_ge(o_done.sem, o_done.at(b, NC))
                        for n in range(2):
                            load_f(sp, n, A["fT"][b])
                        sp.wait_ge(x_copied.sem, x_copied.at(b, 1))
                        sp.dma_start(wm6, scratch_fq[6][:, :, 0:256]).then_inc(ld_sm.sem, 16)
                    n = (j + 1) // 6
                    if j % 6 == 5 and 2 <= n < 8:
                        sp.wait_ge(r_done.sem, r_done.at(b, n - 1))
                        load_f(sp, n, A["fT"][b] if n < NC else f_next[b])
                sp.wait_ge(m_down.sem, m_down.at(b, MT))
                for m in (2, 3, 0, 1):
                    sp.dma_start(wzx[:, m, :, :], scratch_fq[m]).then_inc(ld_sw.sem, 16)
                for m in range(2):
                    sp.dma_start(wout[:, m, :, :], scratch_fq[4 + m]).then_inc(ld_so.sem, 16)
                for ib in range(FB):
                    s = ib % 2
                    if ib == 0:
                        sp.wait_ge(s_xz.sem, s_xz.at(b, NT * 4))
                    elif ib == 1:
                        sp.wait_ge(s_out.sem, s_out.at(b, NT))
                    else:
                        sp.wait_ge(f_down.sem, f_down.at(b, ib - 1))
                    sp.dma_start(fw[s], scratch_mx[ib].rearrange("m p c o -> p m c o")).then_inc(ld_fw[s].sem, 16)
                    if ib == 1:
                        sp.dma_start(gw, A["w_qkvg"][0]).then_inc(ld_gw.sem, 16)
                        sp.dma_start(r3(xnext, T), x_next[b]).then_inc(ld_x.sem, 16)
                sp.wait_ge(x_ready.sem, x_ready.at(b, LAYERS * NC))
                sp.dma_start(out[b], r3(xT[:, :], T)).then_inc(stored.sem, 16)
            sp.wait_ge(stored.sem, 16 * (NB + 1))
            sp.wait_ge(ld_x.sem, 16 * (NB + 1))
            sp.wait_ge(ld_gw.sem, 16 * (NB * NC + 1))

        @block.tensor
        def _(pe):
            pe.wait_ge(ld_const.sem, 16 * 10)
            pe.matmul(bank(0)[:, 0:NB], cst("ones"), condT, start=True, stop=True).then_inc(setup_pe.sem, 1)
            for i in range(NPREP):
                s = i % 2
                pe.wait_ge(prep_q.sem, i + 1)
                if i >= 2:
                    pe.wait_ge(prep_c.sem, i - 1)
                for c in range(4):
                    mm = pe.transpose(bank(6 + s)[:, c * P:(c + 1) * P], pq[s][:, c * P:(c + 1) * P], cst("ident"))
                mm.then_inc(prep_t.sem, 1)

            def project(banks_of, m, k):
                return pe.matmul(bank(banks_of[m]), gw[:, m, k, :], ch(hT, k), start=(k == 0), stop=(k == NC - 1))

            pe.wait_ge(prep_c.sem, NPREP)
            pe.wait_ge(h_ready.sem, h_ready.at(0, 1))
            pe.wait_ge(ld_gw.sem, ld_gw.at(0, 1))
            for m in range(4):
                for k in range(NC):
                    mm = project(PB0, m, k)
            mm.then_inc(g_proj.sem, 1)

            with pe.Fori(0, NB) as b:
                def chunk(c):
                    u = b * NC + c
                    pe.wait_ge(g_evac.sem, u + 1)
                    pe.wait_ge(g_vlo.sem, u + 1)
                    hold(pe)
                    if c < NC - 1:
                        pe.wait_ge(ld_gw.sem, (u + 2) * 16)
                        hold(pe)
                    for v in range(GK):
                        if v >= 3:
                            pe.wait_ge(g_kv.sem, u * GK + v - 2)
                        elif c:
                            pe.wait_ge(g_kv.sem, u * GK)
                        selv = selv_r[:, v * P:(v + 1) * P]
                        pe.matmul(bank(5 + v % 3), selv, vhi[c % 2], start=True, stop=False)
                        pe.matmul(bank(5 + v % 3), selv, vlo[c % 2], start=False, stop=True).then_inc(g_bc.sem, 1)
                        if c < NC - 1 and v % 3 < 2 and v < 24:
                            n = v // 3 * 2 + v % 3
                            mm = project(PB, n // NC, n % NC)
                            if n == 4 * NC - 1:
                                mm.then_inc(g_proj.sem, 1)
                        if v >= 6 and v % 4 == 2:
                            reduce_group(c, v // 4 - 1)
                        if c and v == 2:
                            reduce_group(c - 1, NG - 1)
                        if c == NC - 1 and v in (8, 10, 12):
                            k = (v - 8) // 2
                            pe.matmul(bank(0), cst("avg_d"), ch(yT, k), start=(k == 0), stop=False)
                        if c == NC - 1 and v in (16, 18, 20, 22):
                            if v == 16:
                                pe.wait_ge(ld_wo.sem, ld_wo.at(b, 1))
                            oc = (v - 16) // 2
                            for k in range(NC):
                                mm = pe.matmul(bank(1)[:, oc:oc + 1], wo[:, k, oc * P:(oc + 1) * P],
                                               gb[:, NC + k:NC + k + 1], start=(k == 0), stop=(k == NC - 1))
                            if v == 22:
                                mm.then_inc(wo_beta.sem, 1)
                    if c == NC - 1:
                        reduce_group(c, NG - 1)

                def reduce_group(c, g):
                    u = b * NC + c
                    pe.wait_ge(g_prod.sem, u * GK + 4 * g + 5)
                    if g == 0:
                        pe.wait_ge(y_evac.sem, u + 1)
                        hold(pe)
                    red = cst("red")[:, (7 - g) * HPC:(15 - g) * HPC]
                    for j in range(4):
                        mm = pe.matmul(bank(4)[32 * j:32 * j + 32, :], red, Pb[(c * GK + 4 * g + j) % NPB],
                                       start=(g == 0), stop=(g == NG - 1))
                    mm.then_inc(g_red.sem, 1)

                pe.wait_ge(x_ready.sem, x_ready.at(b, 0))
                hold(pe)
                for c in range(NC):
                    chunk(c)
                pe.wait_ge(y_evac.sem, y_evac.at(b, NC))
                pe.matmul(bank(0), cst("avg_d"), ch(yT, NC - 1), start=False, stop=True).then_inc(ln_mean.sem, 1)
                pe.wait_ge(wo_scaled.sem, wo_scaled.at(b, 1))
                for k in range(NC):
                    pe.wait_ge(ln_cent.sem, ln_cent.at(b, k + 1))
                    for oc in range(NC):
                        mm = pe.matmul(bank(OB[oc]), wo[:, k, oc * P:(oc + 1) * P], ch(yT, k),
                                       start=(k == 0), stop=(k == NC - 1))
                        if k == NC - 1:
                            mm.then_inc(o_done.sem, 1)
                    if k == 0:
                        for q in range(NC):
                            pe.wait_ge(ln_sq.sem, ln_sq.at(b, q + 1))
                            mm = pe.matmul(bank(6), cst("avg_d"), ch(ysq, q), start=(q == 0), stop=(q == NC - 1))
                        mm.then_inc(ln_var.sem, 1)

                pe.wait_ge(h_ready.sem, h_ready.at(b, 2))
                for t in range(NT):
                    for k in range(NC):
                        mm = pe.matmul(bank(7)[:, t * NE:(t + 1) * NE], ch(hT, k)[:, t * P:(t + 1) * P],
                                       gwT[:, k * NE:(k + 1) * NE], start=(k == 0), stop=(k == NC - 1))
                mm.then_inc(m_logit.sem, 1)
                pe.wait_ge(m_hlo.sem, m_hlo.at(b, 1))

                def three(dst, lhs, rhs, first, last):
                    pe.matmul(dst, lhs[0], rhs[0], start=first, stop=False)
                    pe.matmul(dst, lhs[0], rhs[1], start=False, stop=False)
                    return pe.matmul(dst, lhs[1], rhs[0], start=False, stop=last)

                def project_in(j, which, dst):
                    for k in range(NC):
                        a = (which * NC + k) * P
                        mm = three(dst, [x[:, a:a + P] for x in guw[j % 2]], [ch(x, k) for x in hsp],
                                   k == 0, k == NC - 1)
                    return mm

                def down(j):
                    pe.wait_ge(m_dlo.sem, m_dlo.at(b, j + 1))
                    pe.wait_ge(m_inter.sem, m_inter.at(b, j + 1))
                    for oc in range(NC):
                        mm = three(bank(oc), [x[:, oc * P:(oc + 1) * P] for x in dnw[j % 2]], isp[j % 2],
                                   j == 0, j == MT - 1)
                    mm.then_inc(m_down.sem, 1)

                for j in range(MT):
                    i = j - ST
                    pe.wait_ge(m_gulo.sem, m_gulo.at(b, j + 1))
                    if j:
                        pe.wait_ge(m_silu.sem, m_silu.at(b, j))
                    project_in(j, 0, bank(4)).then_inc(m_gate.sem, 1)
                    if j:
                        pe.wait_ge(m_prod.sem, m_prod.at(b, j))
                    if i >= 0:
                        pe.matmul(bank(6), mselb[i % 2], combT, start=True, stop=True)
                    project_in(j, 1, bank(5)).then_inc(m_up.sem, 1)
                    if j:
                        down(j - 1)
                    if j == ST - 2:
                        pe.wait_ge(m_comb.sem, m_comb.at(b, 1))
                        hold(pe)
                        for t in range(NT):
                            mm = pe.transpose(bank(7)[0:3 * NE, t * P:(t + 1) * P], cparts[:, t, :], cst("ident"))
                        mm.then_inc(m_combT.sem, 1)
                    if j == ST - 1:
                        pe.wait_ge(m_combC.sem, m_combC.at(b, 1))
                down(MT - 1)

                pe.wait_ge(h_ready.sem, h_ready.at(b, 3))
                pe.wait_ge(ld_sm.sem, ld_sm.at(b, 1))
                for i, (a, n) in enumerate(((0, 64), (64, 64), (128, 128))):
                    for k in range(NC):
                        mm = pe.matmul(bank(i, n), wm6[:, k, a:a + n], ch(hT, k), start=(k == 0), stop=(k == NC - 1))
                mm.then_inc(s_proj.sem, 1)
                pe.wait_ge(ld_sw.sem, ld_sw.at(b, 4))
                idn = cst("ident")
                for i in range(NT * 4):
                    k, m = i // 4, (2, 3, 0, 1)[i % 4]
                    if i == 2:
                        pe.wait_ge(s_sq.sem, s_sq.at(b, 1))
                        hold(pe)
                        for q in range(2):
                            mm = pe.matmul(bank(3 + q, SN), cst("avg_n", SN), bsq[:, q, :], start=True, stop=True)
                        mm.then_inc(s_ms.sem, 1)
                        pe.wait_ge(s_dt.sem, s_dt.at(b, 1))
                        pe.matmul(bank(5, SN), cst("avg_h", SH), dtt, start=True, stop=True).then_inc(s_dtavg.sem, 1)
                    if i == 8:
                        pe.wait_ge(s_bcn.sem, s_bcn.at(b, 1))
                        hold(pe)
                        for q in range(2):
                            mm = pe.matmul(bank(q, SN), cst("rope", SN), BCn[:, q, :], start=True, stop=True)
                        mm.then_inc(s_perm.sem, 1)
                    if i == 10:
                        pe.wait_ge(s_rope.sem, s_rope.at(b, 1))
                        hold(pe)
                        for kk in range(NT):
                            tk = slice(kk * P, (kk + 1) * P)
                            for a, src in enumerate((gmt, bet, cst_)):
                                pe.transpose(bank(2)[:, (kk * 3 + a) * SH:(kk * 3 + a + 1) * SH], src[:, tk],
                                             idn[0:SH, 0:SH])
                            pe.transpose(bank(3)[:, kk * SN:(kk + 1) * SN], BCn[:, 0, tk], idn[0:SN, 0:SN])
                        pe.matmul(bank(4)[:, 0:NT * SH], cst("ones", SH), dl, start=True, stop=True)\
                          .then_inc(s_tm.sem, 1)
                        for kk in range(NT):
                            tk = slice(kk * P, (kk + 1) * P)
                            mm = pe.matmul(bank(5)[:, tk], BCn[:, 0, tk], BCn[:, 1, tk], start=True, stop=True)
                        mm.then_inc(s_cb.sem, 1)
                    if i >= 2:
                        pe.wait_ge(s_silu.sem, s_silu.at(b, i - 1))
                    for kk in range(NC):
                        mm = pe.matmul(bank(6 + i % 2), ch(hT, kk)[:, k * P:(k + 1) * P], wzx[:, m, kk, :],
                                       start=(kk == 0), stop=(kk == NC - 1))
                    mm.then_inc(s_xz.sem, 1)
                pe.wait_ge(s_silu.sem, s_silu.at(b, NT * 4))
                pe.wait_ge(s_gm.sem, s_gm.at(b, 1))

                def cs_bcast(k, g):
                    for hh in range(4):
                        h = g * 4 + hh
                        mm = pe.matmul(bank(5 + g % 2)[:, hh * P:(hh + 1) * P], cst("selh", SH)[:, h * P:(h + 1) * P],
                                       cst_[:, k * P:(k + 1) * P], start=True, stop=True)
                    mm.then_inc(s_csb.sem, 1)

                def diagonal(k, g):
                    pe.wait_ge(s_m.sem, s_m.at(b, k * 4 + g + 1))
                    for hh in range(4):
                        h = g * 4 + hh
                        mm = pe.matmul(bank(h // 8)[:, (h % 8) * SP_:(h % 8 + 1) * SP_],
                                       Md[:, g % 2, hh * P:(hh + 1) * P],
                                       Xg[k % 2][:, h * SP_:(h + 1) * SP_], start=True, stop=True)
                    mm.then_inc((s_yd if g == 3 else s_mu).sem, 1)

                def y_transposes(k):
                    pe.wait_ge(s_yn.sem, s_yn.at(b, k + 1))
                    for i in range(8):
                        mm = pe.transpose(bank(2 + i // 4)[:, (i % 4) * P:(i % 4 + 1) * P],
                                          Yt[k % 2][:, i * P:(i + 1) * P], idn)
                    mm.then_inc(s_tr.sem, 1)

                def out_project(k, half):
                    if half == 0:
                        pe.wait_ge(s_ynT.sem, s_ynT.at(b, k + 1))
                        if k == 0:
                            pe.wait_ge(ld_so.sem, ld_so.at(b, 2))
                        else:
                            pe.wait_ge(x_ready.sem, x_ready.at(b, 2 * NC + k))
                    for oc in range(2 * half, 2 * half + 2):
                        for i in range(8):
                            mm = pe.matmul(bank(7)[:, oc * P:(oc + 1) * P], wout[:, i // 4, i % 4, oc * P:(oc + 1) * P],
                                           ynT8[:, i, k * P:(k + 1) * P], start=(i == 0), stop=(i == 7))
                    if half:
                        mm.then_inc(s_out.sem, 1)

                for k in range(NT):
                    t = slice(k * P, (k + 1) * P)
                    if k:
                        pe.wait_ge(s_y.sem, s_y.at(b, k))
                    for h in range(2):
                        col = slice(h * 512, (h + 1) * 512)
                        mm = pe.matmul(bank(h), cst("shift"), xh[k][:, col], start=True, stop=(k == 0))
                        if k:
                            mm = pe.matmul(bank(h), cst("edge"), xh[k - 1][:, col], start=False, stop=True)
                    mm.then_inc(s_shift.sem, 1)
                    if k:
                        pe.wait_ge(s_state.sem, s_state.at(b, k))
                    cs_bcast(k, 0)
                    if k:
                        y_transposes(k - 1)
                    cs_bcast(k, 1)
                    pe.wait_ge(s_diff.sem, s_diff.at(b, k * 4 + 1))
                    cs_bcast(k, 2)
                    if k:
                        out_project(k - 1, 0)
                    pe.wait_ge(s_xg.sem, s_xg.at(b, k + 1))
                    diagonal(k, 0)
                    pe.wait_ge(s_diff.sem, s_diff.at(b, k * 4 + 2))
                    cs_bcast(k, 3)
                    diagonal(k, 1)
                    diagonal(k, 2)
                    if k:
                        pe.wait_ge(s_ynT.sem, s_ynT.at(b, k))
                    else:
                        pe.wait_ge(s_tmc.sem, s_tmc.at(b, 1))
                    for h in range(2):
                        mm = pe.matmul(bank(2 + h), BCn[:, 1, t], state[:, h * 512:(h + 1) * 512],
                                       start=True, stop=True)
                    mm.then_inc(s_yo.sem, 1)
                    diagonal(k, 3)
                    if k < NT - 1:
                        pe.wait_ge(s_xdec.sem, s_xdec.at(b, k + 1))
                        for h in range(2):
                            mm = pe.matmul(bank(4 + h, SN), Btm[:, k, :], Xd[:, h * 512:(h + 1) * 512],
                                           start=True, stop=True)
                        mm.then_inc(s_st.sem, 1)
                    if k:
                        out_project(k - 1, 1)
                pe.wait_ge(s_y.sem, s_y.at(b, NT))
                y_transposes(NT - 1)
                out_project(NT - 1, 0)
                out_project(NT - 1, 1)


                def x_transpose(t):
                    pe.wait_ge(h_tile.sem, h_tile.at(b, t + 1))
                    if t:
                        pe.wait_ge(f_vx.sem, f_vx.at(b, t))
                    for c in range(NC):
                        mm = pe.transpose(bank(7)[:, c * P:(c + 1) * P], ch(hT, c)[:, t * P:(t + 1) * P], idn)
                    mm.then_inc(f_tx.sem, 1)

                def xq_transpose(t):
                    pe.wait_ge(f_qx.sem, f_qx.at(b, t + 1))
                    if t == 1:
                        pe.wait_ge(f_xT.sem, f_xT.at(b, 1))
                    elif t > 1:
                        pe.wait_ge(f_hT.sem, f_hT.at(b, t - 1))
                    for c in range(NC):
                        mm = pe.transpose(bank(6)[:, c * P:(c + 1) * P], fqx[t % 2][:, c * P:(c + 1) * P], idn)
                    mm.then_inc(f_tq.sem, 1)

                pe.wait_ge(x_ready.sem, x_ready.at(b, 2 * NC + NT))
                x_transpose(0)
                xq_transpose(0)
                x_transpose(1)

                def f_transposes(i):
                    pe.wait_ge(f_q.sem, f_q.at(b, i + 1))
                    if i < NT - 1:
                        pe.wait_ge(f_xT.sem, f_xT.at(b, i + 2))
                    else:
                        pe.wait_ge(f_hT.sem, f_hT.at(b, i))
                    for c in range(4):
                        mm = pe.transpose(bank(6)[:, c * P:(c + 1) * P], fq[i % 2][:, c * P:(c + 1) * P], idn)
                    mm.then_inc(f_tr.sem, 1)

                def f_downs(ib):
                    pe.wait_ge(f_hT.sem, f_hT.at(b, (ib + 1) * NT))
                    for oc in range(NC):
                        for i in range(4):
                            mm = pe.matmul(bank(oc), fw[ib % 2][:, 2, i, oc * P:(oc + 1) * P], hqT[ib % 2][:, i, :],
                                           start=(ib == 0 and i == 0), stop=(ib == FB - 1 and i == 3))
                    mm.then_inc(f_down.sem, 1)

                for ib in range(FB):
                    pe.wait_ge(ld_fw[ib % 2].sem, ld_fw[ib % 2].at(b, ib // 2 + 1))
                    for t in range(NT):
                        i = ib * NT + t
                        if i:
                            pe.wait_ge(f_silu.sem, f_silu.at(b, i))
                        if ib == 0:
                            pe.wait_ge(f_xT.sem, f_xT.at(b, t + 1))
                        for k in range(NC):
                            mm = pe.matmul(bank(4), xqT[:, k, t * P:(t + 1) * P], fw[ib % 2][:, 0, k, :],
                                           start=(k == 0), stop=(k == NC - 1))
                        mm.then_inc(f_gate.sem, 1)
                        if i:
                            pe.wait_ge(f_mul.sem, f_mul.at(b, i))
                        for k in range(NC):
                            mm = pe.matmul(bank(5), xqT[:, k, t * P:(t + 1) * P], fw[ib % 2][:, 1, k, :],
                                           start=(k == 0), stop=(k == NC - 1))
                        mm.then_inc(f_gu.sem, 1)
                        if i:
                            f_transposes(i - 1)
                        if i + 1 < NT:
                            xq_transpose(i + 1)
                        if i + 2 < NT:
                            x_transpose(i + 2)
                        if t == 1 and ib:
                            f_downs(ib - 1)
                pe.wait_ge(h_ready.sem, h_ready.at(b, LAYERS))
                pe.wait_ge(ld_gw.sem, ld_gw.at(b, NC + 1))
                pe.wait_ge(f_mul.sem, f_mul.at(b, FB * NT))
                for m in (2, 1, 3):
                    for k in range(NC):
                        project(PB0, m, k)
                f_transposes(FB * NT - 1)
                f_downs(FB - 1)
                for k in range(NC):
                    mm = project(PB0, 0, k)
                mm.then_inc(g_proj.sem, 1)

        def ratio_exps(act, b, n, second):
            if second:
                act.wait_ge(r_min2.sem, r_min2.at(b, n + 1))
                act.activation(eup[:, T:2 * T], fmin_u, ACT.Exp).then_inc(r_exp2.sem, 1)
            else:
                act.wait_ge(r_min.sem, r_min.at(b, n + 1))
                act.activation(ekp[:, T:2 * T], fmin_e, ACT.Exp)
                act.activation(eup[:, T:2 * T], fmin_u, ACT.Exp).then_inc(r_exp.sem, 1)

        @block.scalar
        def _(act):
            act.sem_inc(y_evac.sem, 1)
            act.wait_ge(setup_pe.sem, 1)
            act.activation(tf, bank(0)[:, 0:NB], ACT.Sigmoid)
            act.wait_ge(ld_const.sem, 16 * 10)
            act.activation(dec0.rearrange("p (l c) -> p l c", l=LAYERS), wu4[:, :, 0, :], ACT.Exp)
            act.activation(negA, alog, ACT.Exp)
            act.drain()
            act.activation(dec0, dec0, ACT.Exp, scale=-1.0).then_inc(setup_act.sem, 1)
            def first_sigmoids(loaded):
                act.wait_ge(ld_x.sem, loaded)
                for c in range(NC):
                    act.activation(ch(hT, c), ch(xnext, c), ACT.Sigmoid).then_inc(sig_ready.sem, 1)

            for i in range(NPREP):
                s = i % 2
                if i == NFQ + 20:
                    first_sigmoids(ld_x.at(0, 0))
                    act.wait_ge(ld_selv.sem, 32)
                    for h in range(2):
                        act.activation(selv_r[:, h * 2048:(h + 1) * 2048], R[2 + h][:, :], ACT.Copy)
                if i == 0:
                    ratio_exps(act, 0, 4 - 8, 0)
                elif i % 18 == 17 and i < 54:
                    ratio_exps(act, 0, i // 18 + 5 - 8, 0)
                elif i % 18 == 8:
                    ratio_exps(act, 0, i // 18 + 4 - 8, 1)
                act.wait_ge(prep_t.sem, i + 1)
                if i >= 2:
                    act.wait_ge(prep_st[s].sem, 16 * (i // 2))
                act.activation(pt_[s], bank(6 + s), ACT.Copy).then_inc(prep_c.sem, 1)
            act.wait_ge(prep_st[0].sem, 16 * (NPREP // 2))
            act.wait_ge(prep_st[1].sem, 16 * (NPREP // 2))
            with act.Fori(0, NB) as b:
                def sigmoids(i):
                    for c in range(NC):
                        act.wait_ge(x_ready.sem, x_ready.at(b, (i - 1) * NC + c + 1))
                        act.activation(ch(hT, c), ch(xT, c), ACT.Sigmoid).then_inc(sig_ready.sem, 1)

                act.wait_ge(stored.sem, stored.at(b, 0))
                act.activation(xT[:, :], xnext, ACT.Copy).then_inc(x_copied.sem, 1)

                def evacuate(c):
                    s = c % 2
                    act.wait_ge(g_proj.sem, g_proj.at(b, c + 1))
                    if c >= 2:
                        act.wait_ge(g_prod.sem, g_prod.at(b, (c - 1) * GK))
                    q, k, v, g = PB if c else PB0
                    act.activation(vhi[s], bank(v), ACT.Copy)
                    act.activation(ag[s], bank(g), ACT.Sigmoid)
                    act.activation(kg[s], bank(k), ACT.Copy)
                    act.activation(qg[s], bank(q), ACT.Copy, scale=float(GK) ** -0.5).then_inc(g_evac.sem, 1)

                evacuate(0)
                for c in range(NC):
                    if c + 1 < NC:
                        evacuate(c + 1)
                    else:
                        act.wait_ge(wo_beta.sem, wo_beta.at(b, 1))
                        act.activation(wob, bank(1)[:, 0:NC], ACT.Copy)
                        for k in range(NC):
                            q = act.activation(wo[:, k, :], wo[:, k, :], ACT.Copy, scale=gb[:, k:k + 1])
                        q.then_inc(wo_scaled.sem, 1)
                    act.wait_ge(g_red.sem, g_red.at(b, (c + 1) * NG))
                    act.activation(ch(yT, c), bank(4), ACT.Copy).then_inc(y_evac.sem, 1)
                for c in range(NC):
                    act.wait_ge(ln_cent.sem, ln_cent.at(b, c + 1))
                    act.activation(ch(ysq, c), ch(yT, c), ACT.Square).then_inc(ln_sq.sem, 1)
                act.wait_ge(ln_var.sem, ln_var.at(b, 1))
                act.activation(sdv, bank(6), ACT.Sqrt, bias=eps_ln).then_inc(ln_sd.sem, 1)
                sigmoids(1)
                def gu_hi(j):
                    act.wait_ge(ld_mw[j % WSLOTS].sem, ld_mw[j % WSLOTS].at(b, j // WSLOTS + 1))
                    if j >= 2:
                        act.wait_ge(m_up.sem, m_up.at(b, j - 1))
                    i = j - ST
                    if i >= 0:
                        act.wait_ge(ld_ms[i % WSLOTS].sem, ld_ms[i % WSLOTS].at(b, i // WSLOTS + 1))
                        act.activation(mselb[i % 2], msel[i % WSLOTS], ACT.Copy)
                    act.activation(guw[j % 2][0], mraw[j % WSLOTS][:, 0:GUW], ACT.Copy).then_inc(m_guhi.sem, 1)

                gu_hi(0)
                act.wait_ge(h_ready.sem, h_ready.at(b, 2))
                for c in range(NC):
                    act.activation(ch(hsp[0], c), ch(hT, c), ACT.Copy).then_inc(m_hhi.sem, 1)
                act.wait_ge(m_logit.sem, m_logit.at(b, 1))
                act.activation(comb, bank(7)[:, 0:NT * NE], ACT.Sigmoid).then_inc(m_score.sem, 1)
                for j in range(MT):
                    act.wait_ge(m_gate.sem, m_gate.at(b, j + 1))
                    if j >= 2:
                        act.wait_ge(m_prod.sem, m_prod.at(b, j - 1))
                    act.activation(sgt[j % 2], bank(4), ACT.Silu).then_inc(m_silu.sem, 1)
                    if j + 1 < MT:
                        gu_hi(j + 1)
                    if j >= 2:
                        act.wait_ge(m_down.sem, m_down.at(b, j - 1))
                    act.activation(dnw[j % 2][0], mraw[j % WSLOTS][:, GUW:GUW + DW], ACT.Copy).then_inc(m_dhi.sem, 1)
                    if j == ST - 1:
                        act.wait_ge(m_combT.sem, m_combT.at(b, 1))
                        act.activation(combT, bank(7, 3 * NE), ACT.Copy).then_inc(m_combC.sem, 1)
                    n, step = (j - 3) // 6, (j - 3) % 6
                    if j >= 2 and step == 5 and n < 7:
                        ratio_exps(act, b, n + 1, 0)
                    if j >= 2 and step == 2:
                        ratio_exps(act, b, n, 1)
                    act.wait_ge(m_prod.sem, m_prod.at(b, j + 1))
                    act.activation(isp[j % 2][0], inter, ACT.Copy).then_inc(m_ihi.sem, 1)
                sigmoids(2)
                act.wait_ge(s_proj.sem, s_proj.at(b, 1))
                act.activation(vt, bank(2)[64:64 + SH, :], ACT.Copy).then_inc(s_raw.sem, 1)
                for i in range(2):
                    q = act.activation(bsq[:, i, :], bank(i, SN), ACT.Square)
                q.then_inc(s_sq.sem, 1)
                act.activation(th, bank(2, SN), ACT.Copy)
                act.activation(lamt, bank(2)[96:96 + SH, :], ACT.Sigmoid).then_inc(s_th.sem, 1)
                act.wait_ge(s_v.sem, s_v.at(b, 1))
                act.activation(nab, nab, ACT.Exp)
                act.drain()
                act.activation(nab, nab, ACT.Ln, bias=one[0:SH, :]).then_inc(s_ln.sem, 1)
                for i in range(NT * 4):
                    if i == 2:
                        act.wait_ge(s_ms.sem, s_ms.at(b, 1))
                        for q in range(2):
                            mm = act.activation(brs[:, q, :], bank(3 + q, SN), ACT.Sqrt, bias=eps_rms[0:SN, :])
                        mm.then_inc(s_rms.sem, 1)
                        act.wait_ge(s_cs.sem, s_cs.at(b, 1))
                        act.activation(eat, eat, ACT.Exp).then_inc(s_ea.sem, 1)
                    if i == 6:
                        act.wait_ge(s_ang.sem, s_ang.at(b, 1))
                        act.activation(trg[:, :, :], nrd[:, :, :], ACT.Sin).then_inc(s_sin.sem, 1)
                    if i == 13:
                        act.wait_ge(s_tmc.sem, s_tmc.at(b, 1))
                        act.activation(eL, csl, ACT.Exp)
                        act.activation(dend, dend, ACT.Exp)
                        act.activation(r3(ecs, SH), tm[:, :, 2, :], ACT.Exp).then_inc(s_exps.sem, 1)
                    k, h = i // 4, i % 2
                    act.wait_ge(s_xz.sem, s_xz.at(b, i + 1))
                    if i % 4 < 2:
                        q = act.activation(xh[k][:, h * 512:(h + 1) * 512], bank(6 + h), ACT.Silu)
                    else:
                        q = act.activation(ynT8[:, 4 * h:4 * h + 4, k * P:(k + 1) * P], r3(bank(6 + h), P), ACT.Silu)
                    q.then_inc(s_silu.sem, 1)

                def decay_exp(k, g):
                    act.wait_ge(s_diff.sem, s_diff.at(b, k * 4 + g + 1))
                    act.activation(Md[:, g % 2, :], Md[:, g % 2, :], ACT.Exp).then_inc(s_exp.sem, 1)

                def normalise(k):
                    act.wait_ge(s_yr.sem, s_yr.at(b, k + 1))
                    act.activation(Yt[k % 2], Yt[k % 2], ACT.Copy, scale=ss[:, 2:3]).then_inc(s_yn.sem, 1)

                def y_evacuate(k):
                    act.wait_ge(s_tr.sem, s_tr.at(b, k + 1))
                    for i in range(2):
                        q = act.activation(ynT8[:, 4 * i:4 * i + 4, k * P:(k + 1) * P], r3(bank(2 + i), P), ACT.Copy)
                    q.then_inc(s_ynT.sem, 1)

                for k in range(NT):
                    if k:
                        normalise(k - 1)
                    decay_exp(k, 0)
                    if k:
                        y_evacuate(k - 1)
                    decay_exp(k, 1)
                    decay_exp(k, 2)
                    decay_exp(k, 3)
                    act.wait_ge(s_y.sem, s_y.at(b, k + 1))
                    act.activation(Dx, Yt[k % 2], ACT.Square, accum_out=ss[:, 0:1])
                    act.drain()
                    act.activation(ss[:, 1:2], ss[:, 0:1], ACT.Sqrt, bias=eps_rms, scale=1.0 / DI).then_inc(s_yss.sem, 1)
                normalise(NT - 1)
                y_evacuate(NT - 1)
                for k in range(NT):
                    act.wait_ge(x_ready.sem, x_ready.at(b, 2 * NC + k + 1))
                    act.activation(tile_of(hT, k), tile_of(xT, k), ACT.Sigmoid).then_inc(sig_ready.sem, 1)
                for i in range(FB * NT + 1):
                    if i == 8:
                        act.wait_ge(f_tx.sem, f_tx.at(b, NT))
                        first_sigmoids(ld_x.at(b, 1))
                    if i < NT:
                        act.wait_ge(f_tq.sem, f_tq.at(b, i + 1))
                        act.activation(xqT[:, :, i * P:(i + 1) * P], r3(bank(6), P), ACT.Copy).then_inc(f_xT.sem, 1)
                    if i < FB * NT:
                        act.wait_ge(f_gate.sem, f_gate.at(b, i + 1))
                        if i >= 2:
                            act.wait_ge(f_mul.sem, f_mul.at(b, i - 1))
                        act.activation(fs[i % 2], bank(4), ACT.Silu).then_inc(f_silu.sem, 1)
                    if i:
                        ib, t = (i - 1) // NT, (i - 1) % NT
                        act.wait_ge(f_tr.sem, f_tr.at(b, i))
                        if t == 0 and ib >= 2:
                            act.wait_ge(f_down.sem, f_down.at(b, ib - 1))
                        act.activation(hqT[ib % 2][:, :, t * P:(t + 1) * P], r3(bank(6), P), ACT.Copy)\
                           .then_inc(f_hT.sem, 1)

        @block.gpsimd
        def _(pool):
            pool.sem_inc(g_prod.sem, 1)
            for i in range(NPREP):
                s, v, src = i % 2, pv[i % NQV], pin[i % NIN]
                pool.wait_ge(prep_v.sem, i + 1)
                if i >= NFQ:
                    pool.tensor_tensor(v, v, pm[i % NQV], ALU.add)
                    pool.drain()
                    pool.tensor_tensor(v, v, pm[i % NQV], ALU.subtract)
                else:
                    f3 = pamx[i % NQV][:, 4:8].unsqueeze(2).to_broadcast([P, 4, P])
                    pool.tensor_tensor(r3(v, P), r3(v, P), f3, ALU.mult)
                    pool.drain()
                    pool.tensor_tensor(v, v, src, ALU.subtract)
                pool.drain()
                if i >= 2:
                    pool.wait_ge(prep_t.sem, i - 1)
                if i >= NFQ:
                    sc = pamx[i % NQV][:, 16:32].unsqueeze(2).to_broadcast([P, 16, QB])
                    pool.tensor_tensor(r3(pq[s], QB), r3(v, QB), sc, ALU.mult).then_inc(prep_q.sem, 1)
                else:
                    pool.tensor_tensor(pq[s], v, src, ALU.add).then_inc(prep_q.sem, 1)

            with pool.Fori(0, NB) as b:
                for i in range(NS):
                    pool.wait_ge(g_scan.sem, g_scan.at(b, i + 1))
                    if i >= NPB:
                        pool.wait_ge(g_red.sem, g_red.at(b, (i - NPB) // 4 + 1))
                    pool.tensor_tensor(Pb[i % NPB], Sb[i % NSB], qg[i // GK % 2], ALU.mult).then_inc(g_prod.sem, 1)

                def low(dst, src, hi):
                    return pool.tensor_tensor(dst, src, hi.bitcast(F32), ALU.subtract)

                def gu_lo(j):
                    pool.wait_ge(m_guhi.sem, m_guhi.at(b, j + 1))
                    low(guw[j % 2][1], mraw[j % WSLOTS][:, 0:GUW], guw[j % 2][0]).then_inc(m_gulo.sem, 1)

                gu_lo(0)
                for j in range(MT):
                    if j + 1 < MT:
                        gu_lo(j + 1)
                    pool.wait_ge(m_dhi.sem, m_dhi.at(b, j + 1))
                    low(dnw[j % 2][1], mraw[j % WSLOTS][:, GUW:GUW + DW], dnw[j % 2][0]).then_inc(m_dlo.sem, 1)

                def per_head(dst, src, factor):
                    rows = dst.shape[0]
                    f3 = factor.unsqueeze(2).to_broadcast([rows, SH, SP_])
                    return pool.tensor_tensor(r3(dst, SP_), r3(src, SP_), f3, ALU.mult)

                pool.wait_ge(s_tmc.sem, s_tmc.at(b, 1))
                pool.wait_ge(s_silu.sem, s_silu.at(b, NT * 4))
                per_head(Xg[0], xh[0], tm[:, 0, 0, :]).then_inc(s_gx.sem, 1)
                for k in range(NT):
                    hs = slice(k * SH, (k + 1) * SH)
                    if k:
                        pool.wait_ge(s_yss.sem, s_yss.at(b, k))
                    per_head(Dx, xh[k], Dbc).then_inc(s_dx.sem, 1)
                    if k < NT - 1:
                        pool.wait_ge(s_xg.sem, s_xg.at(b, k + 1))
                        per_head(Xd, Xg[k % 2], dend[:, hs]).then_inc(s_xdec.sem, 1)
                        per_head(Xg[(k + 1) % 2], xh[k + 1], tm[:, k + 1, 0, :]).then_inc(s_gx.sem, 1)
                        pool.wait_ge(s_yo.sem, s_yo.at(b, k + 1))
                        per_head(state, state, eL[0:SN, hs]).then_inc(s_sdec.sem, 1)

                for t in range(NT):
                    v, m = fxv[t % 2], fxm[t % 2]
                    pool.wait_ge(f_vx.sem, f_vx.at(b, t + 1))
                    pool.tensor_tensor(v, v, m, ALU.subtract)
                    pool.drain()
                    if t >= 2:
                        pool.wait_ge(f_tq.sem, f_tq.at(b, t - 1))
                    sc = fxamx[t % 2][:, 16:32].unsqueeze(2).to_broadcast([P, 16, QB])
                    pool.tensor_tensor(r3(fqx[t % 2], QB), r3(v, QB), sc, ALU.mult).then_inc(f_qx.sem, 1)

        @block.vector
        def _(dve):
            tt, ts, stt = dve.tensor_tensor, dve.tensor_scalar, dve.scalar_tensor_tensor

            def bcast(ap, n):
                return ap.unsqueeze(2).to_broadcast([ap.shape[0], ap.shape[1], n])

            def quantise_head(src, v, m, amx):
                nbk = 512 // QB
                dve.tensor_reduce(amx[:, 0:nbk], r3(src, QB), AX.X, ALU.max, apply_absolute_value=True)
                dve.drain()
                ts(amx[:, nbk:2 * nbk], amx[:, 0:nbk], 1.0 / 448.0, 1e-30, ALU.mult, ALU.max)
                dve.drain()
                dve.reciprocal(amx[:, 0:nbk], amx[:, nbk:2 * nbk])
                dve.drain()
                tt(r3(v, QB), r3(src, QB), bcast(amx[:, 0:nbk], QB), ALU.mult)
                dve.drain()
                ts(m.bitcast(U32), v.bitcast(U32), 0x7F800000, None, ALU.bitwise_and)
                dve.drain()
                return ts(m, m, 2.0 ** -6, 1.5 * 2.0 ** 20, ALU.max, ALU.mult)

            def quantise(dst, src, v, m, amx):
                nbk = 512 // QB
                quantise_head(src, v, m, amx)
                dve.drain()
                tt(v, v, m, ALU.add)
                dve.drain()
                tt(v, v, m, ALU.subtract)
                dve.drain()
                return tt(r3(dst, QB), r3(v, QB), bcast(amx[:, nbk:2 * nbk], QB), ALU.mult)

            dve.sem_inc(x_ready.sem, 1)
            dve.wait_ge(setup_act.sem, 1)
            ts(dscale, tf, 0.5, 0.5, ALU.mult, ALU.add)
            ts(oscale[:, 0:NB], tf, 0.2, 0.8, ALU.mult, ALU.add)
            ts(negA, negA, -1.0, None, ALU.mult)
            dve.drain()
            decay3 = decay.rearrange("p (b n) -> p b n", n=LAYERS * NC)
            tt(decay3[:, 0:NB, :], bcast(dscale, LAYERS * NC),
               dec0.unsqueeze(1).to_broadcast([P, NB, LAYERS * NC]), ALU.mult)
            dve.tensor_copy(oscale[:, NB:NB + 1], oscale[:, 0:1])
            dve.drain()
            dve.tensor_copy(decay3[:, NB, :], decay3[:, 0, :])
            osc3 = oscale.rearrange("p (b n) -> p b n", n=1)
            LC = LAYERS * NC
            dve.tensor_copy(decay_b[:, LC:2 * LC], decay3[:, 0, :])
            dve.tensor_copy(osc_b[:, 1:2], oscale[:, 0:1])
            dve.drain()

            def ratio_start(b, n):
                g0, c = (2, n) if 0 <= n < NC else (0, n % NC)
                f = fch[n % 2]
                dve.wait_ge(ld_f[n % 2].sem, ld_f[n % 2].at(b, n // 2 + 1))
                ts(fmin_e, f, 30.0, None, ALU.min)
                ts(fmin_u, f, wu4[:, g0, 1, c:c + 1], 30.0, ALU.add, ALU.min).then_inc(r_min.sem, 1)

            def ratio_step(b, n, step):
                g0, c, nxt = (2, n, 0) if 0 <= n < NC else (0, n % NC, 1)
                g, f = g0 + step // 3, fch[n % 2]
                if step % 3 == 0:
                    done = r_exp if step == 0 else r_exp2
                    dve.wait_ge(done.sem, done.at(b, n + 1))
                    if step == 0:
                        tt(ekp[:, 0:T], ekp[:, T:2 * T], f, ALU.mult)
                    tt(eup[:, 0:T], eup[:, T:2 * T], f, ALU.mult)
                    dve.drain()
                    dk = decay_b[:, nxt * LC + g * NC + c:nxt * LC + g * NC + c + 1].to_broadcast([P, T])
                    for a in range(2):
                        src = ekp[:, a * T:(a + 1) * T]
                        dve.tensor_tensor_scan(nf2[:, a * T:(a + 1) * T], dk, src, 0.0, ALU.mult, ALU.add)
                        dve.tensor_tensor_scan(nb2[:, a * T:(a + 1) * T][:, ::-1], dk, src[:, ::-1], 0.0,
                                               ALU.mult, ALU.add)
                elif step % 3 == 1:
                    tt(nf2, nf2, nb2, ALU.add)
                    dve.drain()
                    tt(nf2, nf2, ekp, ALU.subtract)
                    dve.drain()
                    tt(eup, eup, nf2, ALU.add)
                    dve.drain()
                    ts(eup[:, T:2 * T], eup[:, T:2 * T], 1e-8, None, ALU.max)
                else:
                    dve.reciprocal(nb2[:, 0:T], eup[:, T:2 * T])
                    dve.drain()
                    q = stt(out=ch(R[g], c), in0=eup[:, 0:T], scalar=osc_b[:, nxt:nxt + 1], in1=nb2[:, 0:T],
                            op0=ALU.mult, op1=ALU.mult)
                    if step == 5:
                        q.then_inc(r_done.sem, 1)
                    else:
                        dve.drain()
                        ts(fmin_u, f, wu4[:, g0 + 1, 1, c:c + 1], 30.0, ALU.add, ALU.min).then_inc(r_min2.sem, 1)
                dve.drain()


            for i in range(NPREP):
                dve.wait_ge(prep_ld[i % NIN].sem, 16 * (i // NIN + 1))
                if i >= NQV:
                    dve.wait_ge(prep_q.sem, i - NQV + 1)
                src, v, m, amx = pin[i % NIN], pv[i % NQV], pm[i % NQV], pamx[i % NQV]
                if i >= NFQ:
                    quantise_head(src, v, m, amx).then_inc(prep_v.sem, 1)
                else:
                    g3 = r3(src, P)
                    dve.tensor_reduce(amx[:, 0:4], g3, AX.X, ALU.max, apply_absolute_value=True)
                    dve.drain()
                    ts(amx[:, 4:8], amx[:, 0:4], 1e-10, 1.0 / 7.0, ALU.max, ALU.mult)
                    dve.drain()
                    dve.reciprocal(amx[:, 0:4], amx[:, 4:8])
                    dve.drain()
                    tt(r3(v, P), g3, bcast(amx[:, 0:4], P), ALU.mult)
                    dve.drain()
                    ts(v, v, MAGIC, MAGIC, ALU.add, ALU.subtract)
                    dve.drain()
                    ts(v, v, -8.0, 7.0, ALU.max, ALU.min).then_inc(prep_v.sem, 1)
                dve.drain()
                if i == 0:
                    ratio_start(0, 4 - 8)
                if i % 3 == 2:
                    n, step = i // 18 + 4, i // 3 % 6
                    ratio_step(0, n - 8, step)
                    if step == 5 and n < 7:
                        ratio_start(0, n + 1 - 8)

            def gate(b, i):
                for c in range(NC):
                    dve.wait_ge(sig_ready.sem, sig_ready.at(b, i * NC + c + 1))
                    q = tt(ch(hT, c), ch(hT, c), ch(R[i % LAYERS], c), ALU.mult)
                q.then_inc(h_ready.sem, 1)

            gate(0, 0)
            dve.wait_ge(prep_c.sem, NPREP)
            dve.wait_ge(prep_st[0].sem, 16 * (NPREP // 2))
            dve.wait_ge(prep_st[1].sem, 16 * (NPREP // 2))
            with dve.Fori(0, NB) as b:
                def residual(i):
                    for oc in range(NC):
                        tt(ch(xT, oc), ch(xT, oc), bank(oc), ALU.add).then_inc(x_ready.sem, 1)
                    dve.drain()

                def v_low(c):
                    dve.wait_ge(g_evac.sem, g_evac.at(b, c + 1))
                    tt(vlo[c % 2], bank((PB if c else PB0)[2]), vhi[c % 2].bitcast(F32), ALU.subtract).then_inc(g_vlo.sem, 1)

                v_low(0)
                for i in range(NS):
                    c, s = i // GK, i % NSB
                    if i % GK == GK - 2 and c + 1 < NC:
                        v_low(c + 1)
                    if i >= NSB:
                        dve.wait_ge(g_prod.sem, g_prod.at(b, i - NSB + 1))
                    dve.wait_ge(g_bc.sem, g_bc.at(b, i + 1))
                    tt(Sb[s], bank(5 + i % GK % 3), kg[c % 2], ALU.mult).then_inc(g_kv.sem, 1)
                    dve.drain()
                    dve.tensor_tensor_scan(Sb[s], ag[c % 2], Sb[s], 0.0, ALU.mult, ALU.add).then_inc(g_scan.sem, 1)
                dve.wait_ge(ln_mean.sem, ln_mean.at(b, 1))
                for c in range(NC):
                    tt(ch(yT, c), ch(yT, c), bank(0), ALU.subtract).then_inc(ln_cent.sem, 1)
                dve.wait_ge(ln_sd.sem, ln_sd.at(b, 1))
                dve.reciprocal(sdv, sdv)
                dve.drain()
                dve.wait_ge(x_copied.sem, x_copied.at(b, 1))
                for oc in range(NC):
                    dve.wait_ge(o_done.sem, o_done.at(b, oc + 1))
                    tt(ch(ysq, oc), bank(OB[oc]), sdv, ALU.mult)
                    dve.drain()
                    stt(out=ch(xT, oc), in0=ch(ysq, oc), scalar=wob[:, oc:oc + 1], in1=ch(xT, oc),
                        op0=ALU.add, op1=ALU.add).then_inc(x_ready.sem, 1)
                dve.drain()

                gate(b, 1)
                for c in range(NC):
                    dve.wait_ge(m_hhi.sem, m_hhi.at(b, c + 1))
                    q = tt(ch(hsp[1], c), ch(hT, c), ch(hsp[0], c).bitcast(F32), ALU.subtract)
                q.then_inc(m_hlo.sem, 1)
                sc = comb
                sfc, pr, grp, gcm, grk = rk[:, 64:128], rk[:, 128:224], rk[:, 224:240], rk[:, 240:304], rk[:, 304:320]
                gcm2, rnk, wsum = rk[:, 320:384], rk[:, 384:448], rk[:, 448:456]
                cmp, cmp2 = rk[:, 1024:2048], rk[:, 2048:3072]
                dve.wait_ge(m_score.sem, m_score.at(b, 1))
                tt(r3(sfc, NE), r3(sc, NE), gate_bias.unsqueeze(1).to_broadcast([P, NT, NE]), ALU.add)
                dve.drain()
                s4, p6 = r3(sfc, 4), r3(pr, 6)
                tt(p6[:, :, 0:3], s4[:, :, 0:3], s4[:, :, 1:4], ALU.add)
                tt(p6[:, :, 3:5], s4[:, :, 0:2], s4[:, :, 2:4], ALU.add)
                tt(p6[:, :, 5:6], s4[:, :, 0:1], s4[:, :, 3:4], ALU.add)
                dve.drain()
                dve.tensor_reduce(grp, p6, AX.X, ALU.max)
                dve.drain()

                def ranks(val, n, c1, c2, low, rank):
                    v3 = r3(val, n)
                    others = v3.unsqueeze(2).to_broadcast([P, NT, n, n])
                    own = v3.unsqueeze(3).to_broadcast([P, NT, n, n])
                    f4 = [x.rearrange("p (t i j) -> p t i j", t=NT, i=n) for x in (c1, c2)]
                    lw = low.rearrange("p (i j) -> p i j", i=n).unsqueeze(1).to_broadcast([P, NT, n, n])
                    tt(f4[0], others, own, ALU.is_gt)
                    tt(f4[1], others, own, ALU.is_ge)
                    dve.drain()
                    tt(f4[1], f4[1], lw, ALU.mult)
                    dve.drain()
                    tt(c1, c1, c2, ALU.max)
                    dve.drain()
                    dve.tensor_reduce(rank, r3(c1, n), AX.X, ALU.add)
                    dve.drain()

                ranks(grp, 4, gcm, gcm2, cst("low4"), grk)
                ts(grk, grk, 1.5, None, ALU.is_lt)
                dve.drain()
                tt(r3(sfc, 4), r3(sfc, 4), bcast(grk, 4), ALU.mult)
                dve.drain()
                ranks(sfc, NE, cmp, cmp2, cst("low16"), rnk)
                ts(rnk, rnk, 5.5, None, ALU.is_lt)
                dve.drain()
                tt(sc, sc, rnk, ALU.mult)
                dve.drain()
                dve.tensor_reduce(wsum[:, 0:4], r3(sc, NE), AX.X, ALU.add)
                dve.drain()
                ts(wsum[:, 0:4], wsum[:, 0:4], 1e-20, None, ALU.add)
                dve.drain()
                dve.reciprocal(wsum[:, 4:8], wsum[:, 0:4])
                dve.drain()
                stt(out=r3(sc, NE), in0=r3(sc, NE), scalar=2.5, in1=bcast(wsum[:, 4:8], NE),
                    op0=ALU.mult, op1=ALU.mult)
                dve.drain()
                for i in range(3):
                    dve.tensor_copy(cpart_b[i], sc)
                    dve.drain()
                    q = dve.tensor_copy(cparts[:, :, i * NE:(i + 1) * NE], r3(cpart_b[i], NE))
                    if i < 2:
                        tt(sc, sc, cpart_b[i], ALU.subtract)
                        dve.drain()
                q.then_inc(m_comb.sem, 1)
                dve.tensor_copy(decay_b[:, 0:LC], decay3[:, 0:NB, :][:, b, :])
                dve.tensor_copy(decay_b[:, LC:2 * LC], decay3[:, 1:NB + 1, :][:, b, :])
                dve.tensor_copy(osc_b[:, 0:1], osc3[:, 0:NB, :][:, b, :])
                dve.tensor_copy(osc_b[:, 1:2], osc3[:, 1:NB + 1, :][:, b, :])
                dve.drain()
                for j in range(MT):
                    sg = sgt[j % 2]
                    dve.wait_ge(m_silu.sem, m_silu.at(b, j + 1))
                    dve.wait_ge(m_up.sem, m_up.at(b, j + 1))
                    if j >= ST:
                        tt(sg, sg, bank(6), ALU.mult)
                        dve.drain()
                    tt(inter, sg, bank(5), ALU.mult).then_inc(m_prod.sem, 1)
                    dve.drain()
                    n, step = (j - 2) // 6, (j - 2) % 6
                    if j >= 2:
                        ratio_step(b, n, step)
                    if step == 5 and n < 7:
                        ratio_start(b, n + 1)
                    dve.wait_ge(m_ihi.sem, m_ihi.at(b, j + 1))
                    tt(isp[j % 2][1], inter, isp[j % 2][0].bitcast(F32), ALU.subtract).then_inc(m_inter.sem, 1)
                    dve.drain()
                dve.wait_ge(m_down.sem, m_down.at(b, MT))
                residual(1)

                gate(b, 2)
                dve.wait_ge(s_raw.sem, s_raw.at(b, 1))
                ts(vt, vt, dtb, None, ALU.add)
                dve.drain()
                stt(out=nab, in0=vt, scalar=-1.0, in1=vt, op0=ALU.mult, op1=ALU.min).then_inc(s_v.sem, 1)
                dve.wait_ge(s_ln.sem, s_ln.at(b, 1))
                stt(out=dtt, in0=vt, scalar=0.0, in1=nab, op0=ALU.max, op1=ALU.add)
                dve.drain()
                ts(eat, dtt, negA, None, ALU.mult).then_inc(s_dt.sem, 1)
                dve.wait_ge(s_th.sem, s_th.at(b, 1))
                tt(gmt, lamt, dtt, ALU.mult)
                dve.drain()
                for k in range(NT):
                    t = slice(k * P, (k + 1) * P)
                    dve.tensor_tensor_scan(cst_[:, t], one[0:SH, :].to_broadcast([SH, P]), eat[:, t], 0.0,
                                           ALU.mult, ALU.add)
                ts(lamt, lamt, -1.0, 1.0, ALU.mult, ALU.add)
                dve.drain()
                tt(lamt, lamt, dtt, ALU.mult)
                for k in range(NT):
                    ts(dl[:, k * SH:(k + 1) * SH], cst("ident")[0:SH, 0:SH], cst_[:, (k + 1) * P - 1:(k + 1) * P],
                       None, ALU.mult)
                dve.drain().then_inc(s_cs.sem, 1)
                dve.wait_ge(s_ea.sem, s_ea.at(b, 1))
                tt(bet, lamt, eat, ALU.mult)
                dve.wait_ge(s_dtavg.sem, s_dtavg.at(b, 1))
                tt(th, th, bank(5, SN), ALU.mult)
                dve.drain()
                dve.tensor_tensor_scan(ang, one[0:SN, :].to_broadcast([SN, T]), th, 0.0, ALU.mult, ALU.add)
                dve.drain()
                inv = 1.0 / (2.0 * np.pi)
                ts(nrd[:, 0, :], ang, inv, None, ALU.mult)
                ts(nrd[:, 1, :], ang, inv, 0.25, ALU.mult, ALU.add)
                dve.drain()
                ts(nrd[:, :, :], nrd[:, :, :], MAGIC, MAGIC, ALU.add, ALU.subtract)
                dve.drain()
                ang2 = ang.unsqueeze(1).to_broadcast([SN, 2, T])
                stt(out=trg[:, :, :], in0=nrd[:, :, :], scalar=-TWO_PI[0], in1=ang2, op0=ALU.mult, op1=ALU.add)
                dve.drain()
                for cpart in TWO_PI[1:]:
                    stt(out=trg[:, :, :], in0=nrd[:, :, :], scalar=-cpart, in1=trg[:, :, :], op0=ALU.mult, op1=ALU.add)
                    dve.drain()
                ts(trg[:, 1, :], trg[:, 1, :], float(np.pi / 2), None, ALU.add)
                dve.drain()
                ts(nrd[:, :, :], trg[:, :, :], 3.1415925, -3.1415925, ALU.min, ALU.max).then_inc(s_ang.sem, 1)
                dve.wait_ge(s_rms.sem, s_rms.at(b, 1))
                dve.reciprocal(brs[:, :, :], brs[:, :, :])
                dve.drain()
                for i in range(2):
                    tt(BCn[:, i, :], bank(i, SN), brs[:, i, :], ALU.mult)
                dve.drain()
                for i in range(2):
                    q = ts(BCn[:, i, :], BCn[:, i, :], bcb[:, i:i + 1], None, ALU.add)
                q.then_inc(s_bcn.sem, 1)
                dve.wait_ge(s_perm.sem, s_perm.at(b, 1))
                dve.wait_ge(s_sin.sem, s_sin.at(b, 1))
                for i in range(2):
                    tt(bsq[:, i, :], bank(i, SN), trg[:, 0, :], ALU.mult)
                    tt(BCn[:, i, :], BCn[:, i, :], trg[:, 1, :], ALU.mult)
                dve.drain()
                tt(BCn[:, :, :], BCn[:, :, :], bsq[:, :, :], ALU.add).then_inc(s_rope.sem, 1)
                dve.wait_ge(s_tm.sem, s_tm.at(b, 1))
                dve.tensor_copy(tm[:, :, :, :], bank(2)[:, 0:NT * 3 * SH].rearrange("p (k a h) -> p k a h", k=NT, a=3))
                dve.tensor_copy(Btm[:, :, :], bank(3)[:, 0:NT * SN].rearrange("p (k n) -> p k n", k=NT))
                dve.tensor_copy(csl, bank(4)[:, 0:NT * SH])
                dve.memset(state[:, :], 0.0)
                dve.drain()
                tt(r3(dend, SH), r3(csl, SH), tm[:, :, 2, :], ALU.subtract).then_inc(s_tmc.sem, 1)

                dve.drain()
                dve.wait_ge(s_cb.sem, s_cb.at(b, 1))
                tt(Gm[:, :, :], r3(bank(5), P), cst("tri").unsqueeze(1).to_broadcast([P, NT, P]), ALU.mult)\
                    .then_inc(s_gm.sem, 1)
                dve.wait_ge(s_exps.sem, s_exps.at(b, 1))

                def residual_tile(k):
                    dve.wait_ge(s_out.sem, s_out.at(b, k + 1))
                    tt(tile_of(xT, k), tile_of(xT, k), r3(bank(7), P), ALU.add).then_inc(x_ready.sem, 1)

                for k in range(NT):
                    def differences(g):
                        dve.wait_ge(s_csb.sem, s_csb.at(b, k * 4 + g + 1))
                        if g >= 2:
                            dve.wait_ge(s_mu.sem, s_mu.at(b, k * 3 + g - 1))
                        tt(r3(Md[:, g % 2, :], P), r3(bank(5 + g % 2), P),
                           bcast(tm[:, k, 2, g * 4:(g + 1) * 4], P), ALU.subtract).then_inc(s_diff.sem, 1)

                    def masked(g):
                        dve.wait_ge(s_exp.sem, s_exp.at(b, k * 4 + g + 1))
                        m3 = r3(Md[:, g % 2, :], P)
                        stt(out=m3, in0=m3, scalar=10000.0, in1=Gm[:, k, :].unsqueeze(1).to_broadcast([P, 4, P]),
                            op0=ALU.min, op1=ALU.mult).then_inc(s_m.sem, 1)
                        dve.drain()

                    if k:
                        dve.wait_ge(s_yss.sem, s_yss.at(b, k))
                        dve.reciprocal(ss[:, 2:3], ss[:, 1:2]).then_inc(s_yr.sem, 1)
                    differences(0)
                    x = Xg[k % 2]
                    dve.wait_ge(s_shift.sem, s_shift.at(b, k + 1))
                    for h in range(2):
                        tt(r3(Xd[:, h * 512:(h + 1) * 512], SP_), r3(bank(h), SP_),
                           bcast(tm[:, k, 1, h * 8:(h + 1) * 8], SP_), ALU.mult)
                    dve.drain()
                    dve.wait_ge(s_gx.sem, s_gx.at(b, k + 1))
                    tt(x, x, Xd, ALU.add).then_inc(s_xg.sem, 1)
                    differences(1)
                    masked(0)
                    differences(2)
                    masked(1)
                    differences(3)
                    masked(2)
                    masked(3)
                    y = Yt[k % 2]
                    dve.wait_ge(s_yo.sem, s_yo.at(b, k + 1))
                    for h in range(2):
                        tt(r3(y[:, h * 512:(h + 1) * 512], SP_), r3(bank(2 + h), SP_),
                           bcast(ecs[:, k * SH + h * 8:k * SH + h * 8 + 8], SP_), ALU.mult)
                    dve.drain()
                    dve.wait_ge(s_dx.sem, s_dx.at(b, k + 1))
                    tt(y, y, Dx, ALU.add)
                    dve.drain()
                    dve.wait_ge(s_yd.sem, s_yd.at(b, k + 1))
                    for h in range(2):
                        yh = y[:, h * 512:(h + 1) * 512]
                        tt(yh, yh, bank(h), ALU.add)
                    dve.drain()
                    tt(r3(y, P), r3(y, P), ynT8[:, :, k * P:(k + 1) * P], ALU.mult).then_inc(s_y.sem, 1)
                    if k < NT - 1:
                        dve.wait_ge(s_sdec.sem, s_sdec.at(b, k + 1))
                        dve.wait_ge(s_st.sem, s_st.at(b, k + 1))
                        for h in range(2):
                            st = state[:, h * 512:(h + 1) * 512]
                            q = tt(st, st, bank(4 + h, SN), ALU.add)
                        q.then_inc(s_state.sem, 1)
                    if k:
                        residual_tile(k - 1)
                dve.wait_ge(s_yss.sem, s_yss.at(b, NT))
                dve.reciprocal(ss[:, 2:3], ss[:, 1:2]).then_inc(s_yr.sem, 1)
                for k in range(NT):
                    if k == NT - 1:
                        residual_tile(k)
                    dve.wait_ge(sig_ready.sem, sig_ready.at(b, 3 * NC + k + 1))
                    tt(tile_of(hT, k), tile_of(hT, k), tile_of(R[3], k), ALU.mult).then_inc(h_tile.sem, 1)
                dve.drain()
                def quantise_x(t):
                    dve.wait_ge(f_tx.sem, f_tx.at(b, t + 1))
                    if t >= 2:
                        dve.wait_ge(f_qx.sem, f_qx.at(b, t - 1))
                    v, m = fxv[t % 2], fxm[t % 2]
                    quantise_head(bank(7), v, m, fxamx[t % 2])
                    dve.drain()
                    tt(v, v, m, ALU.add).then_inc(f_vx.sem, 1)

                quantise_x(0)
                quantise_x(1)
                for i in range(FB * NT):
                    dve.wait_ge(f_silu.sem, f_silu.at(b, i + 1))
                    dve.wait_ge(f_gu.sem, f_gu.at(b, i + 1))
                    tt(fh, fs[i % 2], bank(5), ALU.mult).then_inc(f_mul.sem, 1)
                    dve.drain()
                    if i >= 2:
                        dve.wait_ge(f_tr.sem, f_tr.at(b, i - 1))
                    quantise(fq[i % 2], fh, fv, fm, famx).then_inc(f_q.sem, 1)
                    dve.drain()
                    if i + 2 < NT:
                        quantise_x(i + 2)
                    if i == 9:
                        gate(b, LAYERS)
                dve.wait_ge(f_down.sem, f_down.at(b, FB))
                residual(3)


def host_arrays(i):
    ct = np.ascontiguousarray

    def channel_major(x):
        return ct(x.transpose(0, 2, 1).reshape(NB, NC, P, T).transpose(0, 2, 1, 3))

    def per_channel(v):
        return v.reshape(NC, P).T

    def k_major(wt):
        o, k = wt.shape
        return wt.T.reshape(k // P, P, o).transpose(1, 0, 2)

    r = {}
    r["consts"] = constant_table()[1]
    r["moe_sel"] = expert_rows()
    rows = np.arange(NB + 1) % NB
    r["xT"] = ct(channel_major(i["x"])[rows])
    r["fT"] = ct(channel_major(i["fside_BxSxS_0"])[rows].transpose(0, 2, 1, 3))
    r["selv"] = value_selectors()
    r["condT"] = ct(i["cond_512"].T)
    r["wu"] = ct(np.concatenate([per_channel(i[f"{n}_{a}"]) for n in ("L0_cond", "L0_cond2", "L1_cond", "L1_cond2")
                                 for a in "wu"], 1))
    def by_value(v):
        return v.reshape(NC, HPC, GK // 4, 4, *v.shape[1:]).swapaxes(1, 3).reshape(v.shape)

    r["gb"] = ct(np.concatenate([per_channel(by_value(i["L0_attn_gamma"])),
                                 per_channel(by_value(i["L0_attn_beta"]))], 1))
    r["gwT"] = ct(k_major(i["L0_ffn_gate_weight"]).reshape(P, NC * NE))
    r["gate_bias"] = i["L0_ffn_e_score_correction_bias"]
    r["bc_bias"] = ct(np.concatenate([i["L1_attn_B_bias"].T, i["L1_attn_C_bias"].T], 1))
    r["A_log"], r["dt_bias"], r["D_param"] = i["L1_attn_A_log"], i["L1_attn_dt_bias"], i["L1_attn_D_param"]
    qkvg = np.stack([k_major(i[f"L0_attn_W{m}"]) for m in "qkvg"], 1)
    r["w_qkvg"] = ct(qkvg.reshape(P, 4, NC, NC, P).transpose(3, 0, 1, 2, 4))
    r["wo"] = ct(k_major(by_value(i["L0_attn_Wo"].T).T))
    pad = np.zeros((ST * P - NSH * EI, D), np.float32)
    gate = np.concatenate([i["L0_ffn_shared_gate_w"], pad, i["L0_ffn_gate_proj"].reshape(NE * EI, D)])
    up = np.concatenate([i["L0_ffn_shared_up_w"], pad, i["L0_ffn_up_proj"].reshape(NE * EI, D)])
    down = np.concatenate([i["L0_ffn_shared_down_w"].T, pad,
                           i["L0_ffn_down_proj"].transpose(0, 2, 1).reshape(NE * EI, D)])
    gu = np.stack([k_major(gate), k_major(up)], 1).reshape(P, 2, NC, MT, P)
    r["moe_w"] = ct(np.concatenate([gu.transpose(3, 0, 1, 2, 4).reshape(MT, P, GUW), down.reshape(MT, P, D)], 2))
    win, th, lam, wout = (i[f"L1_attn_{n}"] for n in ("W_in", "W_theta", "W_lambda", "W_out"))
    dtw = win[2 * DI + 2 * SN:]
    r["w_fq"] = ct(np.concatenate([win[:2 * DI], wout.reshape(D, 2, 512).transpose(1, 0, 2).reshape(2 * D, 512),
                                   win[2 * DI:2 * DI + 2 * SN], th, th, dtw, lam, lam, dtw]).reshape(-1, P, 512))
    g, u, d = i["L1_ffn_gate_w"], i["L1_ffn_up_w"], i["L1_ffn_down_w"]
    mx = np.stack([g.reshape(FB, 512, D), u.reshape(FB, 512, D), d.reshape(D, FB, 512).transpose(1, 0, 2)], 1)
    r["w_mx"] = ct(mx.reshape(-1, P, 512))
    return r


def kernel(**inputs):
    import concourse.bacc as _bacc
    from concourse.bass_utils import run_bass_kernel_spmd as _run

    nc = _bacc.Bacc("TRN2", target_bir_lowering=False, num_devices=1)
    arrays = host_arrays({k: np.asarray(v) for k, v in inputs.items()})
    A = {k: nc.dram_tensor(k, list(v.shape), F32, kind="ExternalInput").ap() for k, v in arrays.items()}
    out = nc.dram_tensor("out", [NB, P, NC, T], F32, kind="ExternalOutput").ap()
    fq = nc.dram_tensor("scratch_fq", [7, P, 4, 512], F32, kind="Internal").ap()
    mx = nc.dram_tensor("scratch_mx", [FB, 3, P, 4, 512], F32, kind="Internal").ap()
    build(nc, A, out, fq, mx)
    got = _run(nc, [arrays], core_ids=[0]).results[0]["out"]
    return np.ascontiguousarray(got.transpose(0, 2, 1, 3).reshape(NB, D, T).transpose(0, 2, 1))
```
